# Optimizing a Trainium2 kernel written in Bass

```python
import numpy as np
import jax
import jax.numpy as jnp

def _softmax(x, axis=-1):
    return jax.nn.softmax(x, axis=axis)

def _gelu(x):
    return jax.nn.gelu(x, approximate=True)

def _silu(x):
    return jax.nn.silu(x)

def _sigmoid(x):
    return jax.nn.sigmoid(x)

def _layernorm(x, axis=-1, eps=1e-05):
    m = jnp.mean(x, axis=axis, keepdims=True)
    v = jnp.var(x, axis=axis, keepdims=True)
    return (x - m) / jnp.sqrt(v + eps)

def _scatter_add(tgt, idx, src, axis=0):
    return tgt.at[idx].add(src)

def _segment_sum(src, seg, n):
    return jax.ops.segment_sum(src, seg, n)
kernel_name = 'mk_adaln_attn_ffn_d1_seqx_r4_480c71'

def setup_inputs(seed: int=0):
    np.random.seed(seed)
    _w = jnp.asarray

    def _rec_inputs():
        import jax
        import jax.numpy as jnp
        _rk = jax.random.key(seed)
        x = -0.0002928 + 1 * jax.random.normal(jax.random.fold_in(_rk, 1), (32, 64, 256), jnp.float32)
        _lenS = 64 - jax.random.randint(jax.random.fold_in(_rk, 7), (32,), 0, max(1, 64 // 4) + 1, jnp.int32)
        _lenS2 = 64 - jax.random.randint(jax.random.fold_in(_rk, 8), (32,), 0, max(1, 64 // 4) + 1, jnp.int32)
        cond_256 = -0.106481 + 1.03144 * jax.random.normal(jax.random.fold_in(_rk, 11), (32, 64), jnp.float32)
        return (x, cond_256)
    x, cond_256 = _rec_inputs()

    def _L0_cond_setup():
        import jax, jax.numpy as jnp
        import numpy as np
        TOP_K = 2
        EPS = 1e-06
        B, S, H, G, E, M = (2, 512, 256, 64, 8, 512)
        key = jax.random.key(seed)
        ks = jax.random.split(key, 16)
        s_h = 1.0 / np.sqrt(H)
        s_g = 1.0 / np.sqrt(G)
        s_m = 1.0 / np.sqrt(M)
        return {'x': jax.random.normal(ks[0], (B, S, H), jnp.float32), 'genre_embed': jax.random.normal(ks[1], (B, 1, G), jnp.float32), 'rms_w': jnp.ones((H,), jnp.float32), 'wg_W': jax.random.normal(ks[2], (H, E), jnp.float32) * s_h, 'wg_b': jnp.zeros((E,), jnp.float32), 'gg_W': jax.random.normal(ks[3], (G, E), jnp.float32) * s_g, 'gg_b': jnp.zeros((E,), jnp.float32), 'W1': jax.random.normal(ks[4], (E, H, M), jnp.float32) * s_h, 'b1': jnp.zeros((E, M), jnp.float32), 'W2': jax.random.normal(ks[5], (E, M, M), jnp.float32) * s_m, 'b2': jnp.zeros((E, M), jnp.float32), 'W3': jax.random.normal(ks[6], (E, M, H), jnp.float32) * s_m, 'b3': jnp.zeros((E, H), jnp.float32)}
    _L0_cond_all = _L0_cond_setup()
    _L0_cond_in = {k: v for k, v in _L0_cond_all.items() if k in ('rms_w', 'wg_W', 'wg_b', 'gg_W', 'gg_b', 'W1', 'b1', 'W2', 'b2', 'W3', 'b3')}
    del _L0_cond_all

    def _L0_attn_setup():
        import jax, jax.numpy as jnp
        import numpy as np
        import math
        B, S, D, H = (4, 512, 256, 16)
        DK = D // H
        key = jax.random.key(seed)
        ks = jax.random.split(key, 5)
        scale = 1.0 / math.sqrt(D)
        return {'x': jax.random.normal(ks[0], (B, S, D), dtype=jnp.float32), 'Wv': jax.random.normal(ks[1], (D, D), dtype=jnp.float32) * scale, 'bv': jax.random.normal(ks[2], (D,), dtype=jnp.float32) * scale, 'Wo': jax.random.normal(ks[3], (D, D), dtype=jnp.float32) * scale, 'bo': jax.random.normal(ks[4], (D,), dtype=jnp.float32) * scale}
    _L0_attn_all = _L0_attn_setup()
    _L0_attn_in = {k: v for k, v in _L0_attn_all.items() if k in ('Wv', 'bv', 'Wo', 'bo')}
    del _L0_attn_all

    def _L0_cond2_setup():
        import jax, jax.numpy as jnp
        import numpy as np
        D_MODEL = 256
        D_T = 64
        N_HEADS = 16
        HIDDEN = 4 * D_MODEL
        EPS = 1e-06

        def _tc_rmsnorm(x, t, gw, gb, bw, bb):
            g = (t @ gw.T + gb)[:, None, :]
            b = (t @ bw.T + bb)[:, None, :]
            inv_rms = jax.lax.rsqrt(jnp.mean(x * x, axis=-1, keepdims=True) + EPS)
            return g * x * inv_rms + b

        def _attention(x, Wq, Wk, Wv, Wo):
            B, L, D = x.shape
            H = N_HEADS
            dh = D // H
            scale = np.sqrt(dh).astype(np.float32)
            q = (x @ Wq.T).reshape(B, L, H, dh)
            k = (x @ Wk.T).reshape(B, L, H, dh)
            v = (x @ Wv.T).reshape(B, L, H, dh)
            attn = jnp.einsum('blhd,bmhd->bhlm', q, k) / scale
            p = jax.nn.softmax(attn, axis=-1)
            o = jnp.einsum('bhlm,bmhd->blhd', p, v).reshape(B, L, D)
            return o @ Wo.T

        def _swiglu(x, gate_w, hid_w, out_w):
            return jax.nn.silu(x @ gate_w.T) * (x @ hid_w.T) @ out_w.T
        key = jax.random.key(seed)
        ks = jax.random.split(key, 20)
        B, L = (8, 256)
        s_d = 1.0 / np.sqrt(D_MODEL)
        s_t = 1.0 / np.sqrt(D_T)
        s_h = 1.0 / np.sqrt(HIDDEN)
        return {'x': jax.random.normal(ks[0], (B, L, D_MODEL), jnp.float32), 't': jax.random.normal(ks[1], (B, D_T), jnp.float32), 'Wq': jax.random.normal(ks[2], (D_MODEL, D_MODEL), jnp.float32) * s_d, 'Wk': jax.random.normal(ks[3], (D_MODEL, D_MODEL), jnp.float32) * s_d, 'Wv': jax.random.normal(ks[4], (D_MODEL, D_MODEL), jnp.float32) * s_d, 'Wo': jax.random.normal(ks[5], (D_MODEL, D_MODEL), jnp.float32) * s_d, 'g1w': jax.random.normal(ks[6], (D_MODEL, D_T), jnp.float32) * s_t, 'g1b': jnp.ones((D_MODEL,), jnp.float32), 'b1w': jax.random.normal(ks[7], (D_MODEL, D_T), jnp.float32) * s_t, 'b1b': jnp.zeros((D_MODEL,), jnp.float32), 'g2w': jax.random.normal(ks[8], (D_MODEL, D_T), jnp.float32) * s_t, 'g2b': jnp.ones((D_MODEL,), jnp.float32), 'b2w': jax.random.normal(ks[9], (D_MODEL, D_T), jnp.float32) * s_t, 'b2b': jnp.zeros((D_MODEL,), jnp.float32), 'gate_w': jax.random.normal(ks[10], (HIDDEN, D_MODEL), jnp.float32) * s_d, 'hid_w': jax.random.normal(ks[11], (HIDDEN, D_MODEL), jnp.float32) * s_d, 'out_w': jax.random.normal(ks[12], (D_MODEL, HIDDEN), jnp.float32) * s_h}
    _L0_cond2_all = _L0_cond2_setup()
    _L0_cond2_in = {k: v for k, v in _L0_cond2_all.items() if k in ('Wq', 'Wk', 'Wv', 'Wo', 'g1w', 'g1b', 'b1w', 'b1b', 'g2w', 'g2b', 'b2w', 'b2b', 'gate_w', 'hid_w', 'out_w')}
    del _L0_cond2_all

    def _L0_ffn_setup():
        import jax, jax.numpy as jnp
        import numpy as np
        B, L, D = (4, 512, 256)
        H = 16
        E = 16
        NS = 16
        S = NS // E
        F = 1024
        EPS = 1e-05

        def _layernorm(x, g, b):
            mu = jnp.mean(x, axis=-1, keepdims=True)
            var = jnp.mean(jnp.square(x - mu), axis=-1, keepdims=True)
            return (x - mu) * jax.lax.rsqrt(var + EPS) * g + b

        def _mha(q, k, v, Wq, bq, Wk, bk, Wv, bv, Wo, bo):
            Bq, Lq, Dm = q.shape
            dh = Dm // H
            qh = (q @ Wq + bq).reshape(Bq, Lq, H, dh)
            kh = (k @ Wk + bk).reshape(Bq, -1, H, dh)
            vh = (v @ Wv + bv).reshape(Bq, -1, H, dh)
            scores = jnp.einsum('bqhd,bkhd->bhqk', qh, kh) / jnp.asarray(np.sqrt(dh), q.dtype)
            attn = jax.nn.softmax(scores, axis=-1)
            out = jnp.einsum('bhqk,bkhd->bqhd', attn, vh).reshape(Bq, Lq, Dm)
            return out @ Wo + bo
        key = jax.random.key(seed)
        ks = jax.random.split(key, 32)
        s = 0.02
        d = {}
        d['x'] = jax.random.normal(ks[0], (B, L, D), jnp.float32)
        d['slot_query'] = jax.random.normal(ks[1], (1, NS, D), jnp.float32) * 0.01
        for i, nm in enumerate(['d_Wq', 'd_Wk', 'd_Wv', 'd_Wo']):
            d[nm] = jax.random.normal(ks[2 + i], (D, D), jnp.float32) * s
        for nm in ['d_bq', 'd_bk', 'd_bv', 'd_bo']:
            d[nm] = jnp.zeros((D,), jnp.float32)
        for i, nm in enumerate(['c_Wq', 'c_Wk', 'c_Wv', 'c_Wo']):
            d[nm] = jax.random.normal(ks[6 + i], (D, D), jnp.float32) * s
        for nm in ['c_bq', 'c_bk', 'c_bv', 'c_bo']:
            d[nm] = jnp.zeros((D,), jnp.float32)
        d['e_ln_g'] = jnp.ones((E, D), jnp.float32)
        d['e_ln_b'] = jnp.zeros((E, D), jnp.float32)
        d['e_W1'] = jax.random.normal(ks[10], (E, D, F), jnp.float32) * s
        d['e_b1'] = jnp.zeros((E, F), jnp.float32)
        d['e_Wg'] = jax.random.normal(ks[11], (E, D, F), jnp.float32) * s
        d['e_bg'] = jnp.zeros((E, F), jnp.float32)
        d['e_W2'] = jax.random.normal(ks[12], (E, F, D), jnp.float32) * s
        d['e_b2'] = jnp.zeros((E, D), jnp.float32)
        return d
    _L0_ffn_all = _L0_ffn_setup()
    _L0_ffn_in = {k: v for k, v in _L0_ffn_all.items() if k in ('slot_query', 'd_Wq', 'd_Wk', 'd_Wv', 'd_Wo', 'd_bq', 'd_bk', 'd_bv', 'd_bo', 'c_Wq', 'c_Wk', 'c_Wv', 'c_Wo', 'c_bq', 'c_bk', 'c_bv', 'c_bo', 'e_ln_g', 'e_ln_b', 'e_W1', 'e_b1', 'e_Wg', 'e_bg', 'e_W2', 'e_b2')}
    del _L0_ffn_all
    return {'x': x, 'cond_256': cond_256, 'L0_cond_rms_w': _L0_cond_in['rms_w'], 'L0_cond_wg_W': _L0_cond_in['wg_W'], 'L0_cond_wg_b': _L0_cond_in['wg_b'], 'L0_cond_gg_W': _L0_cond_in['gg_W'], 'L0_cond_gg_b': _L0_cond_in['gg_b'], 'L0_cond_W1': _L0_cond_in['W1'], 'L0_cond_b1': _L0_cond_in['b1'], 'L0_cond_W2': _L0_cond_in['W2'], 'L0_cond_b2': _L0_cond_in['b2'], 'L0_cond_W3': _L0_cond_in['W3'], 'L0_cond_b3': _L0_cond_in['b3'], 'L0_attn_Wv': _L0_attn_in['Wv'], 'L0_attn_bv': _L0_attn_in['bv'], 'L0_attn_Wo': _L0_attn_in['Wo'], 'L0_attn_bo': _L0_attn_in['bo'], 'L0_cond2_Wq': _L0_cond2_in['Wq'], 'L0_cond2_Wk': _L0_cond2_in['Wk'], 'L0_cond2_Wv': _L0_cond2_in['Wv'], 'L0_cond2_Wo': _L0_cond2_in['Wo'], 'L0_cond2_g1w': _L0_cond2_in['g1w'], 'L0_cond2_g1b': _L0_cond2_in['g1b'], 'L0_cond2_b1w': _L0_cond2_in['b1w'], 'L0_cond2_b1b': _L0_cond2_in['b1b'], 'L0_cond2_g2w': _L0_cond2_in['g2w'], 'L0_cond2_g2b': _L0_cond2_in['g2b'], 'L0_cond2_b2w': _L0_cond2_in['b2w'], 'L0_cond2_b2b': _L0_cond2_in['b2b'], 'L0_cond2_gate_w': _L0_cond2_in['gate_w'], 'L0_cond2_hid_w': _L0_cond2_in['hid_w'], 'L0_cond2_out_w': _L0_cond2_in['out_w'], 'L0_ffn_slot_query': _L0_ffn_in['slot_query'], 'L0_ffn_d_Wq': _L0_ffn_in['d_Wq'], 'L0_ffn_d_Wk': _L0_ffn_in['d_Wk'], 'L0_ffn_d_Wv': _L0_ffn_in['d_Wv'], 'L0_ffn_d_Wo': _L0_ffn_in['d_Wo'], 'L0_ffn_d_bq': _L0_ffn_in['d_bq'], 'L0_ffn_d_bk': _L0_ffn_in['d_bk'], 'L0_ffn_d_bv': _L0_ffn_in['d_bv'], 'L0_ffn_d_bo': _L0_ffn_in['d_bo'], 'L0_ffn_c_Wq': _L0_ffn_in['c_Wq'], 'L0_ffn_c_Wk': _L0_ffn_in['c_Wk'], 'L0_ffn_c_Wv': _L0_ffn_in['c_Wv'], 'L0_ffn_c_Wo': _L0_ffn_in['c_Wo'], 'L0_ffn_c_bq': _L0_ffn_in['c_bq'], 'L0_ffn_c_bk': _L0_ffn_in['c_bk'], 'L0_ffn_c_bv': _L0_ffn_in['c_bv'], 'L0_ffn_c_bo': _L0_ffn_in['c_bo'], 'L0_ffn_e_ln_g': _L0_ffn_in['e_ln_g'], 'L0_ffn_e_ln_b': _L0_ffn_in['e_ln_b'], 'L0_ffn_e_W1': _L0_ffn_in['e_W1'], 'L0_ffn_e_b1': _L0_ffn_in['e_b1'], 'L0_ffn_e_Wg': _L0_ffn_in['e_Wg'], 'L0_ffn_e_bg': _L0_ffn_in['e_bg'], 'L0_ffn_e_W2': _L0_ffn_in['e_W2'], 'L0_ffn_e_b2': _L0_ffn_in['e_b2']}

def reference(x, cond_256, L0_cond_rms_w, L0_cond_wg_W, L0_cond_wg_b, L0_cond_gg_W, L0_cond_gg_b, L0_cond_W1, L0_cond_b1, L0_cond_W2, L0_cond_b2, L0_cond_W3, L0_cond_b3, L0_attn_Wv, L0_attn_bv, L0_attn_Wo, L0_attn_bo, L0_cond2_Wq, L0_cond2_Wk, L0_cond2_Wv, L0_cond2_Wo, L0_cond2_g1w, L0_cond2_g1b, L0_cond2_b1w, L0_cond2_b1b, L0_cond2_g2w, L0_cond2_g2b, L0_cond2_b2w, L0_cond2_b2b, L0_cond2_gate_w, L0_cond2_hid_w, L0_cond2_out_w, L0_ffn_slot_query, L0_ffn_d_Wq, L0_ffn_d_Wk, L0_ffn_d_Wv, L0_ffn_d_Wo, L0_ffn_d_bq, L0_ffn_d_bk, L0_ffn_d_bv, L0_ffn_d_bo, L0_ffn_c_Wq, L0_ffn_c_Wk, L0_ffn_c_Wv, L0_ffn_c_Wo, L0_ffn_c_bq, L0_ffn_c_bk, L0_ffn_c_bv, L0_ffn_c_bo, L0_ffn_e_ln_g, L0_ffn_e_ln_b, L0_ffn_e_W1, L0_ffn_e_b1, L0_ffn_e_Wg, L0_ffn_e_bg, L0_ffn_e_W2, L0_ffn_e_b2):
    import jax
    import jax.numpy as jnp

    def _L0_cond_ref(x, genre_embed, rms_w, wg_W, wg_b, gg_W, gg_b, W1, b1, W2, b2, W3, b3):
        import jax, jax.numpy as jnp
        import numpy as np
        TOP_K = 2
        EPS = 1e-06
        E = W1.shape[0]
        var = jnp.mean(x * x, axis=-1, keepdims=True)
        xn = rms_w * (x * jax.lax.rsqrt(var + EPS))
        gate = xn @ wg_W + wg_b + (genre_embed @ gg_W + gg_b)
        gate_w = jax.nn.softmax(gate, axis=-1)
        topk_w, topk_i = jax.lax.top_k(gate_w, TOP_K)
        cw = jnp.sum(jax.nn.one_hot(topk_i, E, dtype=x.dtype) * topk_w[..., None], axis=-2)
        h1 = jax.nn.relu(jnp.einsum('bsh,ehm->bsem', x, W1) + b1)
        h2 = jax.nn.relu(jnp.einsum('bsem,emn->bsen', h1, W2) + b2)
        out_e = jnp.einsum('bsen,enh->bseh', h2, W3) + b3
        return jnp.einsum('bseh,bse->bsh', out_e, cw)

    def _L0_attn_ref(x, Wv, bv, Wo, bo):
        import jax, jax.numpy as jnp
        import numpy as np
        import math
        B, S, D, H = (4, 512, 256, 16)
        DK = D // H
        b, s, d = x.shape
        h, dk = (H, DK)
        p = jnp.einsum('bsd,ed->bse', x, Wv) + bv
        p = p.reshape(b, s, h, dk).transpose(0, 2, 1, 3)
        q = k = v = p
        scores = jnp.einsum('bhqd,bhkd->bhqk', q, k) / math.sqrt(dk)
        attn = jax.nn.softmax(scores, axis=-1)
        out = jnp.einsum('bhqk,bhkd->bhqd', attn, v)
        out = out.reshape(b, s, h * dk)
        return jnp.einsum('bsd,ed->bse', out, Wo) + bo

    def _L0_cond2_ref(x, t, Wq, Wk, Wv, Wo, g1w, g1b, b1w, b1b, g2w, g2b, b2w, b2b, gate_w, hid_w, out_w):
        import jax, jax.numpy as jnp
        import numpy as np
        D_MODEL = 256
        D_T = 64
        N_HEADS = 16
        HIDDEN = 4 * D_MODEL
        EPS = 1e-06

        def _tc_rmsnorm(x, t, gw, gb, bw, bb):
            g = (t @ gw.T + gb)[:, None, :]
            b = (t @ bw.T + bb)[:, None, :]
            inv_rms = jax.lax.rsqrt(jnp.mean(x * x, axis=-1, keepdims=True) + EPS)
            return g * x * inv_rms + b

        def _attention(x, Wq, Wk, Wv, Wo):
            B, L, D = x.shape
            H = N_HEADS
            dh = D // H
            scale = np.sqrt(dh).astype(np.float32)
            q = (x @ Wq.T).reshape(B, L, H, dh)
            k = (x @ Wk.T).reshape(B, L, H, dh)
            v = (x @ Wv.T).reshape(B, L, H, dh)
            attn = jnp.einsum('blhd,bmhd->bhlm', q, k) / scale
            p = jax.nn.softmax(attn, axis=-1)
            o = jnp.einsum('bhlm,bmhd->blhd', p, v).reshape(B, L, D)
            return o @ Wo.T

        def _swiglu(x, gate_w, hid_w, out_w):
            return jax.nn.silu(x @ gate_w.T) * (x @ hid_w.T) @ out_w.T
        x = x + _attention(_tc_rmsnorm(x, t, g1w, g1b, b1w, b1b), Wq, Wk, Wv, Wo)
        return x + _swiglu(_tc_rmsnorm(x, t, g2w, g2b, b2w, b2b), gate_w, hid_w, out_w)

    def _L0_ffn_ref(x, slot_query, d_Wq, d_Wk, d_Wv, d_Wo, d_bq, d_bk, d_bv, d_bo, c_Wq, c_Wk, c_Wv, c_Wo, c_bq, c_bk, c_bv, c_bo, e_ln_g, e_ln_b, e_W1, e_b1, e_Wg, e_bg, e_W2, e_b2):
        import jax, jax.numpy as jnp
        import numpy as np
        B, L, D = (4, 512, 256)
        H = 16
        E = 16
        NS = 16
        S = NS // E
        F = 1024
        EPS = 1e-05

        def _layernorm(x, g, b):
            mu = jnp.mean(x, axis=-1, keepdims=True)
            var = jnp.mean(jnp.square(x - mu), axis=-1, keepdims=True)
            return (x - mu) * jax.lax.rsqrt(var + EPS) * g + b

        def _mha(q, k, v, Wq, bq, Wk, bk, Wv, bv, Wo, bo):
            Bq, Lq, Dm = q.shape
            dh = Dm // H
            qh = (q @ Wq + bq).reshape(Bq, Lq, H, dh)
            kh = (k @ Wk + bk).reshape(Bq, -1, H, dh)
            vh = (v @ Wv + bv).reshape(Bq, -1, H, dh)
            scores = jnp.einsum('bqhd,bkhd->bhqk', qh, kh) / jnp.asarray(np.sqrt(dh), q.dtype)
            attn = jax.nn.softmax(scores, axis=-1)
            out = jnp.einsum('bhqk,bkhd->bqhd', attn, vh).reshape(Bq, Lq, Dm)
            return out @ Wo + bo
        Bx = x.shape[0]
        q = jnp.broadcast_to(slot_query, (Bx, NS, D))
        o = q + _mha(q, x, x, d_Wq, d_bq, d_Wk, d_bk, d_Wv, d_bv, d_Wo, d_bo)
        os = o.reshape(Bx, E, S, D)
        h = _layernorm(os, e_ln_g[None, :, None, :], e_ln_b[None, :, None, :])
        u = jax.nn.silu(jnp.einsum('besd,edf->besf', h, e_W1) + e_b1[None, :, None, :])
        g = jax.nn.silu(jnp.einsum('besd,edf->besf', h, e_Wg) + e_bg[None, :, None, :])
        y = jnp.einsum('besf,efd->besd', u * g, e_W2) + e_b2[None, :, None, :]
        o = o + y.reshape(Bx, NS, D)
        out = _mha(x, o, o, c_Wq, c_bq, c_Wk, c_bk, c_Wv, c_bv, c_Wo, c_bo)
        return out
    x = x + _L0_attn_ref(_L0_cond_ref(x, cond_256[:, None, :], L0_cond_rms_w, L0_cond_wg_W, L0_cond_wg_b, L0_cond_gg_W, L0_cond_gg_b, L0_cond_W1, L0_cond_b1, L0_cond_W2, L0_cond_b2, L0_cond_W3, L0_cond_b3), L0_attn_Wv, L0_attn_bv, L0_attn_Wo, L0_attn_bo)
    x = x + _L0_ffn_ref(_L0_cond2_ref(x, cond_256, L0_cond2_Wq, L0_cond2_Wk, L0_cond2_Wv, L0_cond2_Wo, L0_cond2_g1w, L0_cond2_g1b, L0_cond2_b1w, L0_cond2_b1b, L0_cond2_g2w, L0_cond2_g2b, L0_cond2_b2w, L0_cond2_b2b, L0_cond2_gate_w, L0_cond2_hid_w, L0_cond2_out_w), L0_ffn_slot_query, L0_ffn_d_Wq, L0_ffn_d_Wk, L0_ffn_d_Wv, L0_ffn_d_Wo, L0_ffn_d_bq, L0_ffn_d_bk, L0_ffn_d_bv, L0_ffn_d_bo, L0_ffn_c_Wq, L0_ffn_c_Wk, L0_ffn_c_Wv, L0_ffn_c_Wo, L0_ffn_c_bq, L0_ffn_c_bk, L0_ffn_c_bv, L0_ffn_c_bo, L0_ffn_e_ln_g, L0_ffn_e_ln_b, L0_ffn_e_W1, L0_ffn_e_b1, L0_ffn_e_Wg, L0_ffn_e_bg, L0_ffn_e_W2, L0_ffn_e_b2)
    return x

_drawn_inputs = setup_inputs


def setup_inputs(seed=0):
    import zlib

    import numpy as np

    out = dict(_drawn_inputs(seed))
    spreads = {'L0_cond_rms_w': (1.0, 0.2),
     'L0_cond_wg_b': (0.0, 0.1),
     'L0_cond_gg_b': (0.0, 0.1),
     'L0_cond_b1': (0.0, 0.1),
     'L0_cond_b2': (0.0, 0.1),
     'L0_cond_b3': (0.0, 0.1),
     'L0_cond2_g1b': (1.0, 0.2),
     'L0_cond2_b1b': (0.0, 0.1),
     'L0_cond2_g2b': (1.0, 0.2),
     'L0_cond2_b2b': (0.0, 0.1),
     'L0_ffn_d_bq': (0.0, 0.1),
     'L0_ffn_d_bk': (0.0, 0.1),
     'L0_ffn_d_bv': (0.0, 0.1),
     'L0_ffn_d_bo': (0.0, 0.1),
     'L0_ffn_c_bq': (0.0, 0.1),
     'L0_ffn_c_bk': (0.0, 0.1),
     'L0_ffn_c_bv': (0.0, 0.1),
     'L0_ffn_c_bo': (0.0, 0.1),
     'L0_ffn_e_ln_g': (1.0, 0.2),
     'L0_ffn_e_ln_b': (0.0, 0.1),
     'L0_ffn_e_b1': (0.0, 0.1),
     'L0_ffn_e_bg': (0.0, 0.1),
     'L0_ffn_e_b2': (0.0, 0.1)}
    factors = {}
    for name, (base, spread) in spreads.items():
        noise = np.random.default_rng([zlib.crc32(name.encode()), seed]).standard_normal(out[name].shape)
        drawn = base * np.exp(spread * noise) if base else spread * noise
        out[name] = jnp.asarray(drawn.astype(out[name].dtype))
    for name, factor in factors.items():
        out[name] = (out[name] * factor).astype(out[name].dtype)
    return out
```

```python
from contextlib import ExitStack

import numpy as np

import concourse.bass as bass
from concourse import mybir

ALU = mybir.AluOpType
ACT = mybir.ActivationFunctionType
F32 = mybir.dt.float32
F32R = mybir.dt.float32r
BF16 = mybir.dt.bfloat16
U32 = mybir.dt.uint32
I32 = mybir.dt.int32
AX_X = mybir.AxisListType.X

P = 128
NB, S, D = 32, 64, 256
T = NB * S
TT = T // P
KD = D // P
DC = 64
E1, M1 = 8, 512
KM = M1 // P
SLOT = 256
NT = (2 * T + E1 * (SLOT - 1)) // SLOT
NH, DH = 16, 16
HC = P // DH
FH = 1024
NS = 16
EPS = 1e-6
LN_EPS = 1e-5
SCALE = float(DH) ** -0.5
PB = 2 * P
NBODY = T // PB


W_V1, W_O1, W_Q2, W_K2, W_V2, W_DQ, W_DK, W_DV, W_DO, W_CQ, W_CK, W_CV, W_CO = range(13)
ROW_BV1, ROW_BO1, ROW_DBO, ROW_CBO = range(4)
COL_BV1, COL_DBQ, COL_DBK, COL_DBV, COL_CBQ, COL_CBK, COL_CBV = range(7)


class Env:
    pass


def scope(nc, ctx, tag):
    def sb(name, shape, dt=F32):
        return ctx.enter_context(nc.sbuf_tensor(f"{tag}_{name}", shape, dt))

    def ps(name, shape, dt=F32):
        return ctx.enter_context(nc.psum_tensor(f"{tag}_{name}", shape, dt))

    sems = []

    def sem(name):
        sems.append(nc.alloc_semaphore(name=f"{tag}_{name}"))
        return sems[-1]

    @ctx.callback
    def _():
        if sems:
            nc.clear_and_free_semaphores(sems)
            nc.all_engine_barrier()
    return sb, ps, sem


def bc(ap, axis, n):
    shape = list(ap.shape)
    return ap.unsqueeze(axis).to_broadcast(shape[:axis] + [n] + shape[axis:])


def mm3(nc, out, ah, al, bh, bl, start, stop):
    nc.tensor.matmul(out, ah, bh, start=start, stop=False)
    nc.tensor.matmul(out, al, bh, start=False, stop=False)
    return nc.tensor.matmul(out, ah, bl, start=False, stop=stop)


def f32(ap):
    return ap.bitcast(F32)


def route(nc, g, dr):
    with ExitStack() as ctx:
        sb, ps, sem = scope(nc, ctx, "route")
        zero = sb("zero", [P, 2048])
        cond_aug = sb("cond_aug", [DC + 2, NB])
        condx = sb("condx", [DC + 2, T])
        gg_aug = sb("gg_aug", [DC + 2, E1])
        wg = sb("wg", [P, KD, E1])
        rms = sb("rms", [P, KD])
        wgs = sb("wgs", [P, KD, 32])
        xT = sb("xT", [P, KD, T])
        sq = sb("sq", [P, TT, D])
        ss = sb("ss", [P, TT])
        rr = sb("rr", [P, TT])
        lT = sb("lT", [P, 512])
        lg = sb("lg", [P, TT, E1])
        gt = sb("gt", [P, TT, E1])
        tmp = sb("tmp", [P, TT, E1])
        col = sb("col", [P, TT])
        oh1 = sb("oh1", [P, TT, E1])
        oh2 = sb("oh2", [P, TT, E1])
        ohb = sb("ohb", [P, TT, E1])
        cum = [sb(f"cum{i}", [P, TT, E1]) for i in range(2)]
        slotf = sb("slotf", [P, TT, E1])
        cmp1 = sb("cmp1", [P, E1, E1])
        cmp2 = sb("cmp2", [P, NT, E1])
        ntl = sb("ntl", [P, E1])
        nin = [sb(f"nin{i}", [P, E1]) for i in range(2)]
        tef = sb("tef", [P, NT])
        pT = [ps(f"pT{i}", [P, 512]) for i in range(3)]
        pG = ps("pG", [P, 512])
        pC = ps("pC", [P, TT, E1])
        pL = ps("pL", [P, 512])
        pR = ps("pR", [P, TT, E1])
        pS = ps("pS", [P, TT, E1])

        zero_set, x_in, small_in, const_in = sem("zero_set"), sem("x_in"), sem("small_in"), sem("r_const_in")
        zero_out, late_in = sem("zero_out"), sem("late_in")
        xT_ps, xT_dve, xT_act = sem("xT_ps"), sem("xT_dve"), sem("xT_act")
        sumsq, root = sem("sumsq"), sem("root")
        cond_ps, gateT_ps, gateT_sb, gate_ps = sem("cond_ps"), sem("gateT_ps"), sem("gateT_sb"), sem("gate_ps")
        logits, expd, onehot, rank_ps = sem("logits"), sem("expd"), sem("onehot"), sem("rank_ps")
        condx_ok = sem("condx_ok")
        slots, scat, wgs_ok, dv, recip = sem("slots"), sem("scat"), sem("wgs_ok"), sem("r_dv"), sem("recip")

        block = ctx.enter_context(nc.Block())

        @block.sync
        def _(sp):
            sp.dma_start(g.x[:, :, :], dr.x_tm).then_inc(x_in, 16)
            sp.wait_ge(zero_set, 1)
            xs = dr.xs.rearrange("(n p) c -> n p c", p=P)
            for j in range(0, NT * SLOT // P, 8):
                n = min(8, NT * SLOT // P - j)
                sp.dma_start(xs[j:j + n].rearrange("n p c -> p n c"),
                             zero[:, 0:n * D].rearrange("p (n c) -> p n c", c=D)).then_inc(zero_out, 16)
            sp.dma_start(g.w_small[:, :, :, :], dr.w_small).then_inc(late_in, 16)
            sp.dma_start(g.wo4[:, :, :], dr.wo4).then_inc(late_in, 16)
            sp.dma_start(g.rows[:, :, :], dr.rows.to_broadcast([P, 4, D])).then_inc(late_in, 16)
            sp.dma_start(g.cols[:, :, :], dr.cols).then_inc(late_in, 16)
            sp.dma_start(g.batchmask[:, :], dr.batchmask).then_inc(late_in, 16)
            sp.wait_ge(late_in, 16 * 5)

        @block.gpsimd
        def _(pool):
            nc.gpsimd.memset(zero[:, :], 0.0).then_inc(zero_set, 1)
            pool.wait_ge(slots, 2)
            pool.wait_ge(zero_out, 16 * ((NT * SLOT // P + 7) // 8))
            pool.wait_ge(x_in, 16)
            for c in range(2):
                for t in range(TT):
                    nc.gpsimd.indirect_dma_start(
                        out=dr.xs, out_offset=bass.IndirectOffsetOnAxis(ap=g.slot[c][:, t:t + 1], axis=0),
                        in_=g.x[:, t, :], in_offset=None).then_inc(scat, 16)
            pool.wait_ge(scat, 16 * 2 * TT)

        @block.scalar
        def _(act):
            act.dma_start(g.ident[:, :], dr.ident).then_inc(const_in, 16)
            act.dma_start(g.tri[:, :], dr.tri).then_inc(const_in, 16)
            act.dma_start(g.rev[:, :], dr.rev).then_inc(const_in, 16)
            act.dma_start(g.headmask[:, :], dr.headmask).then_inc(const_in, 16)
            act.dma_start(cond_aug[0:DC, :], dr.condT).then_inc(small_in, 16)
            act.dma_start(cond_aug[DC:DC + 2, :], dr.ones[0:2, 0:NB]).then_inc(small_in, 16)
            act.dma_start(gg_aug[0:DC, :], dr.gg_W).then_inc(small_in, 16)
            act.dma_start(gg_aug[DC:DC + 1, :], dr.gg_b).then_inc(small_in, 16)
            act.dma_start(gg_aug[DC + 1:DC + 2, :], dr.wg_b).then_inc(small_in, 16)
            act.dma_start(wg[:, :, :], dr.wg_W).then_inc(small_in, 16)
            act.dma_start(rms[:, :], dr.rms_w).then_inc(small_in, 16)
            act.wait_ge(x_in, 16)
            for t in range(TT):
                nc.scalar.activation(sq[:, t, :], g.x[:, t, :], ACT.Square, accum_out=ss[:, t:t + 1]).then_inc(sumsq, 1)
                if t % 4 == 3:
                    i = t // 2
                    act.wait_ge(xT_ps, i + 1)
                    nc.scalar.activation(xT[:, :, i * PB:(i + 1) * PB],
                                         pT[i % 3][:, :].rearrange("p (k n) -> p k n", k=KD), ACT.Copy).then_inc(xT_act, 1)
            act.wait_ge(recip, 1)
            nc.scalar.activation(rr[:, :], rr[:, :], ACT.Sqrt).then_inc(root, 1)
            act.wait_ge(gateT_ps, 1)
            nc.scalar.activation(lT[:, :], pG[:, :], ACT.Copy).then_inc(gateT_sb, 1)
            act.wait_ge(logits, 1)
            nc.scalar.activation(gt[:, :, :], lg[:, :, :], ACT.Exp).then_inc(expd, 1)

        @block.tensor
        def _(pe):
            pe.wait_ge(const_in, 64)
            pe.wait_ge(small_in, 16 * 7)
            pe.wait_ge(condx_ok, 1)
            for t in range(TT):
                last = nc.tensor.matmul(pC[:, t, :], condx[:, t * P:(t + 1) * P], gg_aug[:, :],
                                        start=True, stop=True)
            last.then_inc(cond_ps, 1)
            pe.wait_ge(x_in, 16)
            for i in range(NBODY):
                if i >= 3:
                    pe.wait_ge(xT_dve if (i - 3) % 2 == 0 else xT_act, (i - 3) // 2 + 1)
                for j in range(2):
                    for k in range(KD):
                        last = nc.tensor.transpose(pT[i % 3][:, k * PB + j * P:k * PB + (j + 1) * P],
                                                   g.x[:, 2 * i + j, k * P:(k + 1) * P], g.ident[:, :])
                last.then_inc(xT_ps, 1)
            pe.wait_ge(xT_dve, NBODY // 2)
            pe.wait_ge(xT_act, NBODY // 2)
            pe.wait_ge(wgs_ok, KD)
            for k in range(KD):
                for c in range(4):
                    last = nc.tensor.matmul(pG[32 * c:32 * c + 32, :], wgs[:, k, :], xT[:, k, c * 512:(c + 1) * 512],
                                            start=(k == 0), stop=(k == KD - 1))
            last.then_inc(gateT_ps, 1)
            pe.wait_ge(gateT_sb, 1)
            for j in range(4):
                last = nc.tensor.transpose(pL[:, j * P:(j + 1) * P], lT[:, j * P:(j + 1) * P], g.ident[:, :])
            last.then_inc(gate_ps, 1)
            pe.wait_ge(onehot, 1)
            nc.tensor.matmul(pR[:, :, :], g.tri[:, 0:P], ohb[:, :, :], start=True, stop=True)
            nc.tensor.matmul(pS[:, :, :], g.tri[:, P:2 * P], ohb[:, :, :], start=True, stop=True).then_inc(rank_ps, 1)

        @block.vector
        def _(dve):
            n = [0]

            def step(ins):
                n[0] += 1
                ins.then_inc(dv, 1)
                dve.wait_ge(dv, n[0])
            v = nc.vector
            step(v.memset(wgs[:, :, :], 0.0))
            dve.wait_ge(small_in, 16 * 7)
            v.tensor_copy(condx[:, :].rearrange("p (b s) -> p b s", s=S), bc(cond_aug[:, :], 2, S)).then_inc(condx_ok, 1)
            for k in range(KD):
                v.tensor_scalar(wgs[:, k, 0:E1], wg[:, k, :], rms[:, k:k + 1], None, ALU.mult).then_inc(wgs_ok, 1)
            for i in range(0, NBODY, 2):
                dve.wait_ge(xT_ps, i + 1)
                v.tensor_copy(xT[:, :, i * PB:(i + 1) * PB],
                              pT[i % 3][:, :].rearrange("p (k n) -> p k n", k=KD)).then_inc(xT_dve, 1)
            dve.wait_ge(sumsq, TT)
            step(v.tensor_scalar(ss[:, :], ss[:, :], 1.0 / D, EPS, ALU.mult, ALU.add))
            v.reciprocal(rr[:, :], ss[:, :]).then_inc(recip, 1)
            dve.wait_ge(root, 1)
            dve.wait_ge(gate_ps, 1)
            step(v.tensor_tensor(lg[:, :, :].rearrange("p (c j) e -> p c j e", c=4),
                                 pL[:, :].rearrange("p (j c e) -> p c j e", j=4, c=4)[:, :, :, 0:E1],
                                 bc(rr[:, :].rearrange("p (c j) -> p c j", c=4), 3, E1), ALU.mult))
            dve.wait_ge(cond_ps, 1)
            step(v.tensor_tensor(lg[:, :, :], lg[:, :, :], pC[:, :, :], ALU.add))
            step(v.tensor_reduce(col[:, :], lg[:, :, :], AX_X, ALU.max))
            v.tensor_tensor(lg[:, :, :], lg[:, :, :], bc(col[:, :], 2, E1), ALU.subtract).then_inc(logits, 1)
            dve.wait_ge(expd, 1)
            step(v.tensor_reduce(col[:, :], gt[:, :, :], AX_X, ALU.add))
            step(v.reciprocal(col[:, :], col[:, :]))
            step(v.tensor_tensor(gt[:, :, :], gt[:, :, :], bc(col[:, :], 2, E1), ALU.mult))
            rev = bc(g.rev[:, 0:E1], 1, TT)
            for c, oh in enumerate((oh1, oh2)):
                step(v.tensor_reduce(g.weight[c][:, :], gt[:, :, :], AX_X, ALU.max))
                step(v.tensor_tensor(tmp[:, :, :], gt[:, :, :], bc(g.weight[c][:, :], 2, E1), ALU.is_equal))
                step(v.tensor_tensor(tmp[:, :, :], tmp[:, :, :], rev, ALU.mult))
                step(v.tensor_reduce(col[:, :], tmp[:, :, :], AX_X, ALU.max))
                step(v.tensor_tensor(oh[:, :, :], rev, bc(col[:, :], 2, E1), ALU.is_equal))
                if c == 0:
                    step(v.scalar_tensor_tensor(gt[:, :, :], oh[:, :, :], -2.0, gt[:, :, :], ALU.mult, ALU.add))
            v.tensor_tensor(ohb[:, :, :], oh1[:, :, :], oh2[:, :, :], ALU.add).then_inc(onehot, 1)
            dve.wait_ge(rank_ps, 1)
            step(v.tensor_copy(cum[0][:, :, :], pS[:, :, :]))
            a = 0
            for sh in (1, 2, 4, 8):
                v.tensor_copy(cum[1 - a][:, 0:sh, :], cum[a][:, 0:sh, :])
                step(v.tensor_tensor(cum[1 - a][:, sh:TT, :], cum[a][:, sh:TT, :], cum[a][:, 0:TT - sh, :], ALU.add))
                a = 1 - a
            step(v.tensor_tensor(cmp1[:, :, :], bc(cum[a][:, TT - 1, :], 2, E1), bc(g.rev[:, 32:32 + E1], 1, E1), ALU.is_gt))
            step(v.tensor_reduce(ntl[:, :], cmp1[:, :, :], AX_X, ALU.add))
            step(v.tensor_copy(nin[0][:, :], ntl[:, :]))
            b = 0
            for sh in (1, 2, 4):
                v.tensor_copy(nin[1 - b][:, 0:sh], nin[b][:, 0:sh])
                step(v.tensor_tensor(nin[1 - b][:, sh:E1], nin[b][:, sh:E1], nin[b][:, 0:E1 - sh], ALU.add))
                b = 1 - b
            step(v.tensor_tensor(cmp2[:, :, :], bc(nin[b][:, :], 1, NT), bc(g.rev[:, 64:64 + NT], 2, E1), ALU.is_le))
            step(v.tensor_reduce(tef[:, :], cmp2[:, :, :], AX_X, ALU.add))
            step(v.tensor_scalar(g.tile_expert[:, :], tef[:, :], float(E1 - 1), None, ALU.min))
            step(v.tensor_tensor(nin[1 - b][:, :], nin[b][:, :], ntl[:, :], ALU.subtract))
            step(v.tensor_tensor(slotf[:, :, :], cum[a][:, :, :], pS[:, :, :], ALU.subtract))
            step(v.tensor_tensor(slotf[:, :, :], slotf[:, :, :], pR[:, :, :], ALU.add))
            step(v.scalar_tensor_tensor(slotf[:, :, :], bc(nin[1 - b][:, :], 1, TT), float(SLOT), slotf[:, :, :],
                                        ALU.mult, ALU.add))
            for c, oh in enumerate((oh1, oh2)):
                step(v.tensor_tensor(tmp[:, :, :], oh[:, :, :], slotf[:, :, :], ALU.mult))
                step(v.tensor_reduce(col[:, :], tmp[:, :, :], AX_X, ALU.add))
                v.tensor_copy(g.slot[c][:, :], col[:, :]).then_inc(slots, 1)
                dve.wait_ge(slots, c + 1)


def experts(nc, g, dr):
    with ExitStack() as ctx:
        sb, ps, sem = scope(nc, ctx, "moe")
        WN = (KD * M1, KM * M1, KM * D)
        raw = [sb(f"raw{l}", [P, WN[l]]) for l in range(3)]
        wh = [[sb(f"wh{l}{a}", [P, WN[l]], F32R) for l in range(3)] for a in range(2)]
        wl = [[sb(f"wl{l}{a}", [P, WN[l]], F32R) for l in range(3)] for a in range(2)]
        b12 = [sb(f"b12{a}", [P, 2 * KM]) for a in range(2)]
        b3 = [sb(f"b3{a}", [P, D]) for a in range(2)]
        xr = [sb(f"xr{a}", [P, 2, D]) for a in range(2)]
        xh = sb("xh", [P, KD, SLOT], F32R)
        xl = sb("xl", [P, KD, SLOT], F32R)
        ht = [sb(f"ht{l}", [P, KM, SLOT]) for l in range(2)]
        hh = [sb(f"hh{l}", [P, KM, SLOT], F32R) for l in range(2)]
        hl = [sb(f"hl{l}", [P, KM, SLOT], F32R) for l in range(2)]
        ys = [sb(f"ysb{a}", [P, 2, D]) for a in range(2)]
        pX = ps("pX", [P, KD, SLOT])
        pH = [[ps(f"pH{l}{i}", [P, 2, SLOT]) for i in range(2)] for l in range(2)]
        pY = ps("pY", [P, 2, D])

        raw_in = [sem(f"raw_in{l}") for l in range(3)]
        x_in = [sem(f"x_in{a}") for a in range(2)]
        b_in = [sem(f"b_in{a}") for a in range(2)]
        y_out = [sem(f"y_out{a}") for a in range(2)]
        wh_ok = [sem(f"wh_ok{l}") for l in range(3)]
        wl_ok = [sem(f"wl_ok{l}") for l in range(3)]
        xT_ps, xh_ok, xl_ok = sem("xT_ps"), sem("xh_ok"), sem("xl_ok")
        h_ps = [sem(f"h_ps{l}") for l in range(2)]
        h_t = [sem(f"h_t{l}") for l in range(2)]
        hh_ok = [sem(f"hh_ok{l}") for l in range(2)]
        hl_ok = [sem(f"hl_ok{l}") for l in range(2)]
        y_ps, y_ok = sem("y_ps"), sem("y_ok")

        block = ctx.enter_context(nc.Block())

        def tiles(eng, step):
            step(0, 0, first=True)
            with eng.Fori(0, (NT - 3) // 2) as p:
                step(2 * p + 1, 1)
                step(2 * p + 2, 0)
            for j in range(1 + 2 * ((NT - 3) // 2), NT):
                step(j, j % 2, last=(j == NT - 1))

        def landed(j, a):
            return 8 * (j - a) + 16

        xs_v = dr.xs.rearrange("(n s p) c -> n p s c", p=P, s=2)
        ys_v = dr.ys.rearrange("(n s p) c -> n p s c", p=P, s=2)

        @block.sync
        def _(sp):
            def step(j, a, first=False, last=False):
                e = sp.value_load(g.tile_expert[0:1, bass.ds(j, 1)], min_val=0, max_val=E1 - 1)
                k = j if isinstance(j, int) else None
                early = k is not None and k < 2
                if not early:
                    sp.wait_ge(xT_ps, j - 1)
                sp.dma_start(xr[a][:, :, :], xs_v[bass.ds(j, 1)].rearrange("o p s c -> (o p) s c")).then_inc(x_in[a], 16)
                for l in range(3):
                    if not first:
                        sp.wait_ge(wl_ok[l], j)
                        sp.wait_ge(wh_ok[l], j)
                    sp.dma_start(raw[l][:, :], dr.w[l][bass.ds(e, 1)].rearrange("o p n -> (o p) n")).then_inc(raw_in[l], 16)
                if not early:
                    sp.wait_ge(h_t[1], 2 * (j - 1))
                    sp.wait_ge(y_ok, j - 1)
                sp.dma_start(b12[a][:, :], dr.b12[bass.ds(e, 1)].rearrange("o p n -> (o p) n")).then_inc(b_in[a], 16)
                sp.dma_start(b3[a][:, :], dr.b3[bass.ds(e, 1)].rearrange("o p n -> (o p) n").to_broadcast([P, D])).then_inc(b_in[a], 16)
            tiles(sp, step)

        @block.gpsimd
        def _(pool):
            def step(j, a, first=False, last=False):
                pool.wait_ge(wh_ok[1], j + 1)
                if not (isinstance(j, int) and j < 2):
                    pool.wait_ge(h_ps[1], 2 * (j - 1))
                nc.gpsimd.tensor_tensor(wl[a][1][:, :], raw[1][:, :], f32(wh[a][1][:, :]), ALU.subtract).then_inc(wl_ok[1], 1)
                if first:
                    return
                store(j - 1, 1 - a)

            def store(j, a):
                pool.wait_ge(y_ok, j + 1)
                pool.dma_start(ys_v[bass.ds(j, 1)].rearrange("o p s c -> (o p) s c"), ys[a][:, :, :]).then_inc(y_out[a], 16)
            tiles(pool, step)
            store(NT - 1, (NT - 1) % 2)
            pool.wait_ge(y_out[0], 16 * ((NT + 1) // 2))
            pool.wait_ge(y_out[1], 16 * (NT // 2))

        @block.tensor
        def _(pe):
            def turn(j, a):
                pe.wait_ge(x_in[a], landed(j, a))
                if not (isinstance(j, int) and j == 0):
                    pe.wait_ge(xh_ok, j)
                    pe.wait_ge(xl_ok, j)
                for s in range(2):
                    for k in range(KD):
                        last = nc.tensor.transpose(pX[:, k, s * P:(s + 1) * P], xr[a][:, s, k * P:(k + 1) * P],
                                                   g.ident[:, :])
                last.then_inc(xT_ps, 1)

            def layer(j, a, l):
                pe.wait_ge(wh_ok[l], j + 1)
                pe.wait_ge(wl_ok[l], j + 1)
                kin = KD if l == 0 else KM
                ih, il = (xh, xl) if l == 0 else (hh[0], hl[0])
                if l == 0:
                    pe.wait_ge(xl_ok, j + 1)
                    pe.wait_ge(xh_ok, j + 1)
                w_h = wh[a][l][:, :].rearrange("p (k m) -> p k m", k=kin)
                w_l = wl[a][l][:, :].rearrange("p (k m) -> p k m", k=kin)
                for m in range(KM):
                    if m % 2 == 0 and not (isinstance(j, int) and j == 0):
                        pe.wait_ge(h_t[l], 2 * j - 1 + m // 2)
                    for k in range(kin):
                        if l == 1 and m == 0 and k % 2 == 0:
                            pe.wait_ge(hh_ok[0], 2 * j + 1 + k // 2)
                            pe.wait_ge(hl_ok[0], 2 * j + 1 + k // 2)
                        last = mm3(nc, pH[l][m // 2][:, m % 2, :], w_h[:, k, m * P:(m + 1) * P],
                                   w_l[:, k, m * P:(m + 1) * P], ih[:, k, :], il[:, k, :], k == 0, k == kin - 1)
                    if m % 2 == 1:
                        last.then_inc(h_ps[l], 1)

            def out_layer(j, a):
                pe.wait_ge(wh_ok[2], j + 1)
                pe.wait_ge(wl_ok[2], j + 1)
                pe.wait_ge(hh_ok[1], 2 * j + 2)
                pe.wait_ge(hl_ok[1], 2 * j + 2)
                if not (isinstance(j, int) and j == 0):
                    pe.wait_ge(y_ok, j)
                w_h = wh[a][2][:, :].rearrange("p (k n) -> p k n", k=KM)
                w_l = wl[a][2][:, :].rearrange("p (k n) -> p k n", k=KM)
                for s in range(2):
                    for k in range(KM):
                        last = mm3(nc, pY[:, s, :], hh[1][:, k, s * P:(s + 1) * P], hl[1][:, k, s * P:(s + 1) * P],
                                   w_h[:, k, :], w_l[:, k, :], k == 0, k == KM - 1)
                last.then_inc(y_ps, 1)

            def step(j, a, first=False, last=False):
                layer(j, a, 0)
                if not first:
                    out_layer(j - 1, 1 - a)
                if not last:
                    turn(j + 1, 1 - a)
                layer(j, a, 1)
            turn(0, 0)
            tiles(pe, step)
            out_layer(NT - 1, (NT - 1) % 2)

        @block.scalar
        def _(act):
            def split_w(j, a, l):
                act.wait_ge(raw_in[l], 16 * j + 16)
                if not (isinstance(j, int) and j < 2):
                    if l < 2:
                        act.wait_ge(h_ps[l], 2 * (j - 1))
                    else:
                        act.wait_ge(y_ps, j - 1)
                nc.scalar.activation(wh[a][l][:, :], raw[l][:, :], ACT.Copy).then_inc(wh_ok[l], 1)

            def split_x(j):
                act.wait_ge(xT_ps, j + 1)
                if not (isinstance(j, int) and j == 0):
                    act.wait_ge(h_ps[0], 2 * j)
                nc.scalar.activation(xh[:, :, :], pX[:, :, :], ACT.Copy).then_inc(xh_ok, 1)

            def relu(j, a, l):
                if l == 0:
                    act.wait_ge(b_in[a], 2 * landed(j, a))
                for i in range(2):
                    act.wait_ge(h_ps[l], 2 * j + i + 1)
                    if not (isinstance(j, int) and j == 0):
                        act.wait_ge(hl_ok[l], 2 * j - 1 + i)
                    for m in range(2):
                        last = nc.scalar.activation(ht[l][:, 2 * i + m, :], pH[l][i][:, m, :], ACT.Relu,
                                                    bias=b12[a][:, l * KM + 2 * i + m:l * KM + 2 * i + m + 1])
                    last.then_inc(h_t[l], 1)

            def step(j, a, first=False, last=False):
                relu(j, a, 0)
                if not last:
                    split_w(j + 1, 1 - a, 0)
                    split_x(j + 1)
                    split_w(j + 1, 1 - a, 1)
                relu(j, a, 1)
                if not last:
                    split_w(j + 1, 1 - a, 2)
            split_w(0, 0, 0)
            split_x(0)
            split_w(0, 0, 1)
            split_w(0, 0, 2)
            tiles(act, step)

        @block.vector
        def _(dve):
            v = nc.vector

            def split_w(j, a, l):
                dve.wait_ge(wh_ok[l], j + 1)
                v.tensor_tensor(wl[a][l][:, :], raw[l][:, :], f32(wh[a][l][:, :]), ALU.subtract).then_inc(wl_ok[l], 1)

            def split_x(j):
                dve.wait_ge(xh_ok, j + 1)
                v.tensor_tensor(xl[:, :, :], pX[:, :, :], f32(xh[:, :, :]), ALU.subtract).then_inc(xl_ok, 1)

            def split_h(j, l):
                for i in range(2):
                    dve.wait_ge(h_t[l], 2 * j + i + 1)
                    if not (isinstance(j, int) and j == 0) and i == 0:
                        if l == 0:
                            dve.wait_ge(h_ps[1], 2 * j)
                        else:
                            dve.wait_ge(y_ps, j)
                    s = slice(2 * i, 2 * i + 2)
                    v.tensor_copy(hh[l][:, s, :], ht[l][:, s, :]).then_inc(hh_ok[l], 1)
                    dve.wait_ge(hh_ok[l], 2 * j + i + 1)
                    v.tensor_tensor(hl[l][:, s, :], ht[l][:, s, :], f32(hh[l][:, s, :]), ALU.subtract).then_inc(hl_ok[l], 1)

            def result(j, a):
                dve.wait_ge(y_ps, j + 1)
                dve.wait_ge(b_in[a], 2 * landed(j, a))
                if not (isinstance(j, int) and j < 2):
                    dve.wait_ge(y_out[a], landed(j, a) - 16)
                v.tensor_tensor(ys[a][:, :, :], pY[:, :, :], bc(b3[a][:, :], 1, 2), ALU.add).then_inc(y_ok, 1)

            def step(j, a, first=False, last=False):
                split_h(j, 0)
                if not last:
                    split_w(j + 1, 1 - a, 0)
                if not first:
                    result(j - 1, 1 - a)
                if not last:
                    split_x(j + 1)
                split_h(j, 1)
                if not last:
                    split_w(j + 1, 1 - a, 2)
            split_w(0, 0, 0)
            split_x(0)
            split_w(0, 0, 2)
            tiles(dve, step)
            result(NT - 1, (NT - 1) % 2)


KX_DVE = 5


def self_attention(nc, g, dr, first, w_raw, wo_raw, res, out, ssq):
    with ExitStack() as ctx:
        sb, ps, sem = scope(nc, ctx, "attn1" if first else "attn2")
        nw = len(w_raw)
        NK = KD if first else 1
        wh = [sb(f"wh{n}", [P, KD, D], F32R) for n in range(nw)]
        wl = [sb(f"wl{n}", [P, KD, D], F32R) for n in range(nw)]
        if first:
            otm = [sb(f"otm{a}", [P, 8, 2 * DH]) for a in range(2)]
            gat = [[sb(f"gat{c}{a}", [P, D]) for a in range(2)] for c in range(2)]
            ya = [sb(f"ya{a}", [P, D]) for a in range(2)]
        else:
            woh = sb("woh", [P, 4, D], F32R)
            wol = sb("wol", [P, 4, D], F32R)
            oh = sb("oh", [P, 4, 2, S], F32R)
            ol = sb("ol", [P, 4, 2, S], F32R)
            junk = [sb(f"junk{a}", [P, D]) for a in range(2)]
            u1 = sb("u1", [P, KD, PB])
            u2 = sb("u2", [P, KD, PB])
        yt = [sb(f"yt{a}", [P, D]) for a in range(2)]
        ih = sb("ih", [P, KD, 4, 2, S], F32R)
        il = sb("il", [P, KD, 4, 2, S], F32R)
        qT = None if first else sb("qT", [P, KD, PB])
        kT = sb("kT", [P, KD, PB])
        kx = sb("kx", [P, KD, HC, PB])
        vst = [sb(f"vst{a}", [P, 8, 2, 2, DH]) for a in range(2)]
        mx = [sb(f"mx{c}", [P, HC]) for c in range(2)]
        sm = [sb(f"sm{c}", [P, HC]) for c in range(2)]
        rc = [sb(f"rc{c}", [P, HC]) for c in range(2)]
        df = [sb(f"df{c}", [P, HC, S]) for c in range(2)]
        ex = [sb(f"ex{c}", [P, HC, S]) for c in range(2)]
        pn = [sb(f"pn{c}", [P, HC, S]) for c in range(2)]
        pt = [sb(f"pt{c}", [P, 4, P]) for c in range(2)]

        b0 = ps("b0", [P, 512])
        b1 = ps("b1", [P, 512])
        b2 = ps("b2", [P, 512])
        pS = [ps(f"pS{c}", [P, HC, S]) for c in range(2)]
        pT = [ps(f"pT{c}", [P, 4, P]) for c in range(2)]
        pV = ps("pV", [P, 512])
        pVf = pV[:, :].rearrange("p (j b s) -> p j b s", j=4, b=2)
        pVt = pV[:, :].rearrange("p (j b n) -> p j b n", j=8, b=2)

        wh_ok, wl_ok, vz_ok = sem("wh_ok"), sem("wl_ok"), sem("vz_ok")
        gat_in = [[sem(f"gat_in{c}{a}") for a in range(2)] for c in range(2)]
        ya_ok, yt_ok, x_ps, u1_ok, u2_ok, ih_ok, il_ok = (sem(n) for n in ("ya_ok", "yt_ok", "x_ps", "u1_ok", "u2_ok", "ih_ok", "il_ok"))
        q_ps, k_ps, v_ps, q_sb, k_sb, kx_dve, kx_act, v_sb = (sem(n) for n in ("q_ps", "k_ps", "v_ps", "q_sb", "k_sb", "kx_dve", "kx_act", "v_sb"))
        s_ps, mx_ok, df_ok, ex_ok, sm_ok, rc_ok, pn_ok = (sem(n) for n in ("s_ps", "mx_ok", "df_ok", "ex_ok", "sm_ok", "rc_ok", "pn_ok"))
        pt_ps, pt_sb, pv_ps, oh_ok, ol_ok, o_ps, o_sb, ot_ok, sq_ok = (sem(n) for n in ("pt_ps", "pt_sb", "pv_ps", "oh_ok", "ol_ok", "o_ps", "o_sb", "ot_ok", "sq_ok"))
        ff_in = sem("ff_in")
        o_out = [sem(f"o_out{a}") for a in range(2)]

        block = ctx.enter_context(nc.Block())

        def bodies(eng, body):
            body(0)
            body(1)
            with eng.Fori(2, NBODY - 1) as i:
                body(i)
            body(NBODY - 1)

        def opening(i):
            return isinstance(i, int) and i == 0

        def closing(i):
            return isinstance(i, int) and i == NBODY - 1

        def after(eng, semaphore, value):
            if not (isinstance(value, int) and value <= 0):
                eng.wait_ge(semaphore, value)

        if first:
            @block.sync
            def _(sp):
                def store(i, a):
                    sp.wait_ge(ot_ok, 2 * (2 * i + a) + 2)
                    for b in range(2):
                        sp.dma_start(dr.heads[bass.ds(4 * i + 2 * a + b, 1)].rearrange("o h q d -> (o q) h d"),
                                     otm[a][b * S:(b + 1) * S, :, :].rearrange("p j (s d) -> p (j s) d", s=2)).then_inc(o_out[a], 16)
                sp.dma_start(g.w_ff[:, :, :], dr.w_ff).then_inc(ff_in, 16)
                with sp.Fori(0, NBODY) as i:
                    store(i, 0)
                    store(i, 1)
                sp.wait_ge(ff_in, 16)
                for a in range(2):
                    sp.wait_ge(o_out[a], 16 * 2 * NBODY)

        @block.gpsimd
        def _(pool):
            for a in range(2):
                nc.gpsimd.memset(vst[a][:, :, :, :, :], 0.0).then_inc(vz_ok, 1)

            def gather(i):
                for a in range(2):
                    t = 2 * i + a
                    for c in range(2):
                        after(pool, ya_ok if c == 0 else yt_ok, t - 1)
                        nc.gpsimd.indirect_dma_start(
                            out=gat[c][a][:, :], out_offset=None, in_=dr.ys,
                            in_offset=bass.IndirectOffsetOnAxis(ap=g.slot[c][:, t:t + 1], axis=0)).then_inc(gat_in[c][a], 16)

            def softmax_end(t):
                for c in range(2):
                    pool.wait_ge(rc_ok, 2 * t + c + 1)
                    after(pool, pt_ps, 2 * t + c - 1)
                    nc.gpsimd.tensor_tensor(pn[c][:, :, :], ex[c][:, :, :], bc(rc[c][:, :], 2, S), ALU.mult).then_inc(pn_ok, 1)

            def biased(i):
                pool.wait_ge(u1_ok, i + 1)
                after(pool, il_ok, KD * i)
                after(pool, ih_ok, KD * i)
                v4 = lambda ap: ap.rearrange("p k (b s) -> p k b s", b=4)
                nc.gpsimd.tensor_tensor(v4(u2[:, :, :]), v4(u1[:, :, :]), bc(g.ada[:, 1, :, bass.ds(4 * i, 4)], 3, S), ALU.add).then_inc(u2_ok, 1)

            def body(i):
                if not first and not closing(i):
                    biased(i + 1)
                softmax_end(2 * i)
                if first and i + 2 < NBODY:
                    gather(i + 2)
                softmax_end(2 * i + 1)
            if first:
                gather(0)
                gather(1)
                for i in range(NBODY):
                    body(i)
            else:
                biased(0)
                bodies(pool, body)

        @block.tensor
        def _(pe):
            def turn(i):
                pe.wait_ge(yt_ok, 2 * i + 2)
                after(pe, v_sb, 2 * (2 * i - 1))
                for a in range(2):
                    for k in range(KD):
                        last = nc.tensor.transpose(b0[:, k * PB + a * P:k * PB + (a + 1) * P], yt[a][:, k * P:(k + 1) * P], g.ident[:, :])
                last.then_inc(x_ps, 1)

            def features(bank, n):
                for m in range(KD):
                    for k in range(KD):
                        last = mm3(nc, bank[:, m * PB:(m + 1) * PB], wh[n][:, k, m * P:(m + 1) * P], wl[n][:, k, m * P:(m + 1) * P],
                                   ih[:, k, :, 0, :], il[:, k, :, 0, :], k == 0, k == KD - 1)
                return last

            def queries_keys(i):
                pe.wait_ge(ih_ok, KD * (i + 1))
                pe.wait_ge(il_ok, KD * (i + 1))
                if not first:
                    after(pe, v_sb, 4 * i)
                    features(b1, 0).then_inc(q_ps, 1)
                    after(pe, o_sb, 2 * i - 2)
                after(pe, k_sb, NK * i)
                features(b2, 0 if first else 1).then_inc(k_ps, 1)

            def values(i, a):
                n = nw - 1
                if a == 1:
                    if first:
                        after(pe, v_sb, 4 * i)
                    else:
                        pe.wait_ge(q_sb, i + 1)
                bank = b1 if a else b0
                for b in range(2):
                    for k in range(KD):
                        last = mm3(nc, bank[:, b * D:(b + 1) * D], ih[:, k, 2 * a + b, :, :].rearrange("p r s -> p (r s)"),
                                   il[:, k, 2 * a + b, :, :].rearrange("p r s -> p (r s)"), wh[n][:, k, :], wl[n][:, k, :], k == 0, k == KD - 1)
                last.then_inc(v_ps, 1)

            def scores(i, a):
                t = 2 * i + a
                q = kT if first else qT
                if a == 0:
                    pe.wait_ge(k_sb, NK * (i + 1)) if first else pe.wait_ge(q_sb, i + 1)
                    pe.wait_ge(kx_dve, KX_DVE * (i + 1))
                    pe.wait_ge(kx_act, (HC - KX_DVE) * (i + 1))
                for c in range(2):
                    after(pe, df_ok, 2 * t + c - 1)
                    for b in range(2):
                        tok = slice(a * P + b * S, a * P + (b + 1) * S)
                        last = nc.tensor.matmul(pS[c][b * S:(b + 1) * S, :, :], q[:, c, tok], kx[:, c, :, tok], start=True, stop=True)
                    last.then_inc(s_ps, 1)

            def turn_weights(t):
                for c in range(2):
                    pe.wait_ge(pn_ok, 2 * t + c + 1)
                    after(pe, pt_sb, 2 * t + c - 1)
                    for j in range(4):
                        last = nc.tensor.transpose(pT[c][:, j, :], pn[c][:, 2 * j:2 * j + 2, :].rearrange("p h k -> p (h k)"), g.ident[:, :])
                    last.then_inc(pt_ps, 1)

            def results(t, a):
                pe.wait_ge(v_sb, 2 * (t + 1))
                if first:
                    after(pe, ot_ok, 2 * t)
                    for j in range(8):
                        if j % 4 == 0:
                            pe.wait_ge(pt_sb, 2 * t + j // 4 + 1)
                        last = nc.tensor.matmul(pV[:, j * S:(j + 1) * S], pt[j // 4][:, j % 4, :],
                                                vst[a][:, j, :, :, :].rearrange("p b s d -> p (b s d)"), start=True, stop=True)
                    last.then_inc(pv_ps, 1)
                    return
                after(pe, oh_ok, 2 * t)
                after(pe, ol_ok, 2 * t)
                for j in range(8):
                    if j % 4 == 0:
                        pe.wait_ge(pt_sb, 2 * t + j // 4 + 1)
                    last = nc.tensor.matmul(pVf[64 * (j % 2):64 * (j % 2) + 64, j // 2, :, :],
                                            vst[a][:, j, :, :, :].rearrange("p b s d -> p (b s d)"), pt[j // 4][:, j % 4, :], start=True, stop=True)
                last.then_inc(pv_ps, 1)

            def output(t, i):
                if first:
                    return
                after(pe, o_sb, t)
                pe.wait_ge(k_sb, NK * (i + 1))
                pe.wait_ge(oh_ok, 2 * t + 2)
                pe.wait_ge(ol_ok, 2 * t + 2)
                for j in range(4):
                    last = mm3(nc, b2[:, 0:D], oh[:, j, :, :].rearrange("p b s -> p (b s)"), ol[:, j, :, :].rearrange("p b s -> p (b s)"),
                               woh[:, j, :], wol[:, j, :], j == 0, j == 3)
                last.then_inc(o_ps, 1)

            def body(i):
                if not opening(i):
                    turn_weights(2 * i - 1)
                values(i, 0)
                if not opening(i):
                    output(2 * i - 2, i)
                scores(i, 0)
                if not opening(i):
                    results(2 * i - 1, 1)
                if not closing(i):
                    turn(i + 1)
                values(i, 1)
                scores(i, 1)
                if not opening(i):
                    output(2 * i - 1, i)
                turn_weights(2 * i)
                if not closing(i):
                    queries_keys(i + 1)
                results(2 * i, 0)
            turn(0)
            pe.wait_ge(wh_ok, nw if first else nw + 1)
            pe.wait_ge(wl_ok, nw if first else nw + 1)
            pe.wait_ge(vz_ok, 2)
            queries_keys(0)
            bodies(pe, body)
            turn_weights(TT - 1)
            output(TT - 2, NBODY - 1)
            results(TT - 1, 1)
            output(TT - 1, NBODY - 1)

        @block.scalar
        def _(act):
            for n in range(nw):
                nc.scalar.activation(wh[n][:, :, :], w_raw[n], ACT.Copy).then_inc(wh_ok, 1)
            if not first:
                nc.scalar.activation(woh[:, :, :], wo_raw, ACT.Copy).then_inc(wh_ok, 1)

            def scaled(i):
                for a in range(2):
                    after(act, x_ps, i)
                    nc.scalar.activation(yt[a][:, :], res[:, bass.ds(2 * i + a, 1), :].rearrange("p o n -> p (o n)"), ACT.Copy,
                                         scale=g.inv1[:, bass.ds(2 * i + a, 1)]).then_inc(yt_ok, 1)

            def high(i):
                act.wait_ge(x_ps if first else u2_ok, i + 1)
                after(act, v_ps, 2 * i)
                src = (b0[:, :] if first else u2[:, :, :].rearrange("p k n -> p (k n)")).rearrange("p (k b s) -> p k b s", k=KD, b=4)
                for k in range(KD):
                    last = nc.scalar.activation(ih[:, k, :, :, :], bc(src[:, k, :, :], 2, 2), ACT.Copy)
                    last.then_inc(ih_ok, 1)

            def keys(i):
                if not first:
                    act.wait_ge(q_ps, i + 1)
                    after(act, s_ps, 4 * i)
                    nc.scalar.activation(qT[:, :, :], b1[:, :].rearrange("p (k n) -> p k n", k=KD), ACT.Copy).then_inc(q_sb, 1)
                act.wait_ge(k_ps, i + 1)
                after(act, s_ps, 4 * i)
                after(act, kx_dve, KX_DVE * i)
                if first:
                    for m in range(KD):
                        last = nc.scalar.activation(kT[:, m, :], b2[:, m * PB:(m + 1) * PB], ACT.Identity, bias=g.cols[:, COL_BV1, m:m + 1])
                        last.then_inc(k_sb, 1)
                else:
                    nc.scalar.activation(kT[:, :, :], b2[:, :].rearrange("p (k n) -> p k n", k=KD), ACT.Copy).then_inc(k_sb, 1)

            def masked_keys(i):
                act.wait_ge(k_sb, NK * (i + 1))
                for h in range(KX_DVE, HC):
                    nc.scalar.activation(kx[:, :, h, :], kT[:, :, :], ACT.Copy, scale=g.headmask[:, h:h + 1]).then_inc(kx_act, 1)

            def exps(t, c):
                act.wait_ge(df_ok, 2 * t + c + 1)
                after(act, pn_ok, 2 * t + c - 1)
                nc.scalar.activation(ex[c][:, :, :], df[c][:, :, :], ACT.Exp, scale=SCALE).then_inc(ex_ok, 1)

            def values(i, a):
                if first:
                    return
                t = 2 * i + a
                act.wait_ge(v_ps, t + 1)
                after(act, pv_ps, t - 1)
                for h in range(2):
                    r = slice(64 * h, 64 * h + 64)
                    nc.scalar.activation(vst[a][r, :, :, h, :].rearrange("p j b d -> p b j d"),
                                         (b1 if a else b0)[r, :].rearrange("p (b j s d) -> p b j s d", b=2, j=8, s=2)[:, :, :, h, :],
                                         ACT.Copy).then_inc(v_sb, 1)

            def weights(t):
                for c in range(2):
                    act.wait_ge(pt_ps, 2 * t + c + 1)
                    after(act, pv_ps, t)
                    nc.scalar.activation(pt[c][:, :, :], pT[c][:, :, :], ACT.Copy).then_inc(pt_sb, 1)

            def results(t, a):
                act.wait_ge(pv_ps, t + 1)
                if first:
                    if not (isinstance(t, int) and t < 2):
                        act.wait_ge(o_out[a], 16 * (t - a))
                    for b in range(2):
                        r = slice(b * S, (b + 1) * S)
                        nc.scalar.activation(otm[a][r, :, :], pVt[r, :, b, :], ACT.Copy).then_inc(ot_ok, 1)
                    return
                after(act, o_ps, t)
                for b in range(2):
                    nc.scalar.activation(oh[:, :, b, :], pVf[:, :, b, :], ACT.Copy, scale=g.batchmask[:, b:b + 1]).then_inc(oh_ok, 1)

            def squares(t, a):
                if first:
                    return
                act.wait_ge(o_sb, t + 1)
                after(act, sq_ok, t - 1)
                nc.scalar.activation(junk[a][:, :], out[:, bass.ds(t, 1), :].rearrange("p o n -> p (o n)"), ACT.Square,
                                     accum_out=ssq[:, bass.ds(t, 1)]).then_inc(sq_ok, 1)

            def body(i):
                keys(i)
                if not opening(i):
                    results(2 * i - 2, 0)
                masked_keys(i)
                if not opening(i):
                    weights(2 * i - 1)
                values(i, 0)
                if not first and not closing(i):
                    scaled(i + 1)
                if not opening(i):
                    squares(2 * i - 2, 0)
                exps(2 * i, 0)
                if not opening(i):
                    results(2 * i - 1, 1)
                exps(2 * i, 1)
                values(i, 1)
                if not closing(i):
                    high(i + 1)
                weights(2 * i)
                exps(2 * i + 1, 0)
                exps(2 * i + 1, 1)
                if not opening(i):
                    squares(2 * i - 1, 1)
            if not first:
                scaled(0)
            high(0)
            bodies(act, body)
            results(TT - 2, 0)
            weights(TT - 1)
            results(TT - 1, 1)
            squares(TT - 2, 0)
            squares(TT - 1, 1)

        @block.vector
        def _(dve):
            v = nc.vector
            for n in range(nw):
                dve.wait_ge(wh_ok, n + 1)
                v.tensor_tensor(wl[n][:, :, :], w_raw[n], f32(wh[n][:, :, :]), ALU.subtract).then_inc(wl_ok, 1)
            if not first:
                dve.wait_ge(wh_ok, nw + 1)
                v.tensor_tensor(wol[:, :, :], wo_raw, f32(woh[:, :, :]), ALU.subtract).then_inc(wl_ok, 1)
            dve.wait_ge(vz_ok, 2)

            def combine(i):
                for a in range(2):
                    t = 2 * i + a
                    dve.wait_ge(gat_in[0][a], 16 * i + 16)
                    after(dve, yt_ok, t - 1)
                    v.tensor_scalar(ya[a][:, :], gat[0][a][:, :], g.weight[0][:, bass.ds(t, 1)], None, ALU.mult).then_inc(ya_ok, 1)
                    dve.wait_ge(ya_ok, t + 1)
                    dve.wait_ge(gat_in[1][a], 16 * i + 16)
                    after(dve, x_ps, i)
                    v.scalar_tensor_tensor(yt[a][:, :], gat[1][a][:, :], g.weight[1][:, bass.ds(t, 1)], ya[a][:, :],
                                           ALU.mult, ALU.add).then_inc(yt_ok, 1)

            def adapt(i):
                dve.wait_ge(x_ps, i + 1)
                after(dve, u2_ok, i)
                v4 = lambda ap: ap.rearrange("p k (b s) -> p k b s", b=4)
                v.tensor_tensor(v4(u1[:, :, :]), b0[:, :].rearrange("p (k b s) -> p k b s", k=KD, b=4), bc(g.ada[:, 0, :, bass.ds(4 * i, 4)], 3, S), ALU.mult).then_inc(u1_ok, 1)

            def low(i):
                src = (b0[:, :] if first else u2[:, :, :].rearrange("p k n -> p (k n)")).rearrange("p (k b s) -> p k b s", k=KD, b=4)
                dve.wait_ge(ih_ok, KD * (i + 1))
                for k in range(KD):
                    last = v.tensor_tensor(il[:, k, :, :, :], bc(src[:, k, :, :], 2, 2), f32(ih[:, k, :, :, :]), ALU.subtract)
                    last.then_inc(il_ok, 1)

            def masked_keys(i):
                dve.wait_ge(k_sb, NK * (i + 1))
                after(dve, s_ps, 4 * i)
                for h in range(KX_DVE):
                    v.tensor_scalar(kx[:, :, h, :], kT[:, :, :], g.headmask[:, h:h + 1], None, ALU.mult).then_inc(kx_dve, 1)

            def values(i, a):
                if not first:
                    return
                t = 2 * i + a
                dve.wait_ge(v_ps, t + 1)
                after(dve, pv_ps, t - 1)
                for h in range(2):
                    r = slice(64 * h, 64 * h + 64)
                    v.tensor_tensor(vst[a][r, :, :, h, :].rearrange("p j b d -> p b j d"),
                                    (b1 if a else b0)[r, :].rearrange("p (b j s d) -> p b j s d", b=2, j=8, s=2)[:, :, :, h, :],
                                    bc(g.rows[r, ROW_BV1, :].rearrange("p (j s d) -> p j s d", j=8, s=2)[:, :, h, :], 1, 2), ALU.add).then_inc(v_sb, 1)

            def softmax(t):
                for c in range(2):
                    n = 2 * t + c
                    dve.wait_ge(s_ps, n + 1)
                    after(dve, df_ok, n - 1)
                    v.tensor_reduce(mx[c][:, :], pS[c][:, :, :], AX_X, ALU.max).then_inc(mx_ok, 1)
                    dve.wait_ge(mx_ok, n + 1)
                    after(dve, ex_ok, n - 1)
                    v.tensor_tensor(df[c][:, :, :], pS[c][:, :, :], bc(mx[c][:, :], 2, S), ALU.subtract).then_inc(df_ok, 1)

            def sums(t):
                for c in range(2):
                    n = 2 * t + c
                    dve.wait_ge(ex_ok, n + 1)
                    after(dve, rc_ok, n - 1)
                    v.tensor_reduce(sm[c][:, :], ex[c][:, :, :], AX_X, ALU.add).then_inc(sm_ok, 1)
                    dve.wait_ge(sm_ok, n + 1)
                    after(dve, pn_ok, n - 1)
                    v.reciprocal(rc[c][:, :], sm[c][:, :]).then_inc(rc_ok, 1)

            def results(t):
                if first:
                    return
                dve.wait_ge(oh_ok, 2 * t + 2)
                for b in range(2):
                    v.scalar_tensor_tensor(ol[:, :, b, :], pVf[:, :, b, :], g.batchmask[:, b:b + 1], f32(oh[:, :, b, :]),
                                           ALU.mult, ALU.subtract).then_inc(ol_ok, 1)

            def output(t):
                if first:
                    return
                dve.wait_ge(o_ps, t + 1)
                r = res[:, bass.ds(t, 1), :].rearrange("p o n -> p (o n)")
                v.tensor_tensor(out[:, bass.ds(t, 1), :].rearrange("p o n -> p (o n)"), b2[:, 0:D], r, ALU.add).then_inc(o_sb, 1)

            def body(i):
                masked_keys(i)
                if not opening(i):
                    results(2 * i - 2)
                values(i, 0)
                if first and not closing(i):
                    combine(i + 1)
                if not opening(i):
                    output(2 * i - 2)
                softmax(2 * i)
                if not first and not closing(i):
                    adapt(i + 1)
                sums(2 * i)
                if not opening(i):
                    results(2 * i - 1)
                values(i, 1)
                if not closing(i):
                    low(i + 1)
                softmax(2 * i + 1)
                if not opening(i):
                    output(2 * i - 1)
                sums(2 * i + 1)
            if first:
                combine(0)
            else:
                adapt(0)
            low(0)
            bodies(dve, body)
            results(TT - 2)
            output(TT - 2)
            results(TT - 1)
            output(TT - 1)


def project_first(nc, g, dr):
    with ExitStack() as ctx:
        sb, ps, sem = scope(nc, ctx, "proj")
        wh = sb("wh", [P, KD, D], F32R)
        wl = sb("wl", [P, KD, D], F32R)
        rows = [sb(f"rows{a}", [P, 2, D]) for a in range(2)]
        oh = [sb(f"oh{a}", [P, KD, PB], F32R) for a in range(2)]
        ol = [sb(f"ol{a}", [P, KD, PB], F32R) for a in range(2)]
        xb = [sb(f"xb{a}", [P, 2, D]) for a in range(2)]
        junk = [sb(f"junk{a}", [P, D]) for a in range(2)]
        ss = sb("ss", [P, TT])
        ms = sb("ms", [P, TT])
        rv = sb("rv", [P, TT])
        condT = sb("condT", [DC, NB])
        adaw = sb("adaw", [DC, 4, D])
        adab = sb("adab", [P, 4, KD])
        pX = [ps(f"pX{a}", [P, KD, PB]) for a in range(2)]
        pO = [ps(f"pO{a}", [P, 2, D]) for a in range(2)]
        pA = ps("pA", [P, 4, KD, NB])
        wh_ok, wl_ok, x_ps, oh_ok, ol_ok, xb_ok, o_ps, o_sb, sq_ok = (
            sem(n) for n in ("wh_ok", "wl_ok", "x_ps", "oh_ok", "ol_ok", "xb_ok", "o_ps", "o_sb", "sq_ok"))
        ada_in, ada_ps, ada_sb, ms_ok, rv_ok, inv_ok = (sem(n) for n in ("ada_in", "ada_ps", "ada_sb", "ms_ok", "rv_ok", "inv_ok"))
        rows_in = [sem(f"rows_in{a}") for a in range(2)]
        block = ctx.enter_context(nc.Block())
        heads = dr.heads.rearrange("(n b) h (i l) d -> n (b h i) (l d)", b=4, l=S // 4)

        def pairs(eng, body):
            body(0, 0)
            body(1, 1)
            with eng.Fori(1, NBODY // 2) as p:
                body(2 * p, 0)
                body(2 * p + 1, 1)

        def again(i):
            return not (isinstance(i, int) and i < 2)

        def tiles(t, i):
            return t[:, bass.ds(2 * i, 2), :]

        @block.sync
        def _(sp):
            sp.dma_start(condT[:, :], dr.condT).then_inc(ada_in, 16)
            sp.dma_start(adaw[:, :, :], dr.adaw).then_inc(ada_in, 16)
            sp.dma_start(adab[:, :, :], dr.adab).then_inc(ada_in, 16)

            def body(i, a):
                if again(i):
                    sp.wait_ge(x_ps, i - 1)
                sp.dma_start(rows[a][:, :, :], heads[bass.ds(i, 1)].rearrange("o (s p) c -> p (o s) c", p=P)).then_inc(rows_in[a], 16)
            pairs(sp, body)

        @block.gpsimd
        def _(pool):
            def body(i, a):
                if again(i):
                    pool.wait_ge(o_sb, i - 1)
                nc.gpsimd.tensor_tensor(xb[a][:, :, :], tiles(g.x, i), bc(g.rows[:, ROW_BO1, :], 1, 2), ALU.add).then_inc(xb_ok, 1)
            pairs(pool, body)

        @block.tensor
        def _(pe):
            pe.wait_ge(ada_in, 48)
            for n in range(4):
                for k in range(KD):
                    last = nc.tensor.matmul(pA[:, n, k, :], adaw[:, n, k * P:(k + 1) * P], condT[:, :], start=True, stop=True)
            last.then_inc(ada_ps, 1)

            def turn(i, a):
                pe.wait_ge(rows_in[a], 8 * (i - a) + 16)
                if again(i):
                    pe.wait_ge(oh_ok, i - 1)
                    pe.wait_ge(ol_ok, i - 1)
                for s in range(2):
                    for k in range(KD):
                        last = nc.tensor.transpose(pX[a][:, k, s * P:(s + 1) * P], rows[a][:, s, k * P:(k + 1) * P], g.ident[:, :])
                last.then_inc(x_ps, 1)

            def product(i, a):
                pe.wait_ge(oh_ok, i + 1)
                pe.wait_ge(ol_ok, i + 1)
                if again(i):
                    pe.wait_ge(o_sb, i - 1)
                for s in range(2):
                    for k in range(KD):
                        last = mm3(nc, pO[a][:, s, :], oh[a][:, k, s * P:(s + 1) * P], ol[a][:, k, s * P:(s + 1) * P],
                                   wh[:, k, :], wl[:, k, :], k == 0, k == KD - 1)
                last.then_inc(o_ps, 1)
            turn(0, 0)
            pe.wait_ge(wh_ok, 1)
            pe.wait_ge(wl_ok, 1)
            turn(1, 1)
            product(0, 0)
            with pe.Fori(1, NBODY // 2) as p:
                turn(2 * p, 0)
                product(2 * p - 1, 1)
                turn(2 * p + 1, 1)
                product(2 * p, 0)
            product(NBODY - 1, 1)

        @block.scalar
        def _(act):
            nc.scalar.activation(wh[:, :, :], g.w_o1, ACT.Copy).then_inc(wh_ok, 1)

            def body(i, a):
                act.wait_ge(x_ps, i + 1)
                if again(i):
                    act.wait_ge(o_ps, i - 1)
                nc.scalar.activation(oh[a][:, :, :], pX[a][:, :, :], ACT.Copy).then_inc(oh_ok, 1)

            def squares(i):
                act.wait_ge(o_sb, i + 1)
                for s in range(2):
                    if not (isinstance(i, int) and i < 1):
                        act.wait_ge(sq_ok, 2 * i + s - 1)
                    nc.scalar.activation(junk[s][:, :], g.x1[:, bass.ds(2 * i + s, 1), :].rearrange("p o n -> p (o n)"), ACT.Square,
                                         accum_out=ss[:, bass.ds(2 * i + s, 1)]).then_inc(sq_ok, 1)
            body(0, 0)
            body(1, 1)
            squares(0)
            with act.Fori(1, NBODY // 2) as p:
                body(2 * p, 0)
                squares(2 * p - 1)
                body(2 * p + 1, 1)
                squares(2 * p)
            squares(NBODY - 1)
            act.wait_ge(rv_ok, 1)
            nc.scalar.activation(g.inv1[:, :], rv[:, :], ACT.Sqrt).then_inc(inv_ok, 1)

        @block.vector
        def _(dve):
            v = nc.vector
            dve.wait_ge(wh_ok, 1)
            v.tensor_tensor(wl[:, :, :], g.w_o1, f32(wh[:, :, :]), ALU.subtract).then_inc(wl_ok, 1)
            dve.wait_ge(ada_ps, 1)
            v.tensor_tensor(g.ada[:, :, :, :], pA[:, :, :, :], bc(adab[:, :, :], 3, NB), ALU.add).then_inc(ada_sb, 1)

            def low(i, a):
                dve.wait_ge(oh_ok, i + 1)
                v.tensor_tensor(ol[a][:, :, :], pX[a][:, :, :], f32(oh[a][:, :, :]), ALU.subtract).then_inc(ol_ok, 1)

            def result(i, a):
                dve.wait_ge(o_ps, i + 1)
                dve.wait_ge(xb_ok, i + 1)
                v.tensor_tensor(tiles(g.x1, i), pO[a][:, :, :], xb[a][:, :, :], ALU.add).then_inc(o_sb, 1)
            low(0, 0)
            low(1, 1)
            result(0, 0)
            with dve.Fori(1, NBODY // 2) as p:
                low(2 * p, 0)
                result(2 * p - 1, 1)
                low(2 * p + 1, 1)
                result(2 * p, 0)
            result(NBODY - 1, 1)
            dve.wait_ge(sq_ok, TT)
            v.tensor_scalar(ms[:, :], ss[:, :], 1.0 / D, EPS, ALU.mult, ALU.add).then_inc(ms_ok, 1)
            dve.wait_ge(ms_ok, 1)
            v.reciprocal(rv[:, :], ms[:, :]).then_inc(rv_ok, 1)


KF = FH // P
MP = KF // 2


def swiglu(nc, g, dr):
    with ExitStack() as ctx:
        sb, ps, sem = scope(nc, ctx, "ffn")
        wh = [sb(f"wh{n}", [P, KD * FH], F32R) for n in range(3)]
        wl = [sb(f"wl{n}", [P, KD * FH], F32R) for n in range(3)]
        ms = sb("ms", [P, TT])
        rv = sb("rv", [P, TT])
        inv = sb("inv", [P, TT])
        yt = [sb(f"yt{a}", [P, D]) for a in range(2)]
        u1 = sb("u1", [P, KD, 4, S])
        u2 = sb("u2", [P, KD, 4, S])
        ih = sb("ih", [P, KD, PB], F32R)
        il = sb("il", [P, KD, PB], F32R)
        sg = [sb(f"sg{r}", [P, 2, PB]) for r in range(2)]
        hf = [sb(f"hf{r}", [P, 2, PB]) for r in range(2)]
        hh = [sb(f"hh{r}", [P, 2, PB], F32R) for r in range(2)]
        hl = [sb(f"hl{r}", [P, 2, PB], F32R) for r in range(2)]
        pX = ps("pX", [P, KD, PB])
        pG = [ps(f"pG{r}", [P, 2, PB]) for r in range(2)]
        pH = [ps(f"pH{r}", [P, 2, PB]) for r in range(2)]
        pO = ps("pO", [P, 2, D])
        wh_ok, wl_ok, ms_ok, rv_ok, inv_ok, yt_ok, x_ps, u1_ok, u2_ok, ih_ok, il_ok = (
            sem(n) for n in ("wh_ok", "wl_ok", "ms_ok", "rv_ok", "inv_ok", "yt_ok", "x_ps", "u1_ok", "u2_ok", "ih_ok", "il_ok"))
        g_ps, h_ps, sg_ok, hf_ok, hh_ok, hl_ok, op_ps, o_sb = (
            sem(n) for n in ("g_ps", "h_ps", "sg_ok", "hf_ok", "hh_ok", "hl_ok", "op_ps", "o_sb"))
        block = ctx.enter_context(nc.Block())

        def after(eng, semaphore, value):
            if not (isinstance(value, int) and value <= 0):
                eng.wait_ge(semaphore, value)

        @block.tensor
        def _(pe):
            w_h = [wh[n][:, :].rearrange("p (k m) -> p k m", k=KF if n == 2 else KD) for n in range(3)]
            w_l = [wl[n][:, :].rearrange("p (k m) -> p k m", k=KF if n == 2 else KD) for n in range(3)]

            def turn(i):
                pe.wait_ge(yt_ok, 2 * i + 2)
                after(pe, u1_ok, i)
                for a in range(2):
                    for k in range(KD):
                        last = nc.tensor.transpose(pX[:, k, a * P:(a + 1) * P], yt[a][:, k * P:(k + 1) * P], g.ident[:, :])
                last.then_inc(x_ps, 1)

            def pair(i, j):
                n = MP * i + j
                if j == 0:
                    pe.wait_ge(ih_ok, i + 1)
                    pe.wait_ge(il_ok, i + 1)
                for w, bank, left, done in ((0, pG, sg_ok, g_ps), (1, pH, hf_ok, h_ps)):
                    if isinstance(i, int) and i == 0 and j < 2:
                        pe.wait_ge(wh_ok, w + 1)
                        pe.wait_ge(wl_ok, w + 1)
                    else:
                        pe.wait_ge(left, n - 1)
                    for m in range(2):
                        for k in range(KD):
                            c = slice((2 * j + m) * P, (2 * j + m + 1) * P)
                            last = mm3(nc, bank[j % 2][:, m, :], w_h[w][:, k, c], w_l[w][:, k, c], ih[:, k, :], il[:, k, :],
                                       k == 0, k == KD - 1)
                    last.then_inc(done, 1)

            def output(i, j):
                n = MP * i + j
                if isinstance(i, int) and i == 0 and j == 0:
                    pe.wait_ge(wh_ok, 3)
                    pe.wait_ge(wl_ok, 3)
                pe.wait_ge(hh_ok, n + 1)
                pe.wait_ge(hl_ok, n + 1)
                if j == 0:
                    after(pe, o_sb, i)
                for s in range(2):
                    for m in range(2):
                        c = slice(s * P, (s + 1) * P)
                        first = j == 0 and s == 0 and m == 0
                        nc.tensor.matmul(pO[:, s, :], hh[j % 2][:, m, c], w_h[2][:, 2 * j + m, :], start=first, stop=False, skip_group_check=True)
                        nc.tensor.matmul(pO[:, s, :], hl[j % 2][:, m, c], w_h[2][:, 2 * j + m, :], start=False, stop=False, skip_group_check=True)
                        last = nc.tensor.matmul(pO[:, s, :], hh[j % 2][:, m, c], w_l[2][:, 2 * j + m, :], start=False,
                                                stop=j == MP - 1 and m == 1, skip_group_check=True)
                last.then_inc(op_ps, 1)

            def body(i, last=False):
                pair(i, 0)
                if not (isinstance(i, int) and i == 0):
                    output(i - 1, MP - 1)
                pair(i, 1)
                output(i, 0)
                if not last:
                    turn(i + 1)
                pair(i, 2)
                output(i, 1)
                pair(i, 3)
                output(i, 2)
            turn(0)
            body(0)
            with pe.Fori(1, NBODY - 1) as i:
                body(i)
            body(NBODY - 1, last=True)
            output(NBODY - 1, MP - 1)

        @block.scalar
        def _(act):
            def scaled(i):
                for a in range(2):
                    after(act, x_ps, i)
                    nc.scalar.activation(yt[a][:, :], g.x[:, bass.ds(2 * i + a, 1), :].rearrange("p o n -> p (o n)"), ACT.Copy,
                                         scale=inv[:, bass.ds(2 * i + a, 1)]).then_inc(yt_ok, 1)

            def high(i):
                act.wait_ge(u2_ok, i + 1)
                after(act, h_ps, MP * i)
                nc.scalar.activation(ih[:, :, :], u2[:, :, :, :].rearrange("p k b s -> p k (b s)"), ACT.Copy).then_inc(ih_ok, 1)

            def silu(i, j):
                n = MP * i + j
                act.wait_ge(g_ps, n + 1)
                if not (isinstance(i, int) and i == 0 and j < 2):
                    act.wait_ge(hf_ok, n - 1)
                nc.scalar.activation(sg[j % 2][:, :, :], pG[j % 2][:, :, :], ACT.Silu).then_inc(sg_ok, 1)

            def hidden_high(i, j):
                n = MP * i + j
                act.wait_ge(hf_ok, n + 1)
                if not (isinstance(i, int) and i == 0 and j < 2):
                    act.wait_ge(op_ps, n - 1)
                nc.scalar.activation(hh[j % 2][:, :, :], hf[j % 2][:, :, :], ACT.Copy).then_inc(hh_ok, 1)

            def body(i, last=False):
                for j in range(MP):
                    silu(i, j)
                    hidden_high(i, j)
                    if not last and j == 0:
                        scaled(i + 1)
                    if not last and j == 2:
                        high(i + 1)
            act.wait_ge(rv_ok, 1)
            nc.scalar.activation(inv[:, :], rv[:, :], ACT.Sqrt).then_inc(inv_ok, 1)
            act.wait_ge(inv_ok, 1)
            scaled(0)
            for n in range(3):
                nc.scalar.activation(wh[n][:, :], g.w_ff[:, n, :], ACT.Copy).then_inc(wh_ok, 1)
                if n == 0:
                    high(0)
            body(0)
            with act.Fori(1, NBODY - 1) as i:
                body(i)
            body(NBODY - 1, last=True)

        @block.vector
        def _(dve):
            v = nc.vector

            def adapt(i):
                dve.wait_ge(x_ps, i + 1)
                after(dve, u2_ok, i)
                v.tensor_tensor(u1[:, :, :, :], pX[:, :, :].rearrange("p k (b s) -> p k b s", b=4),
                                bc(g.ada[:, 2, :, bass.ds(4 * i, 4)], 3, S), ALU.mult).then_inc(u1_ok, 1)
                dve.wait_ge(u1_ok, i + 1)
                after(dve, ih_ok, i)
                after(dve, il_ok, i)
                v.tensor_tensor(u2[:, :, :, :], u1[:, :, :, :], bc(g.ada[:, 3, :, bass.ds(4 * i, 4)], 3, S), ALU.add).then_inc(u2_ok, 1)

            def low(i):
                dve.wait_ge(ih_ok, i + 1)
                v.tensor_tensor(il[:, :, :], u2[:, :, :, :].rearrange("p k b s -> p k (b s)"), f32(ih[:, :, :]), ALU.subtract).then_inc(il_ok, 1)

            def gated(i, j):
                n = MP * i + j
                dve.wait_ge(sg_ok, n + 1)
                dve.wait_ge(h_ps, n + 1)
                if not (isinstance(i, int) and i == 0 and j < 2):
                    dve.wait_ge(hl_ok, n - 1)
                v.tensor_tensor(hf[j % 2][:, :, :], pH[j % 2][:, :, :], sg[j % 2][:, :, :], ALU.mult).then_inc(hf_ok, 1)
                dve.wait_ge(hh_ok, n + 1)
                v.tensor_tensor(hl[j % 2][:, :, :], hf[j % 2][:, :, :], f32(hh[j % 2][:, :, :]), ALU.subtract).then_inc(hl_ok, 1)

            def result(i):
                dve.wait_ge(op_ps, MP * i + MP)
                x2 = g.x[:, bass.ds(2 * i, 2), :]
                v.tensor_tensor(x2, pO[:, :, :], x2, ALU.add).then_inc(o_sb, 1)

            def body(i, last=False):
                gated(i, 0)
                if not (isinstance(i, int) and i == 0):
                    result(i - 1)
                gated(i, 1)
                gated(i, 2)
                if not last:
                    adapt(i + 1)
                gated(i, 3)
                if not last:
                    low(i + 1)
            v.tensor_scalar(ms[:, :], g.ss2[:, :], 1.0 / D, EPS, ALU.mult, ALU.add).then_inc(ms_ok, 1)
            dve.wait_ge(ms_ok, 1)
            v.reciprocal(rv[:, :], ms[:, :]).then_inc(rv_ok, 1)
            adapt(0)
            for n in range(3):
                dve.wait_ge(wh_ok, n + 1)
                v.tensor_tensor(wl[n][:, :], g.w_ff[:, n, :], f32(wh[n][:, :]), ALU.subtract).then_inc(wl_ok, 1)
                if n == 0:
                    low(0)
            body(0)
            with dve.Fori(1, NBODY - 1) as i:
                body(i)
            body(NBODY - 1, last=True)
            result(NBODY - 1)


NRING = 4
HS = HC * NS


def load_expert(eng, g, dr, e, r):
    eng.dma_start(g.ring[r][:, :], dr.w_slot[bass.ds(e, 1)].rearrange("o p n -> p (o n)")).then_inc(g.ring_in[r], 16)


def slots(nc, g, dr):
    with ExitStack() as ctx:
        sb, ps, sem = scope(nc, ctx, "slots")
        raw = [g.w_small[:, w] for w in (W_DK, W_CQ, W_DV)]
        wh = [sb(f"wh{n}", [P, KD, D], F32R) for n in range(3)]
        wl = [sb(f"wl{n}", [P, KD, D], F32R) for n in range(3)]
        slotT = sb("slotT", [P, KD, NS])
        sq = sb("sq", [P, KD, NS])
        sx = sb("sx", [P, KD, HC, NS])
        xt = sb("xt", [P, 2, D])
        xh = sb("xh", [P, KD, PB], F32R)
        xl = sb("xl", [P, KD, PB], F32R)
        kT = sb("kT", [P, KD, PB])
        qT = sb("qT", [P, KD, PB])
        vt = sb("vt", [P, 2, D])
        mx = sb("mx", [P, KD, 4])
        df = sb("df", [P, KD, 4, S])
        ex = sb("ex", [P, KD, 4, S])
        sm = sb("sm", [P, KD, 4])
        rc = sb("rc", [P, KD, 4])
        pn = sb("pn", [P, KD, 4, S])
        pt = sb("pt", [P, KD, 2, HS])
        own = [sb(f"own{b}", [P, 4, NS, HC]) for b in range(2)]
        pX = ps("pX", [P, KD, PB])
        pK = ps("pK", [P, KD, PB])
        pQ = ps("pQ", [P, KD, PB])
        pVt = ps("pVt", [P, 2, D])
        pS = ps("pS", [P, KD, 4, S])
        pT = ps("pT", [P, KD, 2, HS])
        pU = [ps(f"pU{b}", [P, 2, KD, HC, NS]) for b in range(2)]
        wh_ok, wl_ok, sl_in, sq_ps, sq_ok, sx_ok = (sem(n) for n in ("wh_ok", "wl_ok", "sl_in", "sq_ps", "sq_ok", "sx_ok"))
        x_in, x_ps, xh_ok, xl_ok, k_ps, k_sb, q_ps, q_sb, q_out, v_ps, v_sb = (
            sem(n) for n in ("x_in", "x_ps", "xh_ok", "xl_ok", "k_ps", "k_sb", "q_ps", "q_sb", "q_out", "v_ps", "v_sb"))
        s_ps, mx_ok, df_ok, ex_ok, sm_ok, rc_ok, pn_ok, pt_ps, pt_sb, u_ps, own_ok, ot_ok = (
            sem(n) for n in ("s_ps", "mx_ok", "df_ok", "ex_ok", "sm_ok", "rc_ok", "pn_ok", "pt_ps", "pt_sb", "u_ps", "own_ok", "ot_ok"))
        block = ctx.enter_context(nc.Block())

        def after(eng, semaphore, value):
            if not (isinstance(value, int) and value <= 0):
                eng.wait_ge(semaphore, value)

        def first_body(i):
            return isinstance(i, int) and i == 0

        def bodies(eng, body):
            body(0)
            body(1)
            with eng.Fori(2, NBODY - 1) as i:
                body(i)
            body(NBODY - 1)

        @block.sync
        def _(sp):
            def load(i):
                after(sp, x_ps, i)
                sp.dma_start(xt[:, :, :], g.x[:, bass.ds(2 * i, 2), :]).then_inc(x_in, 16)

            def store(i):
                sp.wait_ge(q_sb, KD * (i + 1))
                sp.dma_start(dr.q[bass.ds(i, 1)].rearrange("o p k n -> p (o k) n"), qT[:, :, :]).then_inc(q_out, 16)
            load(0)
            sp.dma_start(slotT[:, :, :], dr.slotT).then_inc(sl_in, 16)
            for source, target in ((dr.slot_tm, g.slot_tm[:, :]), (dr.ln, g.ln[:, :, :]), (dr.eb, g.eb[:, :, :]),
                                   (dr.b2, g.b2[:, :, :]), (dr.stack, g.stack[:, :])):
                sp.dma_start(target, source).then_inc(g.ffn_in, 16)
            for i in range(NRING):
                load(i + 1)
                load_expert(sp, g, dr, i, i)
                store(i)
            with sp.Fori(NRING, NBODY - 1) as i:
                load(i + 1)
                store(i)
            store(NBODY - 1)
            sp.wait_ge(q_out, 16 * NBODY)
            sp.wait_ge(g.ffn_in, 16 * 5)

        @block.tensor
        def _(pe):
            pe.wait_ge(sl_in, 16)
            for m in range(KD):
                for k in range(KD):
                    last = nc.tensor.matmul(pS[:, m, 0, 0:NS], g.w_small[:, W_DQ, k, m * P:(m + 1) * P], slotT[:, k, :], start=k == 0, stop=k == KD - 1)
            last.then_inc(sq_ps, 1)

            def turn(i):
                pe.wait_ge(x_in, 16 * (i + 1))
                for a in range(2):
                    for k in range(KD):
                        last = nc.tensor.transpose(pX[:, k, a * P:(a + 1) * P], xt[:, a, k * P:(k + 1) * P], g.ident[:, :])
                last.then_inc(x_ps, 1)

            def feature_major(bank, n):
                for m in range(KD):
                    c = slice(m * P, (m + 1) * P)
                    for k in range(KD):
                        last = mm3(nc, bank[:, m, :], wh[n][:, k, c], wl[n][:, k, c], xh[:, k, :], xl[:, k, :], k == 0, k == KD - 1)
                return last

            def body(i):
                pe.wait_ge(xh_ok, i + 1)
                pe.wait_ge(xl_ok, i + 1)
                after(pe, k_sb, KD * i)
                feature_major(pK, 0).then_inc(k_ps, 1)
                after(pe, q_sb, KD * i)
                feature_major(pQ, 1).then_inc(q_ps, 1)
                if not first_body(i):
                    end_turn(i - 1)
                after(pe, v_sb, i)
                for a in range(2):
                    c = slice(a * P, (a + 1) * P)
                    for k in range(KD):
                        last = mm3(nc, pVt[:, a, :], xh[:, k, c], xl[:, k, c], wh[2][:, k, :], wl[2][:, k, :], k == 0, k == KD - 1)
                last.then_inc(v_ps, 1)
                pe.wait_ge(k_sb, KD * (i + 1))
                after(pe, df_ok, i)
                for c in range(KD):
                    last = nc.tensor.matmul(pS[:, c, :, :].rearrange("p b k -> p (b k)"), sx[:, c, :, :].rearrange("p h s -> p (h s)"), kT[:, c, :], start=True, stop=True)
                last.then_inc(s_ps, 1)

            def end_turn(i):
                pe.wait_ge(pn_ok, i + 1)
                for c in range(KD):
                    for a in range(2):
                        last = nc.tensor.transpose(pT[:, c, a, :], pn[:, c, 2 * a:2 * a + 2, :].rearrange("p b k -> p (b k)"), g.ident[:, :])
                last.then_inc(pt_ps, 1)

            def end(i):
                pe.wait_ge(pt_sb, i + 1)
                after(pe, own_ok, 2 * i)
                for a in range(2):
                    for c in range(KD):
                        for b in range(2):
                            r = slice(b * S, (b + 1) * S)
                            last = nc.tensor.matmul(pU[b][:, a, c, :, :].rearrange("p h s -> p (h s)"), vt[r, a, c * P:(c + 1) * P], pt[r, c, a, :], start=True, stop=True)
                last.then_inc(u_ps, 1)
            turn(0)
            pe.wait_ge(wh_ok, 3)
            pe.wait_ge(wl_ok, 3)
            pe.wait_ge(sx_ok, 1)
            body(0)
            turn(1)
            body(1)
            end(0)
            turn(2)
            with pe.Fori(2, NBODY - 1) as i:
                body(i)
                end(i - 1)
                turn(i + 1)
            body(NBODY - 1)
            end(NBODY - 2)
            end_turn(NBODY - 1)
            pe.wait_ge(v_sb, NBODY)
            end(NBODY - 1)

        @block.scalar
        def _(act):
            for n in range(3):
                nc.scalar.activation(wh[n][:, :, :], raw[n], ACT.Copy).then_inc(wh_ok, 1)
            act.wait_ge(sq_ps, 1)
            for m in range(KD):
                nc.scalar.activation(sq[:, m, :], pS[:, m, 0, 0:NS], ACT.Identity, bias=g.cols[:, COL_DBQ, m:m + 1]).then_inc(sq_ok, 1)

            def high(i):
                act.wait_ge(x_ps, i + 1)
                after(act, v_ps, i)
                nc.scalar.activation(xh[:, :, :], pX[:, :, :], ACT.Copy).then_inc(xh_ok, 1)

            def values(i):
                act.wait_ge(v_ps, i + 1)
                after(act, u_ps, i)
                nc.scalar.activation(vt[:, :, :], pVt[:, :, :], ACT.Copy).then_inc(v_sb, 1)

            def weights(i):
                act.wait_ge(pt_ps, i + 1)
                after(act, u_ps, i)
                nc.scalar.activation(pt[:, :, :, :], pT[:, :, :, :], ACT.Copy).then_inc(pt_sb, 1)

            def body(i):
                act.wait_ge(k_ps, i + 1)
                after(act, s_ps, i)
                for m in range(KD):
                    nc.scalar.activation(kT[:, m, :], pK[:, m, :], ACT.Identity, bias=g.cols[:, COL_DBK, m:m + 1]).then_inc(k_sb, 1)
                act.wait_ge(q_ps, i + 1)
                after(act, q_out, 16 * i)
                for m in range(KD):
                    nc.scalar.activation(qT[:, m, :], pQ[:, m, :], ACT.Identity, bias=g.cols[:, COL_CBQ, m:m + 1]).then_inc(q_sb, 1)
                if not first_body(i):
                    weights(i - 1)
                act.wait_ge(df_ok, i + 1)
                after(act, pn_ok, i)
                nc.scalar.activation(ex[:, :, :, :], df[:, :, :, :], ACT.Exp, scale=SCALE).then_inc(ex_ok, 1)
                if not (isinstance(i, int) and i == NBODY - 1):
                    high(i + 1)
                values(i)
            high(0)
            bodies(act, body)
            weights(NBODY - 1)

        @block.vector
        def _(dve):
            v = nc.vector
            for n in range(3):
                dve.wait_ge(wh_ok, n + 1)
                v.tensor_tensor(wl[n][:, :, :], raw[n], f32(wh[n][:, :, :]), ALU.subtract).then_inc(wl_ok, 1)
            dve.wait_ge(sq_ok, KD)
            v.tensor_tensor(sx[:, :, :, :], bc(sq[:, :, :], 2, HC), bc(bc(g.headmask[:, :], 1, KD), 3, NS), ALU.mult).then_inc(sx_ok, 1)

            def low(i):
                dve.wait_ge(xh_ok, i + 1)
                v.tensor_tensor(xl[:, :, :], pX[:, :, :], f32(xh[:, :, :]), ALU.subtract).then_inc(xl_ok, 1)

            def own_head(i):
                dve.wait_ge(u_ps, i + 1)
                for b in range(2):
                    after(dve, ot_ok, 2 * i + b - 1)
                    v.tensor_tensor(own[b][:, :, :, :], pU[b][:, :, :, :, :].rearrange("p a c h s -> p (a c) s h"),
                                    bc(bc(g.headmask[:, :], 1, NS), 1, 4), ALU.mult).then_inc(own_ok, 1)
                for b in range(2):
                    dve.wait_ge(own_ok, 2 * i + b + 1)
                    v.tensor_reduce(g.oT[:, :, bass.ds(2 * i, 2), b, :].rearrange("p k a s -> p a k s"),
                                    own[b][:, :, :, :].rearrange("p (a c) s h -> p a c s h", a=2), AX_X, ALU.add).then_inc(ot_ok, 1)

            def body(i):
                dve.wait_ge(s_ps, i + 1)
                after(dve, df_ok, i)
                v.tensor_reduce(mx[:, :, :], pS[:, :, :, :], AX_X, ALU.max).then_inc(mx_ok, 1)
                dve.wait_ge(mx_ok, i + 1)
                after(dve, ex_ok, i)
                v.tensor_tensor(df[:, :, :, :], pS[:, :, :, :], bc(mx[:, :, :], 3, S), ALU.subtract).then_inc(df_ok, 1)
                if not (isinstance(i, int) and i == NBODY - 1):
                    low(i + 1)
                dve.wait_ge(ex_ok, i + 1)
                after(dve, rc_ok, i)
                v.tensor_reduce(sm[:, :, :], ex[:, :, :, :], AX_X, ALU.add).then_inc(sm_ok, 1)
                dve.wait_ge(sm_ok, i + 1)
                after(dve, pn_ok, i)
                v.reciprocal(rc[:, :, :], sm[:, :, :]).then_inc(rc_ok, 1)
                dve.wait_ge(rc_ok, i + 1)
                after(dve, pt_ps, i)
                v.tensor_tensor(pn[:, :, :, :], ex[:, :, :, :], bc(rc[:, :, :], 3, S), ALU.mult).then_inc(pn_ok, 1)
                if not first_body(i):
                    own_head(i - 1)
            low(0)
            bodies(dve, body)
            own_head(NBODY - 1)


NG = NB // HC


def slot_norm(nc, g, dr):
    with ExitStack() as ctx:
        sb, ps, sem = scope(nc, ctx, "norm")
        ob = sb("ob", [P, KD, NB * NS])
        base = sb("base", [P, D])
        o = sb("o", [P, NG, D])
        su = sb("su", [P, NG])
        mean = sb("mean", [P, NG])
        xc = sb("xc", [P, NG, D])
        x2 = sb("x2", [P, NG, D])
        ss = sb("ss", [P, NG])
        ms = sb("ms", [P, NG])
        rv = sb("rv", [P, NG])
        inv = sb("inv", [P, NG])
        h1 = sb("h1", [P, NG, D])
        h2 = sb("h2", [P, NG, D])
        h3 = sb("h3", [P, NG, D])
        pO = [ps(f"pO{n}", [P, 2, D]) for n in range(NG // 2)]
        pR = [ps(f"pR{c}", [P, NG, P]) for c in range(KD)]
        pH = [ps(f"pH{c}", [P, NG, P]) for c in range(KD)]
        names = ("ob_ok", "base_ok", "o_ps", "o_ok", "su_ok", "mean_ok", "xc_ok", "x2_ok", "ss_ok", "ms_ok", "rv_ok", "inv_ok",
                 "h1_ok", "h2_ok", "h3_ok", "r_ps", "h_ps", "r_sb", "h_sb")
        (ob_ok, base_ok, o_ps, o_ok, su_ok, mean_ok, xc_ok, x2_ok, ss_ok, ms_ok, rv_ok, inv_ok,
         h1_ok, h2_ok, h3_ok, r_ps, h_ps, r_sb, h_sb) = (sem(n) for n in names)
        block = ctx.enter_context(nc.Block())

        def by_slot(ap):
            return ap.rearrange("p g (b e) -> p e g b", e=NS)

        @block.tensor
        def _(pe):
            pe.wait_ge(ob_ok, KD)
            for n in range(NG):
                for k in range(KD):
                    last = nc.tensor.matmul(pO[n // 2][:, n % 2, :], ob[:, k, n * P:(n + 1) * P], g.w_small[:, W_DO, k, :], start=k == 0, stop=k == KD - 1)
                if n % 2:
                    last.then_inc(o_ps, 1)
            pe.wait_ge(o_ok, NG // 2)
            for c in range(KD):
                for n in range(NG):
                    last = nc.tensor.transpose(pR[c][:, n, :], o[:, n, c * P:(c + 1) * P], g.ident[:, :])
            last.then_inc(r_ps, 1)
            pe.wait_ge(h3_ok, 1)
            for c in range(KD):
                for n in range(NG):
                    last = nc.tensor.transpose(pH[c][:, n, :], h3[:, n, c * P:(c + 1) * P], g.ident[:, :])
                last.then_inc(h_ps, 1)

        @block.scalar
        def _(act):
            for k in range(KD):
                nc.scalar.activation(ob[:, k, :], g.oT[:, k, :, :, :].rearrange("p a b s -> p (a b s)"), ACT.Identity, bias=g.cols[:, COL_DBV, k:k + 1]).then_inc(ob_ok, 1)
            act.wait_ge(su_ok, 1)
            nc.scalar.activation(mean[:, :], su[:, :], ACT.Copy, scale=1.0 / D).then_inc(mean_ok, 1)
            act.wait_ge(r_ps, 1)
            for c in range(KD):
                nc.scalar.activation(g.resT[:, c, :, :].rearrange("p e (g b) -> p e g b", g=NG), by_slot(pR[c][:, :, :]), ACT.Copy).then_inc(r_sb, 1)
            act.wait_ge(rv_ok, 1)
            nc.scalar.activation(inv[:, :], rv[:, :], ACT.Sqrt).then_inc(inv_ok, 1)
            act.wait_ge(h_ps, 1)
            nc.scalar.activation(g.hT[:, 0, :, :].rearrange("p e (g b) -> p e g b", g=NG), by_slot(pH[0][:, :, :]), ACT.Copy).then_inc(h_sb, 1)

        @block.vector
        def _(dve):
            v = nc.vector
            v.tensor_tensor(base[:, :], g.slot_tm[:, :], g.rows[:, ROW_DBO, :], ALU.add).then_inc(base_ok, 1)
            dve.wait_ge(base_ok, 1)
            for n in range(NG // 2):
                dve.wait_ge(o_ps, n + 1)
                v.tensor_tensor(o[:, 2 * n:2 * n + 2, :], pO[n][:, :, :], bc(base[:, :], 1, 2), ALU.add).then_inc(o_ok, 1)
            dve.wait_ge(o_ok, NG // 2)
            v.tensor_reduce(su[:, :], o[:, :, :], AX_X, ALU.add).then_inc(su_ok, 1)
            dve.wait_ge(mean_ok, 1)
            v.tensor_tensor(xc[:, :, :], o[:, :, :], bc(mean[:, :], 2, D), ALU.subtract).then_inc(xc_ok, 1)
            dve.wait_ge(xc_ok, 1)
            v.tensor_tensor(x2[:, :, :], xc[:, :, :], xc[:, :, :], ALU.mult).then_inc(x2_ok, 1)
            dve.wait_ge(x2_ok, 1)
            v.tensor_reduce(ss[:, :], x2[:, :, :], AX_X, ALU.add).then_inc(ss_ok, 1)
            dve.wait_ge(ss_ok, 1)
            v.tensor_scalar(ms[:, :], ss[:, :], 1.0 / D, LN_EPS, ALU.mult, ALU.add).then_inc(ms_ok, 1)
            dve.wait_ge(ms_ok, 1)
            v.reciprocal(rv[:, :], ms[:, :]).then_inc(rv_ok, 1)
            v.tensor_tensor(h1[:, :, :], xc[:, :, :], bc(g.ln[:, 0, :], 1, NG), ALU.mult).then_inc(h1_ok, 1)
            dve.wait_ge(inv_ok, 1)
            dve.wait_ge(h1_ok, 1)
            v.tensor_tensor(h2[:, :, :], h1[:, :, :], bc(inv[:, :], 2, D), ALU.mult).then_inc(h2_ok, 1)
            dve.wait_ge(h2_ok, 1)
            v.tensor_tensor(h3[:, :, :], h2[:, :, :], bc(g.ln[:, 1, :], 1, NG), ALU.add).then_inc(h3_ok, 1)
            dve.wait_ge(r_sb, KD)
            v.tensor_tensor(g.baseT[:, :, :, :], g.resT[:, :, :, :], bc(g.b2[:, :, :], 3, NB), ALU.add).then_inc(h_sb, 1)
            dve.wait_ge(h_ps, 2)
            v.tensor_copy(g.hT[:, 1, :, :].rearrange("p e (g b) -> p e g b", g=NG), by_slot(pH[1][:, :, :])).then_inc(h_sb, 1)


NJ = FH // P
W2_AT = 2 * KD * FH


def slot_experts(nc, g, dr):
    with ExitStack() as ctx:
        sb, ps, sem = scope(nc, ctx, "sexp")
        hs = [sb(f"hs{a}", [P, KD, NB]) for a in range(2)]
        uc = [sb(f"uc{a}", [P, 512]) for a in range(2)]
        ub = [sb(f"ub{a}", [P, 4, 4, NB]) for a in range(2)]
        us = [sb(f"us{a}", [P, 4, 4, NB]) for a in range(2)]
        uf = [sb(f"uf{a}", [P, 4, 2, NB]) for a in range(2)]
        yc = [sb(f"yc{a}", [P, D]) for a in range(2)]
        pA = [ps(f"pA{a}", [P, 512]) for a in range(2)]
        pT = [ps(f"pT{a}", [P, 4, 4, NB]) for a in range(2)]
        pY = [ps(f"pY{a}", [P, 512]) for a in range(2)]
        pR = [ps(f"pR{a}", [P, 512]) for a in range(2)]
        hs_ok, a_ps, uc_ok, t_ps, ub_ok, us_ok, uf_ok, y_ps, yc_ok, r_ps, o_ok = (
            sem(n) for n in ("hs_ok", "a_ps", "uc_ok", "t_ps", "ub_ok", "us_ok", "uf_ok", "y_ps", "yc_ok", "r_ps", "o_ok"))
        block = ctx.enter_context(nc.Block())

        def after(eng, semaphore, value):
            if not (isinstance(value, int) and value <= 0):
                eng.wait_ge(semaphore, value)

        def experts_of(eng, step):
            for r in range(NRING):
                step(r, r)
            with eng.Fori(1, NS // NRING) as n:
                for r in range(NRING):
                    step(NRING * n + r, r)

        @block.sync
        def _(sp):
            def step(e, r):
                sp.wait_ge(y_ps, e + 1)
                load_expert(sp, g, dr, e + NRING, r)
            with sp.Fori(0, NS // NRING - 1) as n:
                for r in range(NRING):
                    step(NRING * n + r, r)

        @block.tensor
        def _(pe):
            def up(e, r):
                a = r % 2
                w = g.ring[r]
                if isinstance(e, int):
                    pe.wait_ge(g.ring_in[r], 16)
                else:
                    pe.wait_ge(g.ring_in[r], (e - r) * (16 // NRING) + 16)
                pe.wait_ge(hs_ok, e + 1)
                after(pe, uc_ok, e - 1)
                for k in range(KD):
                    for n in range(4):
                        at = ((n // 2) * KD + k) * FH + (n % 2) * 512
                        last = nc.tensor.matmul(pA[a][32 * n:32 * n + 32, :], hs[a][:, k, :], w[:, at:at + 512], start=k == 0, stop=k == KD - 1,
                                                tile_position=(0, 32 * n))
                last.then_inc(a_ps, 1)

            def turn(e, r):
                a = r % 2
                pe.wait_ge(uc_ok, e + 1)
                after(pe, ub_ok, e - 1)
                for j in range(4):
                    last = nc.tensor.transpose(pT[a][:, j, :, :].rearrange("p n b -> p (n b)"), uc[a][:, j * P:(j + 1) * P], g.ident[:, :])
                last.then_inc(t_ps, 1)

            def down(e, r):
                a = r % 2
                w = g.ring[r]
                pe.wait_ge(uf_ok, e + 1)
                after(pe, yc_ok, e - 1)
                for h in range(2):
                    for j in range(4):
                        at = W2_AT + (4 * h + j) * D
                        last = nc.tensor.matmul(pY[a][32 * j:32 * j + 32, 0:D], uf[a][:, j, h, :], w[:, at:at + D], start=h == 0, stop=h == 1,
                                                tile_position=(0, 32 * j))
                last.then_inc(y_ps, 1)

            def total(e, r):
                a = r % 2
                pe.wait_ge(yc_ok, e + 1)
                after(pe, o_ok, e - 1)
                for k in range(KD):
                    last = nc.tensor.matmul(pR[a][:, k * NB:(k + 1) * NB], yc[a][:, k * P:(k + 1) * P], g.stack[:, :], start=True, stop=True)
                last.then_inc(r_ps, 1)

            def step(e, r):
                up(e, r)
                if not (isinstance(e, int) and e == 0):
                    down(e - 1, (r - 1) % NRING)
                turn(e, r)
                if not (isinstance(e, int) and e == 0):
                    total(e - 1, (r - 1) % NRING)
            experts_of(pe, step)
            down(NS - 1, NRING - 1)
            total(NS - 1, NRING - 1)

        @block.scalar
        def _(act):
            def sums(e, r):
                act.wait_ge(y_ps, e + 1)
                after(act, r_ps, e - 1)
                nc.scalar.activation(yc[r % 2][:, :], pY[r % 2][:, 0:D], ACT.Copy).then_inc(yc_ok, 1)

            def step(e, r):
                a = r % 2
                act.wait_ge(a_ps, e + 1)
                after(act, t_ps, e - 1)
                nc.scalar.activation(uc[a][:, :], pA[a][:, :], ACT.Copy).then_inc(uc_ok, 1)
                if not (isinstance(e, int) and e == 0):
                    sums(e - 1, r - 1)
                act.wait_ge(ub_ok, e + 1)
                after(act, uf_ok, e - 1)
                nc.scalar.activation(us[a][:, :, :, :], ub[a][:, :, :, :], ACT.Silu).then_inc(us_ok, 1)
            experts_of(act, step)
            sums(NS - 1, NRING - 1)

        @block.vector
        def _(dve):
            v = nc.vector

            def stationary(e, r):
                after(dve, a_ps, e - 1)
                v.tensor_copy(hs[r % 2][:, :, :], g.hT[:, :, bass.ds(e, 1), :].rearrange("p k o b -> p k (o b)")).then_inc(hs_ok, 1)

            def result(e, r):
                dve.wait_ge(r_ps, e + 1)
                v.tensor_tensor(g.o2T[:, :, bass.ds(e, 1), :].rearrange("p k o b -> p k (o b)"),
                                pR[r % 2][:, 0:KD * NB].rearrange("p (k b) -> p k b", k=KD),
                                g.baseT[:, :, bass.ds(e, 1), :].rearrange("p k o b -> p k (o b)"), ALU.add).then_inc(o_ok, 1)

            def step(e, r):
                a = r % 2
                stationary(e, r)
                dve.wait_ge(t_ps, e + 1)
                after(dve, us_ok, e - 1)
                v.tensor_tensor(ub[a][:, :, :, :], pT[a][:, :, :, :],
                                bc(g.eb[:, bass.ds(e, 1), :].rearrange("p o (j n) -> p (o j) n", j=4), 3, NB), ALU.add).then_inc(ub_ok, 1)
                if not (isinstance(e, int) and e == 0):
                    result(e - 1, r - 1)
                dve.wait_ge(us_ok, e + 1)
                after(dve, y_ps, e - 1)
                v.tensor_tensor(uf[a][:, :, :, :], us[a][:, :, 0:2, :], us[a][:, :, 2:4, :], ALU.mult).then_inc(uf_ok, 1)
            experts_of(dve, step)
            result(NS - 1, NRING - 1)


def tokens(nc, g, dr):
    with ExitStack() as ctx:
        sb, ps, sem = scope(nc, ctx, "tok")
        k2 = sb("k2", [P, KD, NB, NS])
        v2 = sb("v2", [P, KD, NB, NS])
        qt = [sb(f"qt{a}", [P, KD, PB]) for a in range(2)]
        kx = sb("kx", [P, KD, 4, HC, NS])
        vx = sb("vx", [P, KD, 4, HC, NS])
        vo = sb("vo", [P, 4, KD, D])
        mx = sb("mx", [P, 2, KD, HC])
        df = sb("df", [P, 2, KD, HC, NS])
        ex = sb("ex", [P, 2, KD, HC, NS])
        sm = sb("sm", [P, 2, KD, HC])
        rc = sb("rc", [P, 2, KD, HC])
        pn = sb("pn", [P, 2, KD, HC, NS])
        pt = sb("pt", [P, 2, KD, P])
        xb = sb("xb", [P, 2, D])
        ot = [sb(f"ot{a}", [P, 2, D]) for a in range(2)]
        pVo = [ps(f"pVo{b}", [P, KD, D]) for b in range(4)]
        pS = ps("pS", [P, 2, KD, HC, NS])
        pT = ps("pT", [P, 2, KD, P])
        pO = [ps(f"pO{a}", [P, 2, D]) for a in range(2)]
        kv_ps, kv_sb, kx_ok, vx_ok, vo_ps, vo_sb = (sem(n) for n in ("kv_ps", "kv_sb", "kx_ok", "vx_ok", "vo_ps", "vo_sb"))
        s_ps, mx_ok, df_ok, ex_ok, sm_ok, rc_ok, pn_ok, pt_ps, pt_sb, o_ps, xb_ok, ot_ok = (
            sem(n) for n in ("s_ps", "mx_ok", "df_ok", "ex_ok", "sm_ok", "rc_ok", "pn_ok", "pt_ps", "pt_sb", "o_ps", "xb_ok", "ot_ok"))
        q_in = [sem(f"q_in{a}") for a in range(2)]
        o_out = [sem(f"o_out{a}") for a in range(2)]
        block = ctx.enter_context(nc.Block())

        def after(eng, semaphore, value):
            if not (isinstance(value, int) and value <= 0):
                eng.wait_ge(semaphore, value)

        def pairs(eng, body):
            body(0, 0)
            body(1, 1)
            with eng.Fori(1, NBODY // 2) as p:
                body(2 * p, 0)
                body(2 * p + 1, 1)

        @block.sync
        def _(sp):
            def load(i, a):
                after(sp, s_ps, i - 1)
                sp.dma_start(qt[a][:, :, :], dr.q[bass.ds(i, 1)].rearrange("o p k n -> p (o k) n")).then_inc(q_in[a], 16)
            pairs(sp, load)
            for a in range(2):
                sp.wait_ge(q_in[a], 16 * NBODY // 2)

        @block.gpsimd
        def _(pool):
            def body(i, a):
                after(pool, ot_ok, i)
                nc.gpsimd.tensor_tensor(xb[:, :, :], g.x1[:, bass.ds(2 * i, 2), :], bc(g.rows[:, ROW_CBO, :], 1, 2), ALU.add).then_inc(xb_ok, 1)
            pairs(pool, body)
            for a in range(2):
                pool.wait_ge(o_out[a], 16 * NBODY // 2)

        @block.tensor
        def _(pe):
            for n, w in enumerate((W_CK, W_CV)):
                for m in range(KD):
                    for k in range(KD):
                        last = nc.tensor.matmul(pVo[2 * n + m][:, :, :].rearrange("p k n -> p (k n)"), g.w_small[:, w, k, m * P:(m + 1) * P],
                                                g.o2T[:, k, :, :].rearrange("p e b -> p (e b)"), start=k == 0, stop=k == KD - 1)
                    last.then_inc(kv_ps, 1)
            pe.wait_ge(kv_sb, 2 * KD)

            def scores(i, a):
                pe.wait_ge(q_in[a], 8 * (i - a) + 16)
                pe.wait_ge(kx_ok, KD * (i + 1))
                after(pe, df_ok, i)
                for s in range(2):
                    for c in range(KD):
                        for b in range(2):
                            last = nc.tensor.matmul(pS[b * S:(b + 1) * S, s, c, :, :].rearrange("p h s -> p (h s)"),
                                                    qt[a][:, c, s * P + b * S:s * P + (b + 1) * S],
                                                    kx[:, c, 2 * s + b, :, :].rearrange("p h s -> p (h s)"), start=True, stop=True)
                last.then_inc(s_ps, 1)

            def values(i):
                pe.wait_ge(vx_ok, KD * (i + 1))
                after(pe, vo_sb, 4 * i)
                for b in range(4):
                    for c in range(KD):
                        last = nc.tensor.matmul(pVo[b][:, c, :], vx[:, c, b, :, :].rearrange("p h s -> p (h s)"), g.w_small[:, W_CO, c, :], start=True, stop=True)
                    last.then_inc(vo_ps, 1)

            def end_turn(i):
                pe.wait_ge(pn_ok, i + 1)
                for s in range(2):
                    for c in range(KD):
                        last = nc.tensor.transpose(pT[:, s, c, :], pn[:, s, c, :, :].rearrange("p h s -> p (h s)"), g.ident[:, :])
                last.then_inc(pt_ps, 1)

            def end(i, a):
                pe.wait_ge(pt_sb, i + 1)
                pe.wait_ge(vo_sb, 4 * (i + 1))
                after(pe, ot_ok, i - 1)
                for s in range(2):
                    for b in range(2):
                        for c in range(KD):
                            last = nc.tensor.matmul(pO[a][b * S:(b + 1) * S, s, :], pt[:, s, c, b * S:(b + 1) * S], vo[:, 2 * s + b, c, :],
                                                    start=c == 0, stop=c == KD - 1)
                last.then_inc(o_ps, 1)

            def body(i, a):
                scores(i, a)
                values(i)
                end_turn(i)
                end(i, a)
            pairs(pe, body)

        @block.scalar
        def _(act):
            for n, (col, to) in enumerate(((COL_CBK, k2), (COL_CBV, v2))):
                for m in range(KD):
                    act.wait_ge(kv_ps, KD * n + m + 1)
                    nc.scalar.activation(to[:, m, :, :].rearrange("p b e -> p e b"), pVo[2 * n + m][:, :, :].rearrange("p k n -> p (k n)").rearrange("p (e b) -> p e b", e=NS),
                                         ACT.Identity, bias=g.cols[:, col, m:m + 1]).then_inc(kv_sb, 1)

            def body(i, a):
                act.wait_ge(df_ok, i + 1)
                after(act, pn_ok, i)
                nc.scalar.activation(ex[:, :, :, :, :], df[:, :, :, :, :], ACT.Exp, scale=SCALE).then_inc(ex_ok, 1)
                for b in range(4):
                    act.wait_ge(vo_ps, 4 * i + b + 1)
                    after(act, o_ps, i)
                    nc.scalar.activation(vo[:, b, :, :], pVo[b][:, :, :], ACT.Copy).then_inc(vo_sb, 1)
                act.wait_ge(pt_ps, i + 1)
                nc.scalar.activation(pt[:, :, :, :], pT[:, :, :, :], ACT.Copy).then_inc(pt_sb, 1)
                act.wait_ge(ot_ok, i + 1)
                act.dma_start(dr.out[:, bass.ds(2 * i, 2), :], ot[a][:, :, :]).then_inc(o_out[a], 16)
            pairs(act, body)

        @block.vector
        def _(dve):
            v = nc.vector
            mask = bc(bc(g.headmask[:, :], 1, 4), 3, NS)
            dve.wait_ge(kv_sb, 2 * KD)

            def masked(i, to, source, done, used, per_body):
                after(dve, used, per_body * i)
                for c in range(KD):
                    v.tensor_tensor(to[:, c, :, :, :], bc(source[:, c, bass.ds(4 * i, 4), :], 2, HC), mask, ALU.mult).then_inc(done, 1)

            def body(i, a):
                masked(i, kx, k2, kx_ok, s_ps, 1)
                masked(i, vx, v2, vx_ok, vo_ps, 4)
                dve.wait_ge(s_ps, i + 1)
                after(dve, df_ok, i)
                v.tensor_reduce(mx[:, :, :, :], pS[:, :, :, :, :], AX_X, ALU.max).then_inc(mx_ok, 1)
                dve.wait_ge(mx_ok, i + 1)
                after(dve, ex_ok, i)
                v.tensor_tensor(df[:, :, :, :, :], pS[:, :, :, :, :], bc(mx[:, :, :, :], 4, NS), ALU.subtract).then_inc(df_ok, 1)
                dve.wait_ge(ex_ok, i + 1)
                after(dve, rc_ok, i)
                v.tensor_reduce(sm[:, :, :, :], ex[:, :, :, :, :], AX_X, ALU.add).then_inc(sm_ok, 1)
                dve.wait_ge(sm_ok, i + 1)
                after(dve, pn_ok, i)
                v.reciprocal(rc[:, :, :, :], sm[:, :, :, :]).then_inc(rc_ok, 1)
                dve.wait_ge(rc_ok, i + 1)
                after(dve, pt_ps, i)
                v.tensor_tensor(pn[:, :, :, :, :], ex[:, :, :, :, :], bc(rc[:, :, :, :], 4, NS), ALU.mult).then_inc(pn_ok, 1)
                dve.wait_ge(o_ps, i + 1)
                dve.wait_ge(xb_ok, i + 1)
                if not (isinstance(i, int) and i < 2):
                    dve.wait_ge(o_out[a], 8 * (i - a))
                v.tensor_tensor(ot[a][:, :, :], pO[a][:, :, :], xb[:, :, :], ALU.add).then_inc(ot_ok, 1)
            pairs(dve, body)


def consts():
    p = np.arange(P)
    ident = np.eye(P, dtype=np.float32)
    tri = np.concatenate([(p[:, None] < p[None, :]), np.ones((P, P), bool)], axis=1).astype(np.float32)
    rev = np.zeros((P, P), np.float32)
    rev[:, 0:E1] = E1 - np.arange(E1)
    rev[:, 32:32 + E1] = SLOT * np.arange(E1)
    rev[:, 64:64 + NT] = np.arange(NT)
    headmask = (p[:, None] // DH == np.arange(HC)[None, :]).astype(np.float32)
    batchmask = (p[:, None] // 32 % 2 == np.arange(2)[None, :]).astype(np.float32)
    stack = (p[:, None] % 32 == np.arange(NB)[None, :]).astype(np.float32)
    return {"stack": stack, "batchmask": batchmask, "ident": ident, "tri": tri, "rev": rev, "headmask": headmask, "ones": np.ones((4, 512), np.float32)}


def layout(a):
    lay = consts()
    lay["x_tm"] = a["x"].reshape(TT, P, D).transpose(1, 0, 2)
    lay["condT"] = a["cond_256"].T
    lay["gg_W"] = a["L0_cond_gg_W"]
    lay["gg_b"] = a["L0_cond_gg_b"][None]
    lay["wg_b"] = a["L0_cond_wg_b"][None]
    lay["wg_W"] = a["L0_cond_wg_W"].reshape(KD, P, E1).transpose(1, 0, 2)
    lay["rms_w"] = a["L0_cond_rms_w"].reshape(KD, P).T
    for l, n in enumerate(("W1", "W2", "W3")):
        w = a["L0_cond_" + n]
        lay[f"w{l}"] = w.reshape(E1, w.shape[1] // P, P, w.shape[2]).transpose(0, 2, 1, 3).reshape(E1, P, -1)
    lay["b12"] = np.concatenate([a["L0_cond_b1"].reshape(E1, KM, P), a["L0_cond_b2"].reshape(E1, KM, P)], axis=1).transpose(0, 2, 1)
    lay["b3"] = a["L0_cond_b3"][:, None]
    c2, f = "L0_cond2_", "L0_ffn_"
    small = [a["L0_attn_Wv"].T, a["L0_attn_Wo"].T, a[c2 + "Wq"].T, a[c2 + "Wk"].T, a[c2 + "Wv"].T, a[f + "d_Wq"], a[f + "d_Wk"], a[f + "d_Wv"],
             a[f + "d_Wo"], a[f + "c_Wq"], a[f + "c_Wk"], a[f + "c_Wv"], a[f + "c_Wo"]]
    lay["w_small"] = np.stack([w.reshape(KD, P, D).transpose(1, 0, 2) for w in small], axis=1)
    p, j = np.arange(P)[:, None], np.arange(4)[None, :]
    feature = 32 * (2 * j + p // 64) + p % 32
    lay["wo4"] = a[c2 + "Wo"].T[feature]
    lay["adaw"] = np.stack([a[c2 + n].T for n in ("g1w", "b1w", "g2w", "b2w")], axis=1)
    lay["adab"] = np.stack([a[c2 + n].reshape(KD, P).T for n in ("g1b", "b1b", "g2b", "b2b")], axis=1)
    lay["w_ff"] = np.stack([a[c2 + "gate_w"].T.reshape(KD, P, FH).transpose(1, 0, 2).reshape(P, -1),
                            a[c2 + "hid_w"].T.reshape(KD, P, FH).transpose(1, 0, 2).reshape(P, -1),
                            a[c2 + "out_w"].T.reshape(FH // P, P, D).transpose(1, 0, 2).reshape(P, -1)], axis=1)
    lay["rows"] = np.stack([a["L0_attn_bv"], a["L0_attn_bo"], a[f + "d_bo"], a[f + "c_bo"]])[None]
    cols = [a["L0_attn_bv"], a[f + "d_bq"], a[f + "d_bk"], a[f + "d_bv"], a[f + "c_bq"], a[f + "c_bk"], a[f + "c_bv"]]
    lay["cols"] = np.stack([v.reshape(KD, P).T for v in cols], axis=1)
    lay["slotT"] = a[f + "slot_query"][0].T.reshape(KD, P, NS).transpose(1, 0, 2)
    lay["slot_tm"] = a[f + "slot_query"][0][p[:, 0] % NS]
    lay["ln"] = np.stack([a[f + "e_ln_g"][p[:, 0] % NS], a[f + "e_ln_b"][p[:, 0] % NS]], axis=1)
    eb = np.stack([a[f + "e_b1"], a[f + "e_bg"]], axis=1).reshape(NS, 4, 4, P)
    lay["eb"] = eb.transpose(3, 0, 2, 1).reshape(P, NS, 16)
    lay["b2"] = a[f + "e_b2"].reshape(NS, KD, P).transpose(2, 1, 0)
    lay["w_slot"] = np.concatenate([a[f + n].reshape(NS, -1, P, a[f + n].shape[2]).transpose(0, 2, 1, 3).reshape(NS, P, -1)
                                    for n in ("e_W1", "e_Wg", "e_W2")], axis=2)
    return lay


def program(nc, dr):
    with ExitStack() as ctx:
        sb, ps, sem = scope(nc, ctx, "k")
        g = Env()
        g.x = sb("x", [P, TT, D])
        g.x1 = sb("x1", [P, TT, D])
        g.ident = sb("ident", [P, P])
        g.tri = sb("tri", [P, 2 * P])
        g.rev = sb("rev", [P, P])
        g.headmask = sb("headmask", [P, HC])
        g.batchmask = sb("batchmask", [P, 2])
        g.slot = [sb(f"slot{c}", [P, TT], U32) for c in range(2)]
        g.weight = [sb(f"weight{c}", [P, TT]) for c in range(2)]
        g.tile_expert = sb("tile_expert", [P, NT], I32)
        g.w_small = sb("w_small", [P, 13, KD, D])
        g.w_o1 = g.w_small[:, W_O1]
        g.wo4 = sb("wo4", [P, 4, D])
        g.rows = sb("rows", [P, 4, D])
        g.cols = sb("cols", [P, 7, KD])
        g.ada = sb("ada", [P, 4, KD, NB])
        g.inv1 = sb("inv1", [P, TT])
        route(nc, g, dr)
        experts(nc, g, dr)
        g.w_ff = sb("w_ff", [P, 3, KD * FH])
        g.ss2 = sb("ss2", [P, TT])
        self_attention(nc, g, dr, True, [g.w_small[:, W_V1]], None, g.x, g.x1, None)
        project_first(nc, g, dr)
        self_attention(nc, g, dr, False, [g.w_small[:, W_Q2], g.w_small[:, W_K2], g.w_small[:, W_V2]], g.wo4[:, :, :], g.x1, g.x, g.ss2)
        swiglu(nc, g, dr)
        g.oT = g.wo4[:, :, :].rearrange("p j n -> p (j n)").rearrange("p (k a b s) -> p k a b s", k=KD, a=TT, b=2)
        g.resT, g.hT, g.baseT, g.o2T = (
            g.x[:, 4 * n:4 * n + 4, :].rearrange("p t n -> p (t n)").rearrange("p (k e b) -> p k e b", k=KD, e=NS) for n in range(4))
        g.slot_tm = sb("slot_tm", [P, D])
        g.ln = sb("ln", [P, 2, D])
        g.eb = sb("eb", [P, NS, 4 * 4])
        g.b2 = sb("b2", [P, KD, NS])
        g.stack = sb("stack", [P, NB])
        g.ffn_in = sem("ffn_in")
        g.ring_in = [sem(f"ring_in{r}") for r in range(NRING)]
        with ExitStack() as ring:
            g.ring = [g.w_ff[:, :, :].rearrange("p n m -> p (n m)")]
            for r in range(1, NRING):
                g.ring.append(ring.enter_context(nc.sbuf_tensor(f"ring{r}", [P, W2_AT + NJ * D], F32)))
            slots(nc, g, dr)
            slot_norm(nc, g, dr)
            slot_experts(nc, g, dr)
        tokens(nc, g, dr)


def kernel(**inputs):
    import concourse.bacc as bacc
    from concourse.bass_utils import run_bass_kernel_spmd
    lay = layout({n: np.asarray(v) for n, v in inputs.items()})
    nc = bacc.Bacc("TRN2", target_bir_lowering=False, num_devices=1)
    arrays, dr = {}, Env()
    for n, v in lay.items():
        v = np.ascontiguousarray(v)
        arrays["in_" + n] = v
        dr.__dict__[n] = nc.dram_tensor("in_" + n, v.shape, mybir.dt.from_np(v.dtype), kind="ExternalInput").ap()
    dr.w = [dr.w0, dr.w1, dr.w2]
    dr.xs = nc.dram_tensor("rows_of_experts", (NT * SLOT, D), F32, kind="Internal").ap()
    dr.ys = nc.dram_tensor("results_of_experts", (NT * SLOT, D), F32, kind="Internal").ap()
    dr.heads = nc.dram_tensor("results_of_heads", (NB, NH, S, DH), F32, kind="Internal").ap()
    dr.q = nc.dram_tensor("queries_of_tokens", (NBODY, P, KD, PB), F32, kind="Internal").ap()
    dr.out = nc.dram_tensor("out", (P, TT, D), F32, kind="ExternalOutput").ap()
    program(nc, dr)
    r = run_bass_kernel_spmd(nc, [arrays], core_ids=[0])
    return r.results[0]["out"].transpose(1, 0, 2).reshape(NB, S, D)
```

```python
from contextlib import ExitStack

import numpy as np

import concourse.bass as bass
from concourse import mybir

ALU = mybir.AluOpType
ACT = mybir.ActivationFunctionType
F32 = mybir.dt.float32
F32R = mybir.dt.float32r
BF16 = mybir.dt.bfloat16
U32 = mybir.dt.uint32
I32 = mybir.dt.int32
AX_X = mybir.AxisListType.X

P = 128
NB, S, D = 32, 64, 256
T = NB * S
TT = T // P
KD = D // P
DC = 64
E1, M1 = 8, 512
KM = M1 // P
SLOT = 256
NT = (2 * T + E1 * (SLOT - 1)) // SLOT
NH, DH = 16, 16
HC = P // DH
FH = 1024
NS = 16
EPS = 1e-6
LN_EPS = 1e-5
SCALE = float(DH) ** -0.5
PB = 2 * P
NBODY = T // PB


W_V1, W_O1, W_Q2, W_K2, W_V2, W_DQ, W_DK, W_DV, W_DO, W_CQ, W_CK, W_CV, W_CO = range(13)
ROW_BV1, ROW_BO1, ROW_DBO, ROW_CBO = range(4)
COL_BV1, COL_DBQ, COL_DBK, COL_DBV, COL_CBQ, COL_CBK, COL_CBV = range(7)


class Env:
    pass


def scope(nc, ctx, tag):
    def sb(name, shape, dt=F32):
        return ctx.enter_context(nc.sbuf_tensor(f"{tag}_{name}", shape, dt))

    def ps(name, shape, dt=F32):
        return ctx.enter_context(nc.psum_tensor(f"{tag}_{name}", shape, dt))

    sems = []

    def sem(name):
        sems.append(nc.alloc_semaphore(name=f"{tag}_{name}"))
        return sems[-1]

    @ctx.callback
    def _():
        if sems:
            nc.clear_and_free_semaphores(sems)
            nc.all_engine_barrier()
    return sb, ps, sem


def bc(ap, axis, n):
    shape = list(ap.shape)
    return ap.unsqueeze(axis).to_broadcast(shape[:axis] + [n] + shape[axis:])


def mm3(nc, out, ah, al, bh, bl, start, stop):
    nc.tensor.matmul(out, ah, bh, start=start, stop=False)
    nc.tensor.matmul(out, al, bh, start=False, stop=False)
    return nc.tensor.matmul(out, ah, bl, start=False, stop=stop)


def f32(ap):
    return ap.bitcast(F32)


def route(nc, g, dr):
    with ExitStack() as ctx:
        sb, ps, sem = scope(nc, ctx, "route")
        zero = sb("zero", [P, 2048])
        cond_aug = sb("cond_aug", [DC + 2, NB])
        condx = sb("condx", [DC + 2, T])
        gg_aug = sb("gg_aug", [DC + 2, E1])
        wg = sb("wg", [P, KD, E1])
        rms = sb("rms", [P, KD])
        wgs = sb("wgs", [P, KD, 32])
        xT = sb("xT", [P, KD, T])
        sq = sb("sq", [P, TT, D])
        ss = sb("ss", [P, TT])
        rr = sb("rr", [P, TT])
        lT = sb("lT", [P, 512])
        lg = sb("lg", [P, TT, E1])
        gt = sb("gt", [P, TT, E1])
        tmp = sb("tmp", [P, TT, E1])
        col = sb("col", [P, TT])
        oh1 = sb("oh1", [P, TT, E1])
        oh2 = sb("oh2", [P, TT, E1])
        ohb = sb("ohb", [P, TT, E1])
        cum = [sb(f"cum{i}", [P, TT, E1]) for i in range(2)]
        slotf = sb("slotf", [P, TT, E1])
        cmp1 = sb("cmp1", [P, E1, E1])
        cmp2 = sb("cmp2", [P, NT, E1])
        ntl = sb("ntl", [P, E1])
        nin = [sb(f"nin{i}", [P, E1]) for i in range(2)]
        tef = sb("tef", [P, NT])
        pT = [ps(f"pT{i}", [P, 512]) for i in range(3)]
        pG = ps("pG", [P, 512])
        pC = ps("pC", [P, TT, E1])
        pL = ps("pL", [P, 512])
        pR = ps("pR", [P, TT, E1])
        pS = ps("pS", [P, TT, E1])

        zero_set, x_in, small_in, const_in = sem("zero_set"), sem("x_in"), sem("small_in"), sem("r_const_in")
        zero_out, late_in = sem("zero_out"), sem("late_in")
        xT_ps, xT_dve, xT_act = sem("xT_ps"), sem("xT_dve"), sem("xT_act")
        sumsq, root = sem("sumsq"), sem("root")
        cond_ps, gateT_ps, gateT_sb, gate_ps = sem("cond_ps"), sem("gateT_ps"), sem("gateT_sb"), sem("gate_ps")
        logits, expd, onehot, rank_ps = sem("logits"), sem("expd"), sem("onehot"), sem("rank_ps")
        condx_ok = sem("condx_ok")
        slots, wgs_ok, dv, recip = sem("slots"), sem("wgs_ok"), sem("r_dv"), sem("recip")

        block = ctx.enter_context(nc.Block())

        @block.sync
        def _(sp):
            sp.dma_start(g.x[:, :, :], dr.x_tm).then_inc(x_in, 16)
            sp.wait_ge(zero_set, 1)
            sp.wait_ge(const_in, 16 * 4)
            sp.wait_ge(small_in, 16 * 7)
            xs = dr.xs.rearrange("(n p) c -> n p c", p=P)
            for j in range(0, NT * SLOT // P, 8):
                n = min(8, NT * SLOT // P - j)
                sp.dma_start(xs[j:j + n].rearrange("n p c -> p n c"),
                             zero[:, 0:n * D].rearrange("p (n c) -> p n c", c=D)).then_inc(zero_out, 16)
            sp.dma_start(g.w_small[:, :, :, :], dr.w_small).then_inc(late_in, 16)
            sp.dma_start(g.wo4[:, :, :], dr.wo4).then_inc(late_in, 16)
            sp.dma_start(g.rows[:, :, :], dr.rows.to_broadcast([P, 4, D])).then_inc(late_in, 16)
            sp.dma_start(g.cols[:, :, :], dr.cols).then_inc(late_in, 16)
            sp.dma_start(g.batchmask[:, :], dr.batchmask).then_inc(late_in, 16)
            sp.wait_ge(late_in, 16 * 5)

        @block.gpsimd
        def _(pool):
            nc.gpsimd.memset(zero[:, :], 0.0).then_inc(zero_set, 1)
            pool.wait_ge(zero_out, 16 * ((NT * SLOT // P + 7) // 8))

        @block.scalar
        def _(act):
            act.dma_start(g.ident[:, :], dr.ident).then_inc(const_in, 16)
            act.dma_start(g.tri[:, :], dr.tri).then_inc(const_in, 16)
            act.dma_start(g.rev[:, :], dr.rev).then_inc(const_in, 16)
            act.dma_start(g.headmask[:, :], dr.headmask).then_inc(const_in, 16)
            act.dma_start(cond_aug[0:DC, :], dr.condT).then_inc(small_in, 16)
            act.dma_start(cond_aug[DC:DC + 2, :], dr.ones[0:2, 0:NB]).then_inc(small_in, 16)
            act.dma_start(gg_aug[0:DC, :], dr.gg_W).then_inc(small_in, 16)
            act.dma_start(gg_aug[DC:DC + 1, :], dr.gg_b).then_inc(small_in, 16)
            act.dma_start(gg_aug[DC + 1:DC + 2, :], dr.wg_b).then_inc(small_in, 16)
            act.dma_start(wg[:, :, :], dr.wg_W).then_inc(small_in, 16)
            act.dma_start(rms[:, :], dr.rms_w).then_inc(small_in, 16)
            act.wait_ge(x_in, 16)
            for t in range(TT):
                nc.scalar.activation(sq[:, t, :], g.x[:, t, :], ACT.Square, accum_out=ss[:, t:t + 1]).then_inc(sumsq, 1)
                if t % 4 == 3:
                    i = t // 2
                    act.wait_ge(xT_ps, i + 1)
                    nc.scalar.activation(xT[:, :, i * PB:(i + 1) * PB],
                                         pT[i % 3][:, :].rearrange("p (k n) -> p k n", k=KD), ACT.Copy).then_inc(xT_act, 1)
            act.wait_ge(recip, 1)
            nc.scalar.activation(rr[:, :], rr[:, :], ACT.Sqrt).then_inc(root, 1)
            act.wait_ge(gateT_ps, 1)
            nc.scalar.activation(lT[:, :], pG[:, :], ACT.Copy).then_inc(gateT_sb, 1)
            act.wait_ge(logits, 1)
            nc.scalar.activation(gt[:, :, :], lg[:, :, :], ACT.Exp).then_inc(expd, 1)

        @block.tensor
        def _(pe):
            pe.wait_ge(const_in, 64)
            pe.wait_ge(x_in, 16)
            for i in range(NBODY):
                if i >= 3:
                    pe.wait_ge(xT_dve if (i - 3) % 2 == 0 else xT_act, (i - 3) // 2 + 1)
                for j in range(2):
                    for k in range(KD):
                        last = nc.tensor.transpose(pT[i % 3][:, k * PB + j * P:k * PB + (j + 1) * P],
                                                   g.x[:, 2 * i + j, k * P:(k + 1) * P], g.ident[:, :])
                last.then_inc(xT_ps, 1)
            pe.wait_ge(small_in, 16 * 7)
            pe.wait_ge(condx_ok, 1)
            for t in range(TT):
                last = nc.tensor.matmul(pC[:, t, :], condx[:, t * P:(t + 1) * P], gg_aug[:, :],
                                        start=True, stop=True)
            last.then_inc(cond_ps, 1)
            pe.wait_ge(xT_dve, NBODY // 2)
            pe.wait_ge(xT_act, NBODY // 2)
            pe.wait_ge(wgs_ok, KD)
            for k in range(KD):
                for c in range(4):
                    last = nc.tensor.matmul(pG[32 * c:32 * c + 32, :], wgs[:, k, :], xT[:, k, c * 512:(c + 1) * 512],
                                            start=(k == 0), stop=(k == KD - 1))
            last.then_inc(gateT_ps, 1)
            pe.wait_ge(gateT_sb, 1)
            for j in range(4):
                last = nc.tensor.transpose(pL[:, j * P:(j + 1) * P], lT[:, j * P:(j + 1) * P], g.ident[:, :])
            last.then_inc(gate_ps, 1)
            pe.wait_ge(onehot, 1)
            nc.tensor.matmul(pR[:, :, :], g.tri[:, 0:P], ohb[:, :, :], start=True, stop=True)
            nc.tensor.matmul(pS[:, :, :], g.tri[:, P:2 * P], ohb[:, :, :], start=True, stop=True).then_inc(rank_ps, 1)

        @block.vector
        def _(dve):
            n = [0]

            def step(ins):
                n[0] += 1
                ins.then_inc(dv, 1)
                dve.wait_ge(dv, n[0])
            v = nc.vector
            step(v.memset(wgs[:, :, :], 0.0))
            dve.wait_ge(small_in, 16 * 7)
            v.tensor_copy(condx[:, :].rearrange("p (b s) -> p b s", s=S), bc(cond_aug[:, :], 2, S)).then_inc(condx_ok, 1)
            for k in range(KD):
                v.tensor_scalar(wgs[:, k, 0:E1], wg[:, k, :], rms[:, k:k + 1], None, ALU.mult).then_inc(wgs_ok, 1)
            for i in range(0, NBODY, 2):
                dve.wait_ge(xT_ps, i + 1)
                v.tensor_copy(xT[:, :, i * PB:(i + 1) * PB],
                              pT[i % 3][:, :].rearrange("p (k n) -> p k n", k=KD)).then_inc(xT_dve, 1)
            dve.wait_ge(sumsq, TT)
            step(v.tensor_scalar(ss[:, :], ss[:, :], 1.0 / D, EPS, ALU.mult, ALU.add))
            v.reciprocal(rr[:, :], ss[:, :]).then_inc(recip, 1)
            dve.wait_ge(root, 1)
            dve.wait_ge(gate_ps, 1)
            step(v.tensor_tensor(lg[:, :, :].rearrange("p (c j) e -> p c j e", c=4),
                                 pL[:, :].rearrange("p (j c e) -> p c j e", j=4, c=4)[:, :, :, 0:E1],
                                 bc(rr[:, :].rearrange("p (c j) -> p c j", c=4), 3, E1), ALU.mult))
            dve.wait_ge(cond_ps, 1)
            step(v.tensor_tensor(lg[:, :, :], lg[:, :, :], pC[:, :, :], ALU.add))
            step(v.tensor_reduce(col[:, :], lg[:, :, :], AX_X, ALU.max))
            v.tensor_tensor(lg[:, :, :], lg[:, :, :], bc(col[:, :], 2, E1), ALU.subtract).then_inc(logits, 1)
            dve.wait_ge(expd, 1)
            step(v.tensor_reduce(col[:, :], gt[:, :, :], AX_X, ALU.add))
            step(v.reciprocal(col[:, :], col[:, :]))
            step(v.tensor_tensor(gt[:, :, :], gt[:, :, :], bc(col[:, :], 2, E1), ALU.mult))
            rev = bc(g.rev[:, 0:E1], 1, TT)
            for c, oh in enumerate((oh1, oh2)):
                step(v.tensor_reduce(g.weight[c][:, :], gt[:, :, :], AX_X, ALU.max))
                step(v.tensor_tensor(tmp[:, :, :], gt[:, :, :], bc(g.weight[c][:, :], 2, E1), ALU.is_equal))
                step(v.tensor_tensor(tmp[:, :, :], tmp[:, :, :], rev, ALU.mult))
                step(v.tensor_reduce(col[:, :], tmp[:, :, :], AX_X, ALU.max))
                step(v.tensor_tensor(oh[:, :, :], rev, bc(col[:, :], 2, E1), ALU.is_equal))
                if c == 0:
                    step(v.scalar_tensor_tensor(gt[:, :, :], oh[:, :, :], -2.0, gt[:, :, :], ALU.mult, ALU.add))
            v.tensor_tensor(ohb[:, :, :], oh1[:, :, :], oh2[:, :, :], ALU.add).then_inc(onehot, 1)
            dve.wait_ge(rank_ps, 1)
            step(v.tensor_copy(cum[0][:, :, :], pS[:, :, :]))
            a = 0
            for sh in (1, 2, 4, 8):
                v.tensor_copy(cum[1 - a][:, 0:sh, :], cum[a][:, 0:sh, :])
                step(v.tensor_tensor(cum[1 - a][:, sh:TT, :], cum[a][:, sh:TT, :], cum[a][:, 0:TT - sh, :], ALU.add))
                a = 1 - a
            step(v.tensor_tensor(cmp1[:, :, :], bc(cum[a][:, TT - 1, :], 2, E1), bc(g.rev[:, 32:32 + E1], 1, E1), ALU.is_gt))
            step(v.tensor_reduce(ntl[:, :], cmp1[:, :, :], AX_X, ALU.add))
            step(v.tensor_copy(nin[0][:, :], ntl[:, :]))
            b = 0
            for sh in (1, 2, 4):
                v.tensor_copy(nin[1 - b][:, 0:sh], nin[b][:, 0:sh])
                step(v.tensor_tensor(nin[1 - b][:, sh:E1], nin[b][:, sh:E1], nin[b][:, 0:E1 - sh], ALU.add))
                b = 1 - b
            step(v.tensor_tensor(cmp2[:, :, :], bc(nin[b][:, :], 1, NT), bc(g.rev[:, 64:64 + NT], 2, E1), ALU.is_le))
            step(v.tensor_reduce(tef[:, :], cmp2[:, :, :], AX_X, ALU.add))
            step(v.tensor_scalar(g.tile_expert[:, :], tef[:, :], float(E1 - 1), None, ALU.min))
            step(v.tensor_tensor(nin[1 - b][:, :], nin[b][:, :], ntl[:, :], ALU.subtract))
            step(v.tensor_tensor(slotf[:, :, :], cum[a][:, :, :], pS[:, :, :], ALU.subtract))
            step(v.tensor_tensor(slotf[:, :, :], slotf[:, :, :], pR[:, :, :], ALU.add))
            step(v.scalar_tensor_tensor(slotf[:, :, :], bc(nin[1 - b][:, :], 1, TT), float(SLOT), slotf[:, :, :],
                                        ALU.mult, ALU.add))
            for c, oh in enumerate((oh1, oh2)):
                step(v.tensor_tensor(tmp[:, :, :], oh[:, :, :], slotf[:, :, :], ALU.mult))
                step(v.tensor_reduce(col[:, :], tmp[:, :, :], AX_X, ALU.add))
                v.tensor_copy(g.slot[c][:, :], col[:, :]).then_inc(slots, 1)
                dve.wait_ge(slots, c + 1)


def experts(nc, g, dr):
    with ExitStack() as ctx:
        sb, ps, sem = scope(nc, ctx, "moe")
        WN = (KD * M1, KM * M1, KM * D)
        raw_w = [[sb(f"raw{l}{a}", [P, WN[l]]) for l in range(3)] for a in range(2)]
        wh = [[sb(f"wh{l}{a}", [P, WN[l]], F32R) for l in range(3)] for a in range(2)]
        wl = [[sb(f"wl{l}{a}", [P, WN[l]], F32R) for l in range(3)] for a in range(2)]
        b12 = [sb(f"b12{a}", [P, 2 * KM]) for a in range(2)]
        b3 = [sb(f"b3{a}", [P, D]) for a in range(2)]
        xr = [sb(f"xr{a}", [P, 2, D]) for a in range(2)]
        xh = sb("xh", [P, KD, SLOT], F32R)
        xl = sb("xl", [P, KD, SLOT], F32R)
        ht = [sb(f"ht{l}", [P, KM, SLOT]) for l in range(2)]
        hh = [sb(f"hh{l}", [P, KM, SLOT], F32R) for l in range(2)]
        hl = [sb(f"hl{l}", [P, KM, SLOT], F32R) for l in range(2)]
        ys = [sb(f"ysb{a}", [P, 2, D]) for a in range(2)]
        pX = ps("pX", [P, KD, SLOT])
        pH = [[ps(f"pH{l}{i}", [P, 2, SLOT]) for i in range(2)] for l in range(2)]
        pY = ps("pY", [P, 2, D])

        raw_in = [[sem(f"raw_in{l}{a}") for l in range(3)] for a in range(2)]
        x_in = [sem(f"x_in{a}") for a in range(2)]
        b_in = [sem(f"b_in{a}") for a in range(2)]
        y_out = [sem(f"y_out{a}") for a in range(2)]
        wh_ok = [sem(f"wh_ok{l}") for l in range(3)]
        wl_ok = [sem(f"wl_ok{l}") for l in range(3)]
        xT_ps, xh_ok, xl_ok = sem("xT_ps"), sem("xh_ok"), sem("xl_ok")
        h_ps = [sem(f"h_ps{l}") for l in range(2)]
        h_t = [sem(f"h_t{l}") for l in range(2)]
        hh_ok = [sem(f"hh_ok{l}") for l in range(2)]
        hl_ok = [sem(f"hl_ok{l}") for l in range(2)]
        y_ps, y_ok = sem("y_ps"), sem("y_ok")
        scat = sem("scat")

        block = ctx.enter_context(nc.Block())

        def tiles(eng, step):
            step(0, 0, first=True)
            with eng.Fori(0, (NT - 3) // 2) as p:
                step(2 * p + 1, 1)
                step(2 * p + 2, 0)
            for j in range(1 + 2 * ((NT - 3) // 2), NT):
                step(j, j % 2, last=(j == NT - 1))

        def landed(j, a):
            return 8 * (j - a) + 16

        xs_v = dr.xs.rearrange("(n s p) c -> n p s c", p=P, s=2)
        ys_v = dr.ys.rearrange("(n s p) c -> n p s c", p=P, s=2)

        @block.sync
        def _(sp):
            def step(j, a, first=False, last=False):
                e = sp.value_load(g.tile_expert[0:1, bass.ds(j, 1)], min_val=0, max_val=E1 - 1)
                k = j if isinstance(j, int) else None
                early = k is not None and k < 2
                if not early:
                    sp.wait_ge(xT_ps, j - 1)

                def rows():
                    sp.dma_start(xr[a][:, :, :], xs_v[bass.ds(j, 1)].rearrange("o p s c -> (o p) s c")).then_inc(x_in[a], 16)
                if not first:
                    rows()
                for l in range(3):
                    if not early:
                        sp.wait_ge(wl_ok[l], j - 1)
                        sp.wait_ge(wh_ok[l], j - 1)
                    sp.dma_start(raw_w[a][l][:, :], dr.w[l][bass.ds(e, 1)].rearrange("o p n -> (o p) n")).then_inc(raw_in[a][l], 16)
                if first:
                    sp.wait_ge(scat, 16 * 2 * TT)
                    rows()
                if not early:
                    sp.wait_ge(h_t[1], 2 * (j - 1))
                    sp.wait_ge(y_ok, j - 1)
                sp.dma_start(b12[a][:, :], dr.b12[bass.ds(e, 1)].rearrange("o p n -> (o p) n")).then_inc(b_in[a], 16)
                sp.dma_start(b3[a][:, :], dr.b3[bass.ds(e, 1)].rearrange("o p n -> (o p) n").to_broadcast([P, D])).then_inc(b_in[a], 16)
            tiles(sp, step)

        @block.gpsimd
        def _(pool):
            for c in range(2):
                for t in range(TT):
                    nc.gpsimd.indirect_dma_start(
                        out=dr.xs, out_offset=bass.IndirectOffsetOnAxis(ap=g.slot[c][:, t:t + 1], axis=0),
                        in_=g.x[:, t, :], in_offset=None).then_inc(scat, 16)

            def step(j, a, first=False, last=False):
                if first:
                    return
                pool.wait_ge(wh_ok[1], j + 1)
                if not (isinstance(j, int) and j < 2):
                    pool.wait_ge(h_ps[1], 2 * (j - 1))
                nc.gpsimd.tensor_tensor(wl[a][1][:, :], raw_w[a][1][:, :], f32(wh[a][1][:, :]), ALU.subtract).then_inc(wl_ok[1], 1)
                store(j - 1, 1 - a)

            def store(j, a):
                pool.wait_ge(y_ok, j + 1)
                pool.dma_start(ys_v[bass.ds(j, 1)].rearrange("o p s c -> (o p) s c"), ys[a][:, :, :]).then_inc(y_out[a], 16)
            tiles(pool, step)
            store(NT - 1, (NT - 1) % 2)
            pool.wait_ge(y_out[0], 16 * ((NT + 1) // 2))
            pool.wait_ge(y_out[1], 16 * (NT // 2))

        @block.tensor
        def _(pe):
            def turn(j, a):
                pe.wait_ge(x_in[a], landed(j, a))
                if not (isinstance(j, int) and j == 0):
                    pe.wait_ge(xh_ok, j)
                    pe.wait_ge(xl_ok, j)
                for s in range(2):
                    for k in range(KD):
                        last = nc.tensor.transpose(pX[:, k, s * P:(s + 1) * P], xr[a][:, s, k * P:(k + 1) * P],
                                                   g.ident[:, :])
                last.then_inc(xT_ps, 1)

            def layer(j, a, l):
                pe.wait_ge(wh_ok[l], j + 1)
                pe.wait_ge(wl_ok[l], j + 1)
                kin = KD if l == 0 else KM
                ih, il = (xh, xl) if l == 0 else (hh[0], hl[0])
                if l == 0:
                    pe.wait_ge(xl_ok, j + 1)
                    pe.wait_ge(xh_ok, j + 1)
                w_h = wh[a][l][:, :].rearrange("p (k m) -> p k m", k=kin)
                w_l = wl[a][l][:, :].rearrange("p (k m) -> p k m", k=kin)
                for m in range(KM):
                    if m % 2 == 0 and not (isinstance(j, int) and j == 0):
                        pe.wait_ge(h_t[l], 2 * j - 1 + m // 2)
                    for k in range(kin):
                        if l == 1 and m == 0 and k % 2 == 0:
                            pe.wait_ge(hh_ok[0], 2 * j + 1 + k // 2)
                            pe.wait_ge(hl_ok[0], 2 * j + 1 + k // 2)
                        last = mm3(nc, pH[l][m // 2][:, m % 2, :], w_h[:, k, m * P:(m + 1) * P],
                                   w_l[:, k, m * P:(m + 1) * P], ih[:, k, :], il[:, k, :], k == 0, k == kin - 1)
                    if m % 2 == 1:
                        last.then_inc(h_ps[l], 1)

            def out_layer(j, a):
                pe.wait_ge(wh_ok[2], j + 1)
                pe.wait_ge(wl_ok[2], j + 1)
                pe.wait_ge(hh_ok[1], 2 * j + 2)
                pe.wait_ge(hl_ok[1], 2 * j + 2)
                if not (isinstance(j, int) and j == 0):
                    pe.wait_ge(y_ok, j)
                w_h = wh[a][2][:, :].rearrange("p (k n) -> p k n", k=KM)
                w_l = wl[a][2][:, :].rearrange("p (k n) -> p k n", k=KM)
                for s in range(2):
                    for k in range(KM):
                        last = mm3(nc, pY[:, s, :], hh[1][:, k, s * P:(s + 1) * P], hl[1][:, k, s * P:(s + 1) * P],
                                   w_h[:, k, :], w_l[:, k, :], k == 0, k == KM - 1)
                last.then_inc(y_ps, 1)

            def step(j, a, first=False, last=False):
                layer(j, a, 0)
                if not first:
                    out_layer(j - 1, 1 - a)
                if not last:
                    turn(j + 1, 1 - a)
                layer(j, a, 1)
            turn(0, 0)
            tiles(pe, step)
            out_layer(NT - 1, (NT - 1) % 2)

        @block.scalar
        def _(act):
            def split_w(j, a, l):
                act.wait_ge(raw_in[a][l], landed(j, a))
                if not (isinstance(j, int) and j < 2):
                    if l < 2:
                        act.wait_ge(h_ps[l], 2 * (j - 1))
                    else:
                        act.wait_ge(y_ps, j - 1)
                nc.scalar.activation(wh[a][l][:, :], raw_w[a][l][:, :], ACT.Copy).then_inc(wh_ok[l], 1)

            def split_x(j):
                act.wait_ge(xT_ps, j + 1)
                if not (isinstance(j, int) and j == 0):
                    act.wait_ge(h_ps[0], 2 * j)
                nc.scalar.activation(xh[:, :, :], pX[:, :, :], ACT.Copy).then_inc(xh_ok, 1)

            def relu(j, a, l, pairs=(0, 1)):
                if l == 0:
                    act.wait_ge(b_in[a], 2 * landed(j, a))
                for i in pairs:
                    act.wait_ge(h_ps[l], 2 * j + i + 1)
                    if not (isinstance(j, int) and j == 0):
                        act.wait_ge(hl_ok[l], 2 * j - 1 + i)
                    for m in range(2):
                        last = nc.scalar.activation(ht[l][:, 2 * i + m, :], pH[l][i][:, m, :], ACT.Relu,
                                                    bias=b12[a][:, l * KM + 2 * i + m:l * KM + 2 * i + m + 1])
                    last.then_inc(h_t[l], 1)

            def step(j, a, first=False, last=False):
                relu(j, a, 0)
                if not last:
                    split_w(j + 1, 1 - a, 0)
                    split_x(j + 1)
                relu(j, a, 1, (0,))
                if not last:
                    split_w(j + 1, 1 - a, 1)
                relu(j, a, 1, (1,))
                if not last:
                    split_w(j + 1, 1 - a, 2)
            for l in range(3):
                split_w(0, 0, l)
            split_x(0)
            tiles(act, step)

        @block.vector
        def _(dve):
            v = nc.vector

            def split_w(j, a, l):
                dve.wait_ge(wh_ok[l], j + 1)
                v.tensor_tensor(wl[a][l][:, :], raw_w[a][l][:, :], f32(wh[a][l][:, :]), ALU.subtract).then_inc(wl_ok[l], 1)

            def split_x(j):
                dve.wait_ge(xh_ok, j + 1)
                v.tensor_tensor(xl[:, :, :], pX[:, :, :], f32(xh[:, :, :]), ALU.subtract).then_inc(xl_ok, 1)

            def split_h(j, l):
                for i in range(2):
                    dve.wait_ge(h_t[l], 2 * j + i + 1)
                    if not (isinstance(j, int) and j == 0) and i == 0:
                        if l == 0:
                            dve.wait_ge(h_ps[1], 2 * j)
                        else:
                            dve.wait_ge(y_ps, j)
                    s = slice(2 * i, 2 * i + 2)
                    v.tensor_copy(hh[l][:, s, :], ht[l][:, s, :]).then_inc(hh_ok[l], 1)
                    dve.wait_ge(hh_ok[l], 2 * j + i + 1)
                    v.tensor_tensor(hl[l][:, s, :], ht[l][:, s, :], f32(hh[l][:, s, :]), ALU.subtract).then_inc(hl_ok[l], 1)

            def result(j, a):
                dve.wait_ge(y_ps, j + 1)
                dve.wait_ge(b_in[a], 2 * landed(j, a))
                if not (isinstance(j, int) and j < 2):
                    dve.wait_ge(y_out[a], landed(j, a) - 16)
                v.tensor_tensor(ys[a][:, :, :], pY[:, :, :], bc(b3[a][:, :], 1, 2), ALU.add).then_inc(y_ok, 1)

            def step(j, a, first=False, last=False):
                split_h(j, 0)
                if not last:
                    split_w(j + 1, 1 - a, 0)
                if not first:
                    result(j - 1, 1 - a)
                if not last:
                    split_x(j + 1)
                split_h(j, 1)
                if not last:
                    split_w(j + 1, 1 - a, 2)
            for l in range(3):
                split_w(0, 0, l)
            split_x(0)
            tiles(dve, step)
            result(NT - 1, (NT - 1) % 2)


KX_DVE = (4, 4)


def self_attention(nc, g, dr, first, w_raw, wo_raw, res, out, ssq):
    with ExitStack() as ctx:
        sb, ps, sem = scope(nc, ctx, "attn1" if first else "attn2")
        nw = len(w_raw)
        n_dve = KX_DVE[0 if first else 1]
        NK = KD if first else 1
        wh = [sb(f"wh{n}", [P, KD, D], F32R) for n in range(nw)]
        wl = [sb(f"wl{n}", [P, KD, D], F32R) for n in range(nw)]
        if first:
            rch = [sb(f"rch{a}", [P, 8, 2]) for a in range(2)]
            otm = [sb(f"otm{a}", [P, 8, 2, DH]) for a in range(2)]
            gat = [[sb(f"gat{c}{a}", [P, D]) for a in range(2)] for c in range(2)]
            ya = [[sb(f"ya{c}{a}", [P, D]) for a in range(2)] for c in range(2)]
        else:
            woh = sb("woh", [P, 4, D], F32R)
            wol = sb("wol", [P, 4, D], F32R)
            oh = sb("oh", [P, 4, 2, S], F32R)
            ol = sb("ol", [P, 4, 2, S], F32R)
            junk = [sb(f"junk{a}", [P, D]) for a in range(2)]
            u1 = sb("u1", [P, KD, PB])
            u2 = sb("u2", [P, KD, PB])
        yt = [sb(f"yt{a}", [P, D]) for a in range(2)]
        ih = sb("ih", [P, KD, 4, 2, S], F32R)
        il = sb("il", [P, KD, 4, 2, S], F32R)
        qT = None if first else sb("qT", [P, KD, PB])
        kT = sb("kT", [P, KD, PB])
        kx = sb("kx", [P, KD, HC, PB])
        vst = [sb(f"vst{a}", [P, 8, 2, 2, DH]) for a in range(2)]
        mx = [sb(f"mx{c}", [P, HC]) for c in range(2)]
        sm = [sb(f"sm{c}", [P, HC]) for c in range(2)]
        rc = None if first else [sb(f"rc{c}", [P, HC]) for c in range(2)]
        df = [sb(f"df{c}", [P, HC, S]) for c in range(2)]
        ex = [sb(f"ex{c}", [P, HC, S]) for c in range(2)]
        pn = None if first else [sb(f"pn{c}", [P, HC, S]) for c in range(2)]
        pt = [sb(f"pt{c}", [P, 4, P]) for c in range(2)]

        b0 = ps("b0", [P, 512])
        b1 = ps("b1", [P, 512])
        b2 = ps("b2", [P, 512])
        pS = [ps(f"pS{c}", [P, HC, S]) for c in range(2)]
        pT = [ps(f"pT{c}", [P, 4, P]) for c in range(2)]
        pV = ps("pV", [P, 512])
        pVf = pV[:, :].rearrange("p (j b s) -> p j b s", j=4, b=2)
        pVt = pV[:, :].rearrange("p (j b n) -> p j b n", j=8, b=2)

        wh_ok, wl_ok, vz_ok = sem("wh_ok"), sem("wl_ok"), sem("vz_ok")
        gat_in = [[sem(f"gat_in{c}{a}") for a in range(2)] for c in range(2)]
        ya_ok, yt_ok, x_ps, u1_ok, u2_ok, ih_ok, il_ok = (sem(n) for n in ("ya_ok", "yt_ok", "x_ps", "u1_ok", "u2_ok", "ih_ok", "il_ok"))
        q_ps, k_ps, v_ps, q_sb, k_sb, kx_dve, kx_act, v_sb = (sem(n) for n in ("q_ps", "k_ps", "v_ps", "q_sb", "k_sb", "kx_dve", "kx_act", "v_sb"))
        s_ps, mx_ok, df_ok, ex_ok, sm_ok, rc_ok, pn_ok = (sem(n) for n in ("s_ps", "mx_ok", "df_ok", "ex_ok", "sm_ok", "rc_ok", "pn_ok"))
        pt_ps, pt_sb, pv_ps, oh_ok, ol_ok, o_ps, o_sb, ot_ok, sq_ok = (sem(n) for n in ("pt_ps", "pt_sb", "pv_ps", "oh_ok", "ol_ok", "o_ps", "o_sb", "ot_ok", "sq_ok"))
        ff_in = sem("ff_in")
        o_out = [sem(f"o_out{a}") for a in range(2)]

        block = ctx.enter_context(nc.Block())

        def bodies(eng, body):
            body(0)
            body(1)
            with eng.Fori(2, NBODY - 1) as i:
                body(i)
            body(NBODY - 1)

        def opening(i):
            return isinstance(i, int) and i == 0

        def closing(i):
            return isinstance(i, int) and i == NBODY - 1

        def after(eng, semaphore, value):
            if not (isinstance(value, int) and value <= 0):
                eng.wait_ge(semaphore, value)

        if first:
            @block.sync
            def _(sp):
                def store(i, a):
                    sp.wait_ge(ot_ok, 2 * (2 * i + a) + 2)
                    for b in range(2):
                        sp.dma_start(dr.heads[bass.ds(4 * i + 2 * a + b, 1)].rearrange("o h q d -> (o q) h d"),
                                     otm[a][b * S:(b + 1) * S, :, :, :].rearrange("p j s d -> p (j s) d")).then_inc(o_out[a], 16)
                store(0, 0)
                store(0, 1)
                sp.dma_start(g.w_ff[:, :, :], dr.w_ff).then_inc(ff_in, 16)
                with sp.Fori(1, NBODY) as i:
                    store(i, 0)
                    store(i, 1)
                sp.wait_ge(ff_in, 16)
                for a in range(2):
                    sp.wait_ge(o_out[a], 16 * 2 * NBODY)

        @block.gpsimd
        def _(pool):
            for a in range(2):
                nc.gpsimd.memset(vst[a][:, :, :, :, :], 0.0).then_inc(vz_ok, 1)

            def gather(i):
                for a in range(2):
                    t = 2 * i + a
                    for c in range(2):
                        after(pool, ya_ok, 2 * (t - 2) + c + 1)
                        nc.gpsimd.indirect_dma_start(
                            out=gat[c][a][:, :], out_offset=None, in_=dr.ys,
                            in_offset=bass.IndirectOffsetOnAxis(ap=g.slot[c][:, t:t + 1], axis=0)).then_inc(gat_in[c][a], 16)

            def combine(i):
                for a in range(2):
                    t = 2 * i + a
                    pool.wait_ge(ya_ok, 2 * t + 2)
                    after(pool, x_ps, i)
                    nc.gpsimd.tensor_tensor(yt[a][:, :], ya[0][a][:, :], ya[1][a][:, :], ALU.add).then_inc(yt_ok, 1)

            def softmax_end(t):
                for c in range(2):
                    pool.wait_ge(rc_ok, 2 * t + c + 1)
                    after(pool, pt_ps, 2 * t + c - 1)
                    nc.gpsimd.tensor_tensor(pn[c][:, :, :], ex[c][:, :, :], bc(rc[c][:, :], 2, S), ALU.mult).then_inc(pn_ok, 1)

            def biased(i):
                pool.wait_ge(u1_ok, i + 1)
                after(pool, il_ok, KD * i)
                after(pool, ih_ok, KD * i)
                v4 = lambda ap: ap.rearrange("p k (b s) -> p k b s", b=4)
                nc.gpsimd.tensor_tensor(v4(u2[:, :, :]), v4(u1[:, :, :]), bc(g.ada[:, 1, :, bass.ds(4 * i, 4)], 3, S), ALU.add).then_inc(u2_ok, 1)

            def body(i):
                if not closing(i):
                    biased(i + 1)
                softmax_end(2 * i)
                softmax_end(2 * i + 1)
            if first:
                gather(0)
                for i in range(NBODY):
                    combine(i)
                    if i + 1 < NBODY:
                        gather(i + 1)
            else:
                biased(0)
                bodies(pool, body)

        @block.tensor
        def _(pe):
            def turn(i):
                pe.wait_ge(yt_ok, 2 * i + 2)
                after(pe, v_sb, 2 * (2 * i - 1))
                for a in range(2):
                    for k in range(KD):
                        last = nc.tensor.transpose(b0[:, k * PB + a * P:k * PB + (a + 1) * P], yt[a][:, k * P:(k + 1) * P], g.ident[:, :])
                last.then_inc(x_ps, 1)

            def features(bank, n):
                for m in range(KD):
                    for k in range(KD):
                        last = mm3(nc, bank[:, m * PB:(m + 1) * PB], wh[n][:, k, m * P:(m + 1) * P], wl[n][:, k, m * P:(m + 1) * P],
                                   ih[:, k, :, 0, :], il[:, k, :, 0, :], k == 0, k == KD - 1)
                return last

            def queries_keys(i):
                pe.wait_ge(ih_ok, KD * (i + 1))
                pe.wait_ge(il_ok, KD * (i + 1))
                if not first:
                    after(pe, v_sb, 4 * i)
                    features(b1, 0).then_inc(q_ps, 1)
                    after(pe, o_sb, 2 * i - 2)
                after(pe, k_sb, NK * i)
                features(b2, 0 if first else 1).then_inc(k_ps, 1)

            def values(i, a):
                n = nw - 1
                if a == 1:
                    if first:
                        after(pe, v_sb, 4 * i)
                    else:
                        pe.wait_ge(q_sb, i + 1)
                bank = b1 if a else b0
                for b in range(2):
                    for k in range(KD):
                        last = mm3(nc, bank[:, b * D:(b + 1) * D], ih[:, k, 2 * a + b, :, :].rearrange("p r s -> p (r s)"),
                                   il[:, k, 2 * a + b, :, :].rearrange("p r s -> p (r s)"), wh[n][:, k, :], wl[n][:, k, :], k == 0, k == KD - 1)
                last.then_inc(v_ps, 1)

            def scores(i, a):
                t = 2 * i + a
                q = kT if first else qT
                if a == 0:
                    pe.wait_ge(k_sb, NK * (i + 1)) if first else pe.wait_ge(q_sb, i + 1)
                    pe.wait_ge(kx_dve, n_dve * (i + 1))
                    pe.wait_ge(kx_act, (HC - n_dve) * (i + 1))
                for c in range(2):
                    after(pe, df_ok, 2 * t + c - 1)
                    for b in range(2):
                        tok = slice(a * P + b * S, a * P + (b + 1) * S)
                        last = nc.tensor.matmul(pS[c][b * S:(b + 1) * S, :, :], q[:, c, tok], kx[:, c, :, tok], start=True, stop=True)
                    last.then_inc(s_ps, 1)

            def turn_weights(t):
                for c in range(2):
                    pe.wait_ge(ex_ok if first else pn_ok, 2 * t + c + 1)
                    after(pe, pt_sb, 2 * t + c - 1)
                    w = ex[c] if first else pn[c]
                    for j in range(4):
                        last = nc.tensor.transpose(pT[c][:, j, :], w[:, 2 * j:2 * j + 2, :].rearrange("p h k -> p (h k)"), g.ident[:, :])
                    last.then_inc(pt_ps, 1)

            def results(t, a):
                pe.wait_ge(v_sb, 2 * (t + 1))
                if first:
                    after(pe, ot_ok, 2 * t)
                    for j in range(8):
                        if j % 4 == 0:
                            pe.wait_ge(pt_sb, 2 * t + j // 4 + 1)
                        last = nc.tensor.matmul(pV[:, j * S:(j + 1) * S], pt[j // 4][:, j % 4, :],
                                                vst[a][:, j, :, :, :].rearrange("p b s d -> p (b s d)"), start=True, stop=True)
                    last.then_inc(pv_ps, 1)
                    return
                after(pe, oh_ok, 2 * t)
                after(pe, ol_ok, 2 * t)
                for j in range(8):
                    if j % 4 == 0:
                        pe.wait_ge(pt_sb, 2 * t + j // 4 + 1)
                    last = nc.tensor.matmul(pVf[64 * (j % 2):64 * (j % 2) + 64, j // 2, :, :],
                                            vst[a][:, j, :, :, :].rearrange("p b s d -> p (b s d)"), pt[j // 4][:, j % 4, :], start=True, stop=True)
                last.then_inc(pv_ps, 1)

            def output(t, i):
                if first:
                    return
                after(pe, o_sb, t)
                pe.wait_ge(k_sb, NK * (i + 1))
                pe.wait_ge(oh_ok, 2 * t + 2)
                pe.wait_ge(ol_ok, 2 * t + 2)
                for j in range(4):
                    last = mm3(nc, b2[:, 0:D], oh[:, j, :, :].rearrange("p b s -> p (b s)"), ol[:, j, :, :].rearrange("p b s -> p (b s)"),
                               woh[:, j, :], wol[:, j, :], j == 0, j == 3)
                last.then_inc(o_ps, 1)

            def body(i):
                values(i, 0)
                if not opening(i):
                    turn_weights(2 * i - 1)
                    output(2 * i - 2, i)
                scores(i, 0)
                if not opening(i):
                    results(2 * i - 1, 1)
                if not closing(i):
                    turn(i + 1)
                values(i, 1)
                scores(i, 1)
                if not opening(i):
                    output(2 * i - 1, i)
                turn_weights(2 * i)
                if not closing(i):
                    queries_keys(i + 1)
                results(2 * i, 0)
            turn(0)
            pe.wait_ge(wh_ok, 1 if first else 2)
            pe.wait_ge(wl_ok, 1 if first else 2)
            queries_keys(0)
            pe.wait_ge(wh_ok, nw if first else nw + 1)
            pe.wait_ge(wl_ok, nw if first else nw + 1)
            pe.wait_ge(vz_ok, 2)
            bodies(pe, body)
            turn_weights(TT - 1)
            output(TT - 2, NBODY - 1)
            results(TT - 1, 1)
            output(TT - 1, NBODY - 1)

        @block.scalar
        def _(act):
            def weight_high(n):
                if n < nw:
                    nc.scalar.activation(wh[n][:, :, :], w_raw[n], ACT.Copy).then_inc(wh_ok, 1)
                elif not first:
                    nc.scalar.activation(woh[:, :, :], wo_raw, ACT.Copy).then_inc(wh_ok, 1)

            def scaled(i):
                for a in range(2):
                    after(act, x_ps, i)
                    nc.scalar.activation(yt[a][:, :], res[:, bass.ds(2 * i + a, 1), :].rearrange("p o n -> p (o n)"), ACT.Copy,
                                         scale=g.inv1[:, bass.ds(2 * i + a, 1)]).then_inc(yt_ok, 1)

            def weighted(i):
                for a in range(2):
                    t = 2 * i + a
                    after(act, yt_ok, t - 1)
                    for c in range(2):
                        act.wait_ge(gat_in[c][a], 16 * i + 16)
                        nc.scalar.activation(ya[c][a][:, :], gat[c][a][:, :], ACT.Copy, scale=g.weight[c][:, bass.ds(t, 1)]).then_inc(ya_ok, 1)

            def high(i):
                act.wait_ge(x_ps if first else u2_ok, i + 1)
                after(act, v_ps, 2 * i)
                src = (b0[:, :] if first else u2[:, :, :].rearrange("p k n -> p (k n)")).rearrange("p (k b s) -> p k b s", k=KD, b=4)
                for k in range(KD):
                    last = nc.scalar.activation(ih[:, k, :, :, :], bc(src[:, k, :, :], 2, 2), ACT.Copy)
                    last.then_inc(ih_ok, 1)

            def keys(i):
                if not first:
                    act.wait_ge(q_ps, i + 1)
                    after(act, s_ps, 4 * i)
                    nc.scalar.activation(qT[:, :, :], b1[:, :].rearrange("p (k n) -> p k n", k=KD), ACT.Copy).then_inc(q_sb, 1)
                act.wait_ge(k_ps, i + 1)
                after(act, s_ps, 4 * i)
                after(act, kx_dve, n_dve * i)
                if first:
                    for m in range(KD):
                        last = nc.scalar.activation(kT[:, m, :], b2[:, m * PB:(m + 1) * PB], ACT.Identity, bias=g.cols[:, COL_BV1, m:m + 1])
                        last.then_inc(k_sb, 1)
                else:
                    nc.scalar.activation(kT[:, :, :], b2[:, :].rearrange("p (k n) -> p k n", k=KD), ACT.Copy).then_inc(k_sb, 1)

            def masked_keys(i):
                act.wait_ge(k_sb, NK * (i + 1))
                for h in range(n_dve, HC):
                    nc.scalar.activation(kx[:, :, h, :], kT[:, :, :], ACT.Copy, scale=g.headmask[:, h:h + 1]).then_inc(kx_act, 1)

            def exps(t, c):
                act.wait_ge(df_ok, 2 * t + c + 1)
                after(act, pt_ps if first else pn_ok, 2 * t + c - 1)
                nc.scalar.activation(ex[c][:, :, :], df[c][:, :, :], ACT.Exp, scale=SCALE).then_inc(ex_ok, 1)

            def values(i, a):
                if first:
                    return
                t = 2 * i + a
                act.wait_ge(v_ps, t + 1)
                after(act, pv_ps, t - 1)
                for h in range(2):
                    r = slice(64 * h, 64 * h + 64)
                    nc.scalar.activation(vst[a][r, :, :, h, :].rearrange("p j b d -> p b j d"),
                                         (b1 if a else b0)[r, :].rearrange("p (b j s d) -> p b j s d", b=2, j=8, s=2)[:, :, :, h, :],
                                         ACT.Copy).then_inc(v_sb, 1)

            def weights(t):
                for c in range(2):
                    act.wait_ge(pt_ps, 2 * t + c + 1)
                    after(act, pv_ps, t)
                    nc.scalar.activation(pt[c][:, :, :], pT[c][:, :, :], ACT.Copy).then_inc(pt_sb, 1)

            def results(t, a):
                if first:
                    return
                act.wait_ge(pv_ps, t + 1)
                after(act, o_ps, t)
                for b in range(2):
                    nc.scalar.activation(oh[:, :, b, :], pVf[:, :, b, :], ACT.Copy, scale=g.batchmask[:, b:b + 1]).then_inc(oh_ok, 1)

            def squares(t, a):
                if first:
                    return
                act.wait_ge(o_sb, t + 1)
                after(act, sq_ok, t - 1)
                nc.scalar.activation(junk[a][:, :], out[:, bass.ds(t, 1), :].rearrange("p o n -> p (o n)"), ACT.Square,
                                     accum_out=ssq[:, bass.ds(t, 1)]).then_inc(sq_ok, 1)

            def body(i):
                keys(i)
                if not opening(i):
                    results(2 * i - 2, 0)
                masked_keys(i)
                if not opening(i):
                    weights(2 * i - 1)
                values(i, 0)
                if not closing(i):
                    weighted(i + 1) if first else scaled(i + 1)
                if not opening(i):
                    squares(2 * i - 2, 0)
                exps(2 * i, 0)
                if not opening(i):
                    results(2 * i - 1, 1)
                exps(2 * i, 1)
                values(i, 1)
                if not closing(i):
                    high(i + 1)
                weights(2 * i)
                exps(2 * i + 1, 0)
                exps(2 * i + 1, 1)
                if not opening(i):
                    squares(2 * i - 1, 1)
            if first:
                weight_high(0)
                weighted(0)
                high(0)
            else:
                scaled(0)
                weight_high(0)
                weight_high(1)
                high(0)
                weight_high(2)
                weight_high(3)
            bodies(act, body)
            results(TT - 2, 0)
            weights(TT - 1)
            results(TT - 1, 1)
            squares(TT - 2, 0)
            squares(TT - 1, 1)

        @block.vector
        def _(dve):
            v = nc.vector

            def weight_low(n):
                dve.wait_ge(wh_ok, n + 1)
                if n < nw:
                    v.tensor_tensor(wl[n][:, :, :], w_raw[n], f32(wh[n][:, :, :]), ALU.subtract).then_inc(wl_ok, 1)
                else:
                    v.tensor_tensor(wol[:, :, :], wo_raw, f32(woh[:, :, :]), ALU.subtract).then_inc(wl_ok, 1)

            def adapt(i):
                dve.wait_ge(x_ps, i + 1)
                after(dve, u2_ok, i)
                v4 = lambda ap: ap.rearrange("p k (b s) -> p k b s", b=4)
                v.tensor_tensor(v4(u1[:, :, :]), b0[:, :].rearrange("p (k b s) -> p k b s", k=KD, b=4), bc(g.ada[:, 0, :, bass.ds(4 * i, 4)], 3, S), ALU.mult).then_inc(u1_ok, 1)

            def low(i):
                src = (b0[:, :] if first else u2[:, :, :].rearrange("p k n -> p (k n)")).rearrange("p (k b s) -> p k b s", k=KD, b=4)
                dve.wait_ge(ih_ok, KD * (i + 1))
                for k in range(KD):
                    last = v.tensor_tensor(il[:, k, :, :, :], bc(src[:, k, :, :], 2, 2), f32(ih[:, k, :, :, :]), ALU.subtract)
                    last.then_inc(il_ok, 1)

            def masked_keys(i):
                dve.wait_ge(k_sb, NK * (i + 1))
                after(dve, s_ps, 4 * i)
                for h in range(n_dve):
                    v.tensor_scalar(kx[:, :, h, :], kT[:, :, :], g.headmask[:, h:h + 1], None, ALU.mult).then_inc(kx_dve, 1)

            def values(i, a):
                if not first:
                    return
                t = 2 * i + a
                dve.wait_ge(v_ps, t + 1)
                after(dve, pv_ps, t - 1)
                for h in range(2):
                    r = slice(64 * h, 64 * h + 64)
                    v.tensor_tensor(vst[a][r, :, :, h, :].rearrange("p j b d -> p b j d"),
                                    (b1 if a else b0)[r, :].rearrange("p (b j s d) -> p b j s d", b=2, j=8, s=2)[:, :, :, h, :],
                                    bc(g.rows[r, ROW_BV1, :].rearrange("p (j s d) -> p j s d", j=8, s=2)[:, :, h, :], 1, 2), ALU.add).then_inc(v_sb, 1)

            def softmax(t):
                for c in range(2):
                    n = 2 * t + c
                    dve.wait_ge(s_ps, n + 1)
                    after(dve, df_ok, n - 1)
                    v.tensor_reduce(mx[c][:, :], pS[c][:, :, :], AX_X, ALU.max).then_inc(mx_ok, 1)
                    dve.wait_ge(mx_ok, n + 1)
                    after(dve, ex_ok, n - 1)
                    v.tensor_tensor(df[c][:, :, :], pS[c][:, :, :], bc(mx[c][:, :], 2, S), ALU.subtract).then_inc(df_ok, 1)

            def sums(t, a):
                for c in range(2):
                    n = 2 * t + c
                    dve.wait_ge(ex_ok, n + 1)
                    after(dve, rc_ok, n - 1)
                    v.tensor_reduce(sm[c][:, :], ex[c][:, :, :], AX_X, ALU.add).then_inc(sm_ok, 1)
                    dve.wait_ge(sm_ok, n + 1)
                    if first:
                        after(dve, ot_ok, 2 * t - 2)
                        v.reciprocal(rch[a][:, 4 * c:4 * c + 4, :], sm[c][:, :].rearrange("p (j s) -> p j s", s=2)).then_inc(rc_ok, 1)
                    else:
                        after(dve, pn_ok, n - 1)
                        v.reciprocal(rc[c][:, :], sm[c][:, :]).then_inc(rc_ok, 1)

            def results(t, a):
                if first:
                    dve.wait_ge(pv_ps, t + 1)
                    dve.wait_ge(rc_ok, 2 * t + 2)
                    if not (isinstance(t, int) and t < 2):
                        dve.wait_ge(o_out[a], 16 * (t - a))
                    for b in range(2):
                        r = slice(b * S, (b + 1) * S)
                        v.tensor_tensor(otm[a][r, :, :, :], pVt[r, :, b, :].rearrange("p j (s d) -> p j s d", s=2),
                                        bc(rch[a][r, :, :], 3, DH), ALU.mult).then_inc(ot_ok, 1)
                    return
                dve.wait_ge(oh_ok, 2 * t + 2)
                for b in range(2):
                    v.scalar_tensor_tensor(ol[:, :, b, :], pVf[:, :, b, :], g.batchmask[:, b:b + 1], f32(oh[:, :, b, :]),
                                           ALU.mult, ALU.subtract).then_inc(ol_ok, 1)

            def output(t):
                if first:
                    return
                dve.wait_ge(o_ps, t + 1)
                r = res[:, bass.ds(t, 1), :].rearrange("p o n -> p (o n)")
                v.tensor_tensor(out[:, bass.ds(t, 1), :].rearrange("p o n -> p (o n)"), b2[:, 0:D], r, ALU.add).then_inc(o_sb, 1)

            def body(i):
                masked_keys(i)
                if not opening(i):
                    results(2 * i - 2, 0)
                values(i, 0)
                if not opening(i):
                    output(2 * i - 2)
                softmax(2 * i)
                if not first and not closing(i):
                    adapt(i + 1)
                sums(2 * i, 0)
                if not opening(i):
                    results(2 * i - 1, 1)
                values(i, 1)
                if not closing(i):
                    low(i + 1)
                softmax(2 * i + 1)
                if not opening(i):
                    output(2 * i - 1)
                sums(2 * i + 1, 1)
            weight_low(0)
            if not first:
                weight_low(1)
                adapt(0)
            low(0)
            if not first:
                weight_low(2)
                weight_low(3)
            dve.wait_ge(vz_ok, 2)
            bodies(dve, body)
            results(TT - 2, 0)
            output(TT - 2)
            results(TT - 1, 1)
            output(TT - 1)


def project_first(nc, g, dr):
    with ExitStack() as ctx:
        sb, ps, sem = scope(nc, ctx, "proj")
        wh = sb("wh", [P, KD, D], F32R)
        wl = sb("wl", [P, KD, D], F32R)
        rows = [sb(f"rows{a}", [P, 2, D]) for a in range(2)]
        oh = [sb(f"oh{a}", [P, KD, PB], F32R) for a in range(2)]
        ol = [sb(f"ol{a}", [P, KD, PB], F32R) for a in range(2)]
        xb = [sb(f"xb{a}", [P, 2, D]) for a in range(2)]
        junk = [sb(f"junk{a}", [P, D]) for a in range(2)]
        ss = sb("ss", [P, TT])
        ms = sb("ms", [P, TT])
        rv = sb("rv", [P, TT])
        condT = sb("condT", [DC, NB])
        adaw = sb("adaw", [DC, 4, D])
        adab = sb("adab", [P, 4, KD])
        pX = [ps(f"pX{a}", [P, KD, PB]) for a in range(2)]
        pO = [ps(f"pO{a}", [P, 2, D]) for a in range(2)]
        pA = ps("pA", [P, 4, KD, NB])
        wh_ok, wl_ok, x_ps, oh_ok, ol_ok, xb_ok, o_ps, o_sb, sq_ok = (
            sem(n) for n in ("wh_ok", "wl_ok", "x_ps", "oh_ok", "ol_ok", "xb_ok", "o_ps", "o_sb", "sq_ok"))
        ada_in, ada_ps, ada_sb, ms_ok, rv_ok, inv_ok = (sem(n) for n in ("ada_in", "ada_ps", "ada_sb", "ms_ok", "rv_ok", "inv_ok"))
        rows_in = [sem(f"rows_in{a}") for a in range(2)]
        block = ctx.enter_context(nc.Block())
        heads = dr.heads.rearrange("(n b) h (i l) d -> n (b h i) (l d)", b=4, l=S // 4)

        def pairs(eng, body):
            body(0, 0)
            body(1, 1)
            with eng.Fori(1, NBODY // 2) as p:
                body(2 * p, 0)
                body(2 * p + 1, 1)

        def again(i):
            return not (isinstance(i, int) and i < 2)

        def tiles(t, i):
            return t[:, bass.ds(2 * i, 2), :]

        @block.sync
        def _(sp):
            sp.dma_start(condT[:, :], dr.condT).then_inc(ada_in, 16)
            sp.dma_start(adaw[:, :, :], dr.adaw).then_inc(ada_in, 16)
            sp.dma_start(adab[:, :, :], dr.adab).then_inc(ada_in, 16)

            def body(i, a):
                if again(i):
                    sp.wait_ge(x_ps, i - 1)
                sp.dma_start(rows[a][:, :, :], heads[bass.ds(i, 1)].rearrange("o (s p) c -> p (o s) c", p=P)).then_inc(rows_in[a], 16)
            pairs(sp, body)

        @block.gpsimd
        def _(pool):
            def body(i, a):
                if again(i):
                    pool.wait_ge(o_sb, i - 1)
                nc.gpsimd.tensor_tensor(xb[a][:, :, :], tiles(g.x, i), bc(g.rows[:, ROW_BO1, :], 1, 2), ALU.add).then_inc(xb_ok, 1)
            pairs(pool, body)

        @block.tensor
        def _(pe):
            def turn(i, a):
                pe.wait_ge(rows_in[a], 8 * (i - a) + 16)
                if again(i):
                    pe.wait_ge(oh_ok, i - 1)
                    pe.wait_ge(ol_ok, i - 1)
                for s in range(2):
                    for k in range(KD):
                        last = nc.tensor.transpose(pX[a][:, k, s * P:(s + 1) * P], rows[a][:, s, k * P:(k + 1) * P], g.ident[:, :])
                last.then_inc(x_ps, 1)

            def product(i, a):
                pe.wait_ge(oh_ok, i + 1)
                pe.wait_ge(ol_ok, i + 1)
                if again(i):
                    pe.wait_ge(o_sb, i - 1)
                for s in range(2):
                    for k in range(KD):
                        last = mm3(nc, pO[a][:, s, :], oh[a][:, k, s * P:(s + 1) * P], ol[a][:, k, s * P:(s + 1) * P],
                                   wh[:, k, :], wl[:, k, :], k == 0, k == KD - 1)
                last.then_inc(o_ps, 1)
            turn(0, 0)
            pe.wait_ge(wh_ok, 1)
            pe.wait_ge(wl_ok, 1)
            turn(1, 1)
            pe.wait_ge(ada_in, 48)
            for n in range(4):
                for k in range(KD):
                    last = nc.tensor.matmul(pA[:, n, k, :], adaw[:, n, k * P:(k + 1) * P], condT[:, :], start=True, stop=True)
            last.then_inc(ada_ps, 1)

            product(0, 0)
            with pe.Fori(1, NBODY // 2) as p:
                turn(2 * p, 0)
                product(2 * p - 1, 1)
                turn(2 * p + 1, 1)
                product(2 * p, 0)
            product(NBODY - 1, 1)

        @block.scalar
        def _(act):
            nc.scalar.activation(wh[:, :, :], g.w_o1, ACT.Copy).then_inc(wh_ok, 1)

            def body(i, a):
                act.wait_ge(x_ps, i + 1)
                if again(i):
                    act.wait_ge(o_ps, i - 1)
                nc.scalar.activation(oh[a][:, :, :], pX[a][:, :, :], ACT.Copy).then_inc(oh_ok, 1)

            def squares(i):
                act.wait_ge(o_sb, i + 1)
                for s in range(2):
                    if not (isinstance(i, int) and i < 1):
                        act.wait_ge(sq_ok, 2 * i + s - 1)
                    nc.scalar.activation(junk[s][:, :], g.x1[:, bass.ds(2 * i + s, 1), :].rearrange("p o n -> p (o n)"), ACT.Square,
                                         accum_out=ss[:, bass.ds(2 * i + s, 1)]).then_inc(sq_ok, 1)
            for i in range(4):
                body(i, i % 2)
                if i >= 2:
                    squares(i - 2)
            with act.Fori(2, NBODY // 2) as p:
                body(2 * p, 0)
                squares(2 * p - 2)
                body(2 * p + 1, 1)
                squares(2 * p - 1)
            squares(NBODY - 2)
            squares(NBODY - 1)
            act.wait_ge(rv_ok, 1)
            nc.scalar.activation(g.inv1[:, :], rv[:, :], ACT.Sqrt).then_inc(inv_ok, 1)

        @block.vector
        def _(dve):
            v = nc.vector
            dve.wait_ge(wh_ok, 1)
            v.tensor_tensor(wl[:, :, :], g.w_o1, f32(wh[:, :, :]), ALU.subtract).then_inc(wl_ok, 1)

            def low(i, a):
                dve.wait_ge(oh_ok, i + 1)
                v.tensor_tensor(ol[a][:, :, :], pX[a][:, :, :], f32(oh[a][:, :, :]), ALU.subtract).then_inc(ol_ok, 1)

            def result(i, a):
                dve.wait_ge(o_ps, i + 1)
                dve.wait_ge(xb_ok, i + 1)
                v.tensor_tensor(tiles(g.x1, i), pO[a][:, :, :], xb[a][:, :, :], ALU.add).then_inc(o_sb, 1)
            low(0, 0)
            low(1, 1)
            dve.wait_ge(ada_ps, 1)
            v.tensor_tensor(g.ada[:, :, :, :], pA[:, :, :, :], bc(adab[:, :, :], 3, NB), ALU.add).then_inc(ada_sb, 1)
            result(0, 0)
            with dve.Fori(1, NBODY // 2) as p:
                low(2 * p, 0)
                result(2 * p - 1, 1)
                low(2 * p + 1, 1)
                result(2 * p, 0)
            result(NBODY - 1, 1)
            dve.wait_ge(sq_ok, TT)
            v.tensor_scalar(ms[:, :], ss[:, :], 1.0 / D, EPS, ALU.mult, ALU.add).then_inc(ms_ok, 1)
            dve.wait_ge(ms_ok, 1)
            v.reciprocal(rv[:, :], ms[:, :]).then_inc(rv_ok, 1)


KF = FH // P
MP = KF // 2


def swiglu(nc, g, dr):
    with ExitStack() as ctx:
        sb, ps, sem = scope(nc, ctx, "ffn")
        wh = [sb(f"wh{n}", [P, KD * FH], F32R) for n in range(3)]
        wl = [sb(f"wl{n}", [P, KD * FH], F32R) for n in range(3)]
        ms = sb("ms", [P, TT])
        rv = sb("rv", [P, TT])
        inv = sb("inv", [P, TT])
        yt = [sb(f"yt{a}", [P, D]) for a in range(2)]
        u1 = sb("u1", [P, KD, 4, S])
        u2 = sb("u2", [P, KD, 4, S])
        ih = [sb(f"ih{a}", [P, KD, PB], F32R) for a in range(2)]
        il = [sb(f"il{a}", [P, KD, PB], F32R) for a in range(2)]
        sg = [sb(f"sg{r}", [P, 2, PB]) for r in range(2)]
        hf = [sb(f"hf{r}", [P, 2, PB]) for r in range(2)]
        hh = [sb(f"hh{r}", [P, 2, PB], F32R) for r in range(2)]
        hl = [sb(f"hl{r}", [P, 2, PB], F32R) for r in range(2)]
        pX = ps("pX", [P, KD, PB])
        pG = [ps(f"pG{r}", [P, 2, PB]) for r in range(2)]
        pH = [ps(f"pH{r}", [P, 2, PB]) for r in range(2)]
        pO = ps("pO", [P, 2, D])
        wh_ok, wl_ok, ms_ok, rv_ok, inv_ok, yt_ok, x_ps, u1_ok, u2_ok, ih_ok, il_ok = (
            sem(n) for n in ("wh_ok", "wl_ok", "ms_ok", "rv_ok", "inv_ok", "yt_ok", "x_ps", "u1_ok", "u2_ok", "ih_ok", "il_ok"))
        g_ps, h_ps, sg_ok, hf_ok, hh_ok, hl_ok, op_ps, o_sb = (
            sem(n) for n in ("g_ps", "h_ps", "sg_ok", "hf_ok", "hh_ok", "hl_ok", "op_ps", "o_sb"))
        block = ctx.enter_context(nc.Block())

        def after(eng, semaphore, value):
            if not (isinstance(value, int) and value <= 0):
                eng.wait_ge(semaphore, value)

        def pairs(eng, body):
            body(0, 0)
            body(1, 1)
            with eng.Fori(1, NBODY // 2 - 1) as p:
                body(2 * p, 0)
                body(2 * p + 1, 1)
            body(NBODY - 2, 0)
            body(NBODY - 1, 1)

        def closing(i):
            return isinstance(i, int) and i == NBODY - 1

        @block.tensor
        def _(pe):
            w_h = [wh[n][:, :].rearrange("p (k m) -> p k m", k=KF if n == 2 else KD) for n in range(3)]
            w_l = [wl[n][:, :].rearrange("p (k m) -> p k m", k=KF if n == 2 else KD) for n in range(3)]

            def turn(i):
                pe.wait_ge(yt_ok, 2 * i + 2)
                after(pe, u1_ok, i)
                for a in range(2):
                    for k in range(KD):
                        last = nc.tensor.transpose(pX[:, k, a * P:(a + 1) * P], yt[a][:, k * P:(k + 1) * P], g.ident[:, :])
                last.then_inc(x_ps, 1)

            def pair(i, j, a):
                n = MP * i + j
                if j == 0:
                    pe.wait_ge(ih_ok, i + 1)
                    pe.wait_ge(il_ok, i + 1)
                for w, bank, left, done in ((0, pG, sg_ok, g_ps), (1, pH, hf_ok, h_ps)):
                    if isinstance(i, int) and i == 0 and j < 2:
                        pe.wait_ge(wh_ok, w + 1)
                        pe.wait_ge(wl_ok, w + 1)
                    else:
                        pe.wait_ge(left, n - 1)
                    for m in range(2):
                        for k in range(KD):
                            c = slice((2 * j + m) * P, (2 * j + m + 1) * P)
                            last = mm3(nc, bank[j % 2][:, m, :], w_h[w][:, k, c], w_l[w][:, k, c], ih[a][:, k, :], il[a][:, k, :],
                                       k == 0, k == KD - 1)
                    last.then_inc(done, 1)

            def output(i, j):
                n = MP * i + j
                if isinstance(i, int) and i == 0 and j == 0:
                    pe.wait_ge(wh_ok, 3)
                    pe.wait_ge(wl_ok, 3)
                pe.wait_ge(hh_ok, n + 1)
                pe.wait_ge(hl_ok, n + 1)
                if j == 0:
                    after(pe, o_sb, i)
                for s in range(2):
                    for m in range(2):
                        c = slice(s * P, (s + 1) * P)
                        first = j == 0 and s == 0 and m == 0
                        nc.tensor.matmul(pO[:, s, :], hh[j % 2][:, m, c], w_h[2][:, 2 * j + m, :], start=first, stop=False, skip_group_check=True)
                        nc.tensor.matmul(pO[:, s, :], hl[j % 2][:, m, c], w_h[2][:, 2 * j + m, :], start=False, stop=False, skip_group_check=True)
                        last = nc.tensor.matmul(pO[:, s, :], hh[j % 2][:, m, c], w_l[2][:, 2 * j + m, :], start=False,
                                                stop=j == MP - 1 and m == 1, skip_group_check=True)
                last.then_inc(op_ps, 1)

            def body(i, a):
                pair(i, 0, a)
                if not (isinstance(i, int) and i == 0):
                    output(i - 1, MP - 1)
                if not closing(i):
                    turn(i + 1)
                for j in range(1, MP):
                    pair(i, j, a)
                    output(i, j - 1)
            turn(0)
            pairs(pe, body)
            output(NBODY - 1, MP - 1)

        @block.scalar
        def _(act):
            def scaled(i):
                for a in range(2):
                    after(act, x_ps, i)
                    nc.scalar.activation(yt[a][:, :], g.x[:, bass.ds(2 * i + a, 1), :].rearrange("p o n -> p (o n)"), ACT.Copy,
                                         scale=inv[:, bass.ds(2 * i + a, 1)]).then_inc(yt_ok, 1)

            def high(i, a):
                act.wait_ge(u2_ok, i + 1)
                after(act, h_ps, MP * (i - 1))
                nc.scalar.activation(ih[a][:, :, :], u2[:, :, :, :].rearrange("p k b s -> p k (b s)"), ACT.Copy).then_inc(ih_ok, 1)

            def silu(i, j):
                n = MP * i + j
                act.wait_ge(g_ps, n + 1)
                if not (isinstance(i, int) and i == 0 and j < 2):
                    act.wait_ge(hf_ok, n - 1)
                nc.scalar.activation(sg[j % 2][:, :, :], pG[j % 2][:, :, :], ACT.Silu).then_inc(sg_ok, 1)

            def hidden_high(i, j):
                n = MP * i + j
                act.wait_ge(hf_ok, n + 1)
                if not (isinstance(i, int) and i == 0 and j < 2):
                    act.wait_ge(op_ps, n - 1)
                nc.scalar.activation(hh[j % 2][:, :, :], hf[j % 2][:, :, :], ACT.Copy).then_inc(hh_ok, 1)

            def body(i, a):
                for j in range(MP):
                    silu(i, j)
                    hidden_high(i, j)
                    if not closing(i) and j == 1:
                        high(i + 1, 1 - a)
                    if not closing(i) and j == 2:
                        if not (isinstance(i, int) and i == NBODY - 2):
                            scaled(i + 2)
            act.wait_ge(rv_ok, 1)
            nc.scalar.activation(inv[:, :], rv[:, :], ACT.Sqrt).then_inc(inv_ok, 1)
            act.wait_ge(inv_ok, 1)
            scaled(0)
            scaled(1)
            for n in range(3):
                nc.scalar.activation(wh[n][:, :], g.w_ff[:, n, :], ACT.Copy).then_inc(wh_ok, 1)
                if n == 0:
                    high(0, 0)
            pairs(act, body)

        @block.vector
        def _(dve):
            v = nc.vector

            def adapt(i):
                dve.wait_ge(x_ps, i + 1)
                after(dve, u2_ok, i)
                v.tensor_tensor(u1[:, :, :, :], pX[:, :, :].rearrange("p k (b s) -> p k b s", b=4),
                                bc(g.ada[:, 2, :, bass.ds(4 * i, 4)], 3, S), ALU.mult).then_inc(u1_ok, 1)
                dve.wait_ge(u1_ok, i + 1)
                after(dve, ih_ok, i)
                after(dve, il_ok, i)
                v.tensor_tensor(u2[:, :, :, :], u1[:, :, :, :], bc(g.ada[:, 3, :, bass.ds(4 * i, 4)], 3, S), ALU.add).then_inc(u2_ok, 1)

            def low(i, a):
                dve.wait_ge(ih_ok, i + 1)
                v.tensor_tensor(il[a][:, :, :], u2[:, :, :, :].rearrange("p k b s -> p k (b s)"), f32(ih[a][:, :, :]), ALU.subtract).then_inc(il_ok, 1)

            def gated(i, j):
                n = MP * i + j
                dve.wait_ge(sg_ok, n + 1)
                dve.wait_ge(h_ps, n + 1)
                if not (isinstance(i, int) and i == 0 and j < 2):
                    dve.wait_ge(hl_ok, n - 1)
                v.tensor_tensor(hf[j % 2][:, :, :], pH[j % 2][:, :, :], sg[j % 2][:, :, :], ALU.mult).then_inc(hf_ok, 1)
                dve.wait_ge(hh_ok, n + 1)
                v.tensor_tensor(hl[j % 2][:, :, :], hf[j % 2][:, :, :], f32(hh[j % 2][:, :, :]), ALU.subtract).then_inc(hl_ok, 1)

            def result(i):
                dve.wait_ge(op_ps, MP * i + MP)
                x2 = g.x[:, bass.ds(2 * i, 2), :]
                v.tensor_tensor(x2, pO[:, :, :], x2, ALU.add).then_inc(o_sb, 1)

            def body(i, a):
                gated(i, 0)
                if not (isinstance(i, int) and i == 0):
                    result(i - 1)
                if not closing(i):
                    adapt(i + 1)
                gated(i, 1)
                gated(i, 2)
                if not closing(i):
                    low(i + 1, 1 - a)
                gated(i, 3)
            v.tensor_scalar(ms[:, :], g.ss2[:, :], 1.0 / D, EPS, ALU.mult, ALU.add).then_inc(ms_ok, 1)
            dve.wait_ge(ms_ok, 1)
            v.reciprocal(rv[:, :], ms[:, :]).then_inc(rv_ok, 1)
            adapt(0)
            for n in range(3):
                dve.wait_ge(wh_ok, n + 1)
                v.tensor_tensor(wl[n][:, :], g.w_ff[:, n, :], f32(wh[n][:, :]), ALU.subtract).then_inc(wl_ok, 1)
                if n == 0:
                    low(0, 0)
            pairs(dve, body)
            result(NBODY - 1)


NRING = 4
HS = HC * NS
NJ = FH // P
W2_AT = 2 * KD * FH
W_SLOT = W2_AT + NJ * D


def load_up(eng, g, dr, e, buffer, done):
    eng.dma_start(buffer[:, 0:W2_AT], dr.w_slot[bass.ds(e, 1), :, 0:W2_AT].rearrange("o p n -> p (o n)")).then_inc(done, 16)


def load_down(eng, g, dr, e, buffer, done):
    eng.dma_start(buffer[:, W2_AT:W_SLOT], dr.w_slot[bass.ds(e, 1), :, W2_AT:W_SLOT].rearrange("o p n -> p (o n)")).then_inc(done, 16)


def slots(nc, g, dr):
    with ExitStack() as ctx:
        sb, ps, sem = scope(nc, ctx, "slots")
        raw = [g.w_small[:, w] for w in (W_DK, W_CQ, W_DV)]
        wh = [sb(f"wh{n}", [P, KD, D], F32R) for n in range(3)]
        wl = [sb(f"wl{n}", [P, KD, D], F32R) for n in range(3)]
        slotT = sb("slotT", [P, KD, NS])
        sq = sb("sq", [P, KD, NS])
        sx = sb("sx", [P, KD, HC, NS])
        xt = sb("xt", [P, 2, D])
        xh = sb("xh", [P, KD, PB], F32R)
        xl = sb("xl", [P, KD, PB], F32R)
        kT = sb("kT", [P, KD, PB])
        qT = sb("qT", [P, KD, PB])
        vt = sb("vt", [P, 2, D])
        mx = sb("mx", [P, KD, 4])
        df = sb("df", [P, KD, 4, S])
        ex = sb("ex", [P, KD, 4, S])
        sm = sb("sm", [P, KD, 4])
        rc = sb("rc", [P, KD, 4])
        pn = sb("pn", [P, KD, 4, S])
        pt = sb("pt", [P, KD, 2, HS])
        own = [sb(f"own{b}", [P, 4, NS, HC]) for b in range(2)]
        pX = ps("pX", [P, KD, PB])
        pK = ps("pK", [P, KD, PB])
        pQ = ps("pQ", [P, KD, PB])
        pVt = ps("pVt", [P, 2, D])
        pS = ps("pS", [P, KD, 4, S])
        pT = ps("pT", [P, KD, 2, HS])
        pU = [ps(f"pU{b}", [P, 2, KD, HC, NS]) for b in range(2)]
        wh_ok, wl_ok, sl_in, sq_ps, sq_ok, sx_ok = (sem(n) for n in ("wh_ok", "wl_ok", "sl_in", "sq_ps", "sq_ok", "sx_ok"))
        x_in, x_ps, xh_ok, xl_ok, k_ps, k_sb, q_ps, q_sb, q_out, v_ps, v_sb = (
            sem(n) for n in ("x_in", "x_ps", "xh_ok", "xl_ok", "k_ps", "k_sb", "q_ps", "q_sb", "q_out", "v_ps", "v_sb"))
        s_ps, mx_ok, df_ok, ex_ok, sm_ok, rc_ok, pn_ok, pt_ps, pt_sb, u_ps, own_ok, ot_ok = (
            sem(n) for n in ("s_ps", "mx_ok", "df_ok", "ex_ok", "sm_ok", "rc_ok", "pn_ok", "pt_ps", "pt_sb", "u_ps", "own_ok", "ot_ok"))
        block = ctx.enter_context(nc.Block())

        def after(eng, semaphore, value):
            if not (isinstance(value, int) and value <= 0):
                eng.wait_ge(semaphore, value)

        def first_body(i):
            return isinstance(i, int) and i == 0

        def bodies(eng, body):
            body(0)
            body(1)
            with eng.Fori(2, NBODY - 1) as i:
                body(i)
            body(NBODY - 1)

        @block.sync
        def _(sp):
            def load(i):
                after(sp, x_ps, i)
                sp.dma_start(xt[:, :, :], g.x[:, bass.ds(2 * i, 2), :]).then_inc(x_in, 16)

            def store(i):
                sp.wait_ge(q_sb, KD * (i + 1))
                sp.dma_start(dr.q[bass.ds(i, 1)].rearrange("o p k n -> p (o k) n"), qT[:, :, :]).then_inc(q_out, 16)
            load(0)
            sp.dma_start(slotT[:, :, :], dr.slotT).then_inc(sl_in, 16)
            for source, target in ((dr.slot_tm, g.slot_tm[:, :]), (dr.ln, g.ln[:, :, :]), (dr.eb, g.eb[:, :, :]),
                                   (dr.b2, g.b2[:, :, :]), (dr.stack, g.stack[:, :])):
                sp.dma_start(target, source).then_inc(g.ffn_in, 16)
            for i in range(NRING):
                load(i + 1)
                load_up(sp, g, dr, i, g.ring[i], g.up_in[i])
                load_down(sp, g, dr, i, g.ring[i], g.down_in[i])
                store(i)
            with sp.Fori(NRING, NBODY - 1) as i:
                load(i + 1)
                store(i)
            store(NBODY - 1)
            sp.wait_ge(q_out, 16 * NBODY)
            sp.wait_ge(g.ffn_in, 16 * 5)

        @block.tensor
        def _(pe):
            def turn(i):
                pe.wait_ge(x_in, 16 * (i + 1))
                for a in range(2):
                    for k in range(KD):
                        last = nc.tensor.transpose(pX[:, k, a * P:(a + 1) * P], xt[:, a, k * P:(k + 1) * P], g.ident[:, :])
                last.then_inc(x_ps, 1)

            def feature_major(bank, n):
                for m in range(KD):
                    c = slice(m * P, (m + 1) * P)
                    for k in range(KD):
                        last = mm3(nc, bank[:, m, :], wh[n][:, k, c], wl[n][:, k, c], xh[:, k, :], xl[:, k, :], k == 0, k == KD - 1)
                return last

            def body(i):
                pe.wait_ge(xh_ok, i + 1)
                pe.wait_ge(xl_ok, i + 1)
                after(pe, k_sb, KD * i)
                feature_major(pK, 0).then_inc(k_ps, 1)
                after(pe, q_sb, KD * i)
                feature_major(pQ, 1).then_inc(q_ps, 1)
                if not first_body(i):
                    end_turn(i - 1)
                after(pe, v_sb, i)
                for a in range(2):
                    c = slice(a * P, (a + 1) * P)
                    for k in range(KD):
                        last = mm3(nc, pVt[:, a, :], xh[:, k, c], xl[:, k, c], wh[2][:, k, :], wl[2][:, k, :], k == 0, k == KD - 1)
                last.then_inc(v_ps, 1)
                if not (isinstance(i, int) and i == NBODY - 1):
                    turn(i + 1)
                pe.wait_ge(k_sb, KD * (i + 1))
                after(pe, df_ok, i)
                for c in range(KD):
                    last = nc.tensor.matmul(pS[:, c, :, :].rearrange("p b k -> p (b k)"), sx[:, c, :, :].rearrange("p h s -> p (h s)"), kT[:, c, :], start=True, stop=True)
                last.then_inc(s_ps, 1)

            def end_turn(i):
                pe.wait_ge(pn_ok, i + 1)
                for c in range(KD):
                    for a in range(2):
                        last = nc.tensor.transpose(pT[:, c, a, :], pn[:, c, 2 * a:2 * a + 2, :].rearrange("p b k -> p (b k)"), g.ident[:, :])
                last.then_inc(pt_ps, 1)

            def end(i):
                pe.wait_ge(pt_sb, i + 1)
                after(pe, own_ok, 2 * i)
                for a in range(2):
                    for c in range(KD):
                        for b in range(2):
                            r = slice(b * S, (b + 1) * S)
                            last = nc.tensor.matmul(pU[b][:, a, c, :, :].rearrange("p h s -> p (h s)"), vt[r, a, c * P:(c + 1) * P], pt[r, c, a, :], start=True, stop=True)
                last.then_inc(u_ps, 1)
            turn(0)
            pe.wait_ge(sl_in, 16)
            for m in range(KD):
                for k in range(KD):
                    last = nc.tensor.matmul(pS[:, m, 0, 0:NS], g.w_small[:, W_DQ, k, m * P:(m + 1) * P], slotT[:, k, :], start=k == 0, stop=k == KD - 1)
            last.then_inc(sq_ps, 1)
            pe.wait_ge(wh_ok, 3)
            pe.wait_ge(wl_ok, 3)
            pe.wait_ge(sx_ok, 1)
            body(0)
            body(1)
            end(0)
            with pe.Fori(2, NBODY - 1) as i:
                body(i)
                end(i - 1)
            body(NBODY - 1)
            end(NBODY - 2)
            end_turn(NBODY - 1)
            pe.wait_ge(v_sb, NBODY)
            end(NBODY - 1)

        @block.scalar
        def _(act):
            for n in range(3):
                nc.scalar.activation(wh[n][:, :, :], raw[n], ACT.Copy).then_inc(wh_ok, 1)

            def slot_queries():
                act.wait_ge(sq_ps, 1)
                for m in range(KD):
                    nc.scalar.activation(sq[:, m, :], pS[:, m, 0, 0:NS], ACT.Identity, bias=g.cols[:, COL_DBQ, m:m + 1]).then_inc(sq_ok, 1)

            def high(i):
                act.wait_ge(x_ps, i + 1)
                after(act, v_ps, i)
                nc.scalar.activation(xh[:, :, :], pX[:, :, :], ACT.Copy).then_inc(xh_ok, 1)

            def values(i):
                act.wait_ge(v_ps, i + 1)
                after(act, u_ps, i)
                nc.scalar.activation(vt[:, :, :], pVt[:, :, :], ACT.Copy).then_inc(v_sb, 1)

            def weights(i):
                act.wait_ge(pt_ps, i + 1)
                after(act, u_ps, i)
                nc.scalar.activation(pt[:, :, :, :], pT[:, :, :, :], ACT.Copy).then_inc(pt_sb, 1)

            def body(i):
                act.wait_ge(k_ps, i + 1)
                after(act, s_ps, i)
                for m in range(KD):
                    nc.scalar.activation(kT[:, m, :], pK[:, m, :], ACT.Identity, bias=g.cols[:, COL_DBK, m:m + 1]).then_inc(k_sb, 1)
                act.wait_ge(q_ps, i + 1)
                after(act, q_out, 16 * i)
                for m in range(KD):
                    nc.scalar.activation(qT[:, m, :], pQ[:, m, :], ACT.Identity, bias=g.cols[:, COL_CBQ, m:m + 1]).then_inc(q_sb, 1)
                if not first_body(i):
                    weights(i - 1)
                if not (isinstance(i, int) and i == NBODY - 1):
                    high(i + 1)
                act.wait_ge(df_ok, i + 1)
                after(act, pn_ok, i)
                nc.scalar.activation(ex[:, :, :, :], df[:, :, :, :], ACT.Exp, scale=SCALE).then_inc(ex_ok, 1)
                values(i)
            high(0)
            slot_queries()
            bodies(act, body)
            weights(NBODY - 1)

        @block.vector
        def _(dve):
            v = nc.vector
            for n in range(3):
                dve.wait_ge(wh_ok, n + 1)
                v.tensor_tensor(wl[n][:, :, :], raw[n], f32(wh[n][:, :, :]), ALU.subtract).then_inc(wl_ok, 1)

            def stationary():
                dve.wait_ge(sq_ok, KD)
                v.tensor_tensor(sx[:, :, :, :], bc(sq[:, :, :], 2, HC), bc(bc(g.headmask[:, :], 1, KD), 3, NS), ALU.mult).then_inc(sx_ok, 1)

            def low(i):
                dve.wait_ge(xh_ok, i + 1)
                v.tensor_tensor(xl[:, :, :], pX[:, :, :], f32(xh[:, :, :]), ALU.subtract).then_inc(xl_ok, 1)

            def own_head(i):
                dve.wait_ge(u_ps, i + 1)
                for b in range(2):
                    after(dve, ot_ok, 2 * i + b - 1)
                    v.tensor_tensor(own[b][:, :, :, :], pU[b][:, :, :, :, :].rearrange("p a c h s -> p (a c) s h"),
                                    bc(bc(g.headmask[:, :], 1, NS), 1, 4), ALU.mult).then_inc(own_ok, 1)
                for b in range(2):
                    dve.wait_ge(own_ok, 2 * i + b + 1)
                    v.tensor_reduce(g.oT[:, :, bass.ds(2 * i, 2), b, :].rearrange("p k a s -> p a k s"),
                                    own[b][:, :, :, :].rearrange("p (a c) s h -> p a c s h", a=2), AX_X, ALU.add).then_inc(ot_ok, 1)

            def body(i):
                if not (isinstance(i, int) and i == NBODY - 1):
                    low(i + 1)
                dve.wait_ge(s_ps, i + 1)
                after(dve, df_ok, i)
                v.tensor_reduce(mx[:, :, :], pS[:, :, :, :], AX_X, ALU.max).then_inc(mx_ok, 1)
                dve.wait_ge(mx_ok, i + 1)
                after(dve, ex_ok, i)
                v.tensor_tensor(df[:, :, :, :], pS[:, :, :, :], bc(mx[:, :, :], 3, S), ALU.subtract).then_inc(df_ok, 1)
                dve.wait_ge(ex_ok, i + 1)
                after(dve, rc_ok, i)
                v.tensor_reduce(sm[:, :, :], ex[:, :, :, :], AX_X, ALU.add).then_inc(sm_ok, 1)
                dve.wait_ge(sm_ok, i + 1)
                after(dve, pn_ok, i)
                v.reciprocal(rc[:, :, :], sm[:, :, :]).then_inc(rc_ok, 1)
                dve.wait_ge(rc_ok, i + 1)
                after(dve, pt_ps, i)
                v.tensor_tensor(pn[:, :, :, :], ex[:, :, :, :], bc(rc[:, :, :], 3, S), ALU.mult).then_inc(pn_ok, 1)
                if not first_body(i):
                    own_head(i - 1)
            low(0)
            stationary()
            bodies(dve, body)
            own_head(NBODY - 1)


NG = NB // HC


def slot_norm(nc, g, dr):
    with ExitStack() as ctx:
        sb, ps, sem = scope(nc, ctx, "norm")
        ob = sb("ob", [P, KD, NB * NS])
        base = sb("base", [P, D])
        o = sb("o", [P, NG, D])
        su = sb("su", [P, NG])
        mean = sb("mean", [P, NG])
        xc = sb("xc", [P, NG, D])
        x2 = ob[:, :, :].rearrange("p k n -> p (k n)").rearrange("p (g n) -> p g n", g=NG)
        ss = sb("ss", [P, NG])
        ms = sb("ms", [P, NG])
        rv = sb("rv", [P, NG])
        inv = sb("inv", [P, NG])
        pO = [ps(f"pO{n}", [P, 2, D]) for n in range(NG // 2)]
        pR = [ps(f"pR{c}", [P, NG, P]) for c in range(KD)]
        pH = [ps(f"pH{c}", [P, NG, P]) for c in range(KD)]
        names = ("ob_ok", "base_ok", "o_ps", "o_ok", "su_ok", "mean_ok", "xc_ok", "x2_ok", "ss_ok", "ms_ok", "rv_ok", "inv_ok",
                 "h1_ok", "h2_ok", "h3_ok", "r_ps", "h_ps", "r_sb", "h_sb")
        (ob_ok, base_ok, o_ps, o_ok, su_ok, mean_ok, xc_ok, x2_ok, ss_ok, ms_ok, rv_ok, inv_ok,
         h1_ok, h2_ok, h3_ok, r_ps, h_ps, r_sb, h_sb) = (sem(n) for n in names)
        block = ctx.enter_context(nc.Block())

        def by_slot(ap):
            return ap.rearrange("p g (b e) -> p e g b", e=NS)

        @block.sync
        def _(sp):
            load_up(sp, g, dr, NS - 1, g.extra, g.extra_up)
            load_down(sp, g, dr, NS - 1, g.extra, g.extra_down)

        @block.tensor
        def _(pe):
            pe.wait_ge(ob_ok, KD)
            for n in range(NG):
                for k in range(KD):
                    last = nc.tensor.matmul(pO[n // 2][:, n % 2, :], ob[:, k, n * P:(n + 1) * P], g.w_small[:, W_DO, k, :], start=k == 0, stop=k == KD - 1)
                if n % 2:
                    last.then_inc(o_ps, 1)
            pe.wait_ge(o_ok, NG // 2)
            for c in range(KD):
                for n in range(NG):
                    last = nc.tensor.transpose(pR[c][:, n, :], o[:, n, c * P:(c + 1) * P], g.ident[:, :])
            last.then_inc(r_ps, 1)
            pe.wait_ge(h3_ok, 1)
            for c in range(KD):
                for n in range(NG):
                    last = nc.tensor.transpose(pH[c][:, n, :], xc[:, n, c * P:(c + 1) * P], g.ident[:, :])
                last.then_inc(h_ps, 1)

        @block.scalar
        def _(act):
            for k in range(KD):
                nc.scalar.activation(ob[:, k, :], g.oT[:, k, :, :, :].rearrange("p a b s -> p (a b s)"), ACT.Identity, bias=g.cols[:, COL_DBV, k:k + 1]).then_inc(ob_ok, 1)
            act.wait_ge(su_ok, 1)
            nc.scalar.activation(mean[:, :], su[:, :], ACT.Copy, scale=1.0 / D).then_inc(mean_ok, 1)
            act.wait_ge(r_ps, 1)
            for c in range(KD):
                nc.scalar.activation(g.resT[:, c, :, :].rearrange("p e (g b) -> p e g b", g=NG), by_slot(pR[c][:, :, :]), ACT.Copy).then_inc(r_sb, 1)
            act.wait_ge(rv_ok, 1)
            nc.scalar.activation(inv[:, :], rv[:, :], ACT.Sqrt).then_inc(inv_ok, 1)
            act.wait_ge(h_ps, 1)
            nc.scalar.activation(g.hT[:, 0, :, :].rearrange("p e (g b) -> p e g b", g=NG), by_slot(pH[0][:, :, :]), ACT.Copy).then_inc(h_sb, 1)

        @block.vector
        def _(dve):
            v = nc.vector
            v.tensor_tensor(base[:, :], g.slot_tm[:, :], g.rows[:, ROW_DBO, :], ALU.add).then_inc(base_ok, 1)
            dve.wait_ge(base_ok, 1)
            for n in range(NG // 2):
                dve.wait_ge(o_ps, n + 1)
                v.tensor_tensor(o[:, 2 * n:2 * n + 2, :], pO[n][:, :, :], bc(base[:, :], 1, 2), ALU.add).then_inc(o_ok, 1)
            dve.wait_ge(o_ok, NG // 2)
            v.tensor_reduce(su[:, :], o[:, :, :], AX_X, ALU.add).then_inc(su_ok, 1)
            dve.wait_ge(mean_ok, 1)
            v.tensor_tensor(xc[:, :, :], o[:, :, :], bc(mean[:, :], 2, D), ALU.subtract).then_inc(xc_ok, 1)
            dve.wait_ge(xc_ok, 1)
            v.tensor_tensor(x2, xc[:, :, :], xc[:, :, :], ALU.mult).then_inc(x2_ok, 1)
            dve.wait_ge(x2_ok, 1)
            v.tensor_reduce(ss[:, :], x2, AX_X, ALU.add).then_inc(ss_ok, 1)
            dve.wait_ge(ss_ok, 1)
            v.tensor_scalar(ms[:, :], ss[:, :], 1.0 / D, LN_EPS, ALU.mult, ALU.add).then_inc(ms_ok, 1)
            dve.wait_ge(ms_ok, 1)
            v.reciprocal(rv[:, :], ms[:, :]).then_inc(rv_ok, 1)
            v.tensor_tensor(xc[:, :, :], xc[:, :, :], bc(g.ln[:, 0, :], 1, NG), ALU.mult).then_inc(h1_ok, 1)
            dve.wait_ge(inv_ok, 1)
            dve.wait_ge(h1_ok, 1)
            v.tensor_tensor(xc[:, :, :], xc[:, :, :], bc(inv[:, :], 2, D), ALU.mult).then_inc(h2_ok, 1)
            dve.wait_ge(h2_ok, 1)
            v.tensor_tensor(xc[:, :, :], xc[:, :, :], bc(g.ln[:, 1, :], 1, NG), ALU.add).then_inc(h3_ok, 1)
            dve.wait_ge(r_sb, KD)
            v.tensor_tensor(g.baseT[:, :, :, :], g.resT[:, :, :, :], bc(g.b2[:, :, :], 3, NB), ALU.add).then_inc(h_sb, 1)
            dve.wait_ge(h_ps, 2)
            v.tensor_copy(g.hT[:, 1, :, :].rearrange("p e (g b) -> p e g b", g=NG), by_slot(pH[1][:, :, :])).then_inc(h_sb, 1)




def slot_experts(nc, g, dr):
    with ExitStack() as ctx:
        sb, ps, sem = scope(nc, ctx, "sexp")
        hs = [sb(f"hs{a}", [P, KD, NB]) for a in range(2)]
        uc = [sb(f"uc{a}", [P, 512]) for a in range(2)]
        ub = [sb(f"ub{a}", [P, 4, 4, NB]) for a in range(2)]
        uf = [sb(f"uf{a}", [P, 4, 2, NB]) for a in range(2)]
        yc = [sb(f"yc{a}", [P, D]) for a in range(2)]
        pA = [ps(f"pA{a}", [P, 512]) for a in range(2)]
        pT = [ps(f"pT{a}", [P, 4, 4, NB]) for a in range(2)]
        pY = [ps(f"pY{a}", [P, 512]) for a in range(2)]
        pR = [ps(f"pR{a}", [P, 512]) for a in range(2)]
        hs_ok, a_ps, uc_ok, t_ps, ub_ok, us_ok, uf_ok, y_ps, yc_ok, r_ps, o_ok = (
            sem(n) for n in ("hs_ok", "a_ps", "uc_ok", "t_ps", "ub_ok", "us_ok", "uf_ok", "y_ps", "yc_ok", "r_ps", "o_ok"))
        block = ctx.enter_context(nc.Block())

        def after(eng, semaphore, value):
            if not (isinstance(value, int) and value <= 0):
                eng.wait_ge(semaphore, value)

        def experts_of(eng, step):
            for j in range(NRING):
                step(j, j)
            with eng.Fori(1, NS // NRING - 1) as m:
                for j in range(NRING):
                    step(NRING * m + j, j)
            for j in range(NRING):
                step(NS - NRING + j, j)

        def expert(n):
            return NS - 1 if isinstance(n, int) and n == 0 else n - 1

        def weights(n, j):
            if isinstance(n, int) and n == 0:
                return g.extra, g.extra_up, g.extra_down, 16
            r = (j - 1) % NRING
            return g.ring[r], g.up_in[r], g.down_in[r], (n - 1 - r) * (16 // NRING) + 16

        @block.sync
        def _(sp):
            def step(n, j):
                r = (j - 1) % NRING
                sp.wait_ge(a_ps, n + 1)
                load_up(sp, g, dr, n - 1 + NRING, g.ring[r], g.up_in[r])
                sp.wait_ge(y_ps, n + 1)
                load_down(sp, g, dr, n - 1 + NRING, g.ring[r], g.down_in[r])
            turns = (NS - 1 - NRING) // NRING
            with sp.Fori(0, turns) as m:
                for j in range(1, NRING + 1):
                    step(NRING * m + j, j)
            for n in range(NRING * turns + 1, NS - NRING):
                step(n, n)

        @block.tensor
        def _(pe):
            def up(n, j):
                a = j % 2
                w, up_in, _, landed = weights(n, j)
                pe.wait_ge(up_in, landed)
                pe.wait_ge(hs_ok, n + 1)
                after(pe, uc_ok, n - 1)
                for k in range(KD):
                    for q in range(4):
                        at = ((q // 2) * KD + k) * FH + (q % 2) * 512
                        last = nc.tensor.matmul(pA[a][32 * q:32 * q + 32, :], hs[a][:, k, :], w[:, at:at + 512], start=k == 0, stop=k == KD - 1,
                                                tile_position=(0, 32 * q))
                last.then_inc(a_ps, 1)

            def turn(n, j):
                a = j % 2
                pe.wait_ge(uc_ok, n + 1)
                after(pe, ub_ok, n - 1)
                for q in range(4):
                    last = nc.tensor.transpose(pT[a][:, q, :, :].rearrange("p n b -> p (n b)"), uc[a][:, q * P:(q + 1) * P], g.ident[:, :])
                last.then_inc(t_ps, 1)

            def down(n, j):
                a = j % 2
                w, _, down_in, landed = weights(n, j)
                pe.wait_ge(down_in, landed)
                pe.wait_ge(uf_ok, n + 1)
                after(pe, yc_ok, n - 1)
                for h in range(2):
                    for q in range(4):
                        at = W2_AT + (4 * h + q) * D
                        last = nc.tensor.matmul(pY[a][32 * q:32 * q + 32, 0:D], uf[a][:, q, h, :], w[:, at:at + D], start=h == 0, stop=h == 1,
                                                tile_position=(0, 32 * q))
                last.then_inc(y_ps, 1)

            def total(n, j):
                a = j % 2
                pe.wait_ge(yc_ok, n + 1)
                after(pe, o_ok, n - 1)
                for k in range(KD):
                    last = nc.tensor.matmul(pR[a][:, k * NB:(k + 1) * NB], yc[a][:, k * P:(k + 1) * P], g.stack[:, :], start=True, stop=True)
                last.then_inc(r_ps, 1)

            def step(n, j):
                up(n, j)
                if not (isinstance(n, int) and n == 0):
                    down(n - 1, (j - 1) % NRING)
                turn(n, j)
                if not (isinstance(n, int) and n == 0):
                    total(n - 1, (j - 1) % NRING)
            experts_of(pe, step)
            down(NS - 1, NRING - 1)
            total(NS - 1, NRING - 1)

        @block.scalar
        def _(act):
            def sums(n, j):
                act.wait_ge(y_ps, n + 1)
                after(act, r_ps, n - 1)
                nc.scalar.activation(yc[j % 2][:, :], pY[j % 2][:, 0:D], ACT.Copy).then_inc(yc_ok, 1)

            def step(n, j):
                a = j % 2
                act.wait_ge(a_ps, n + 1)
                after(act, t_ps, n - 1)
                nc.scalar.activation(uc[a][:, :], pA[a][:, :], ACT.Copy).then_inc(uc_ok, 1)
                if not (isinstance(n, int) and n == 0):
                    sums(n - 1, (j - 1) % NRING)
                act.wait_ge(ub_ok, n + 1)
                nc.scalar.activation(ub[a][:, :, :, :], ub[a][:, :, :, :], ACT.Silu).then_inc(us_ok, 1)
            experts_of(act, step)
            sums(NS - 1, NRING - 1)

        @block.vector
        def _(dve):
            v = nc.vector

            def stationary(n, j):
                after(dve, a_ps, n - 1)
                v.tensor_copy(hs[j % 2][:, :, :], g.hT[:, :, bass.ds(expert(n), 1), :].rearrange("p k o b -> p k (o b)")).then_inc(hs_ok, 1)

            def result(n, j):
                dve.wait_ge(r_ps, n + 1)
                v.tensor_tensor(g.o2T[:, :, bass.ds(expert(n), 1), :].rearrange("p k o b -> p k (o b)"),
                                pR[j % 2][:, 0:KD * NB].rearrange("p (k b) -> p k b", k=KD),
                                g.baseT[:, :, bass.ds(expert(n), 1), :].rearrange("p k o b -> p k (o b)"), ALU.add).then_inc(o_ok, 1)

            def step(n, j):
                a = j % 2
                if not (isinstance(n, int) and n == NS - 1):
                    stationary(n + 1, (j + 1) % NRING)
                dve.wait_ge(t_ps, n + 1)
                after(dve, uf_ok, n - 1)
                v.tensor_tensor(ub[a][:, :, :, :], pT[a][:, :, :, :],
                                bc(g.eb[:, bass.ds(expert(n), 1), :].rearrange("p o (j n) -> p (o j) n", j=4), 3, NB), ALU.add).then_inc(ub_ok, 1)
                if not (isinstance(n, int) and n == 0):
                    result(n - 1, (j - 1) % NRING)
                dve.wait_ge(us_ok, n + 1)
                after(dve, y_ps, n - 1)
                v.tensor_tensor(uf[a][:, :, :, :], ub[a][:, :, 0:2, :], ub[a][:, :, 2:4, :], ALU.mult).then_inc(uf_ok, 1)
            stationary(0, 0)
            experts_of(dve, step)
            result(NS - 1, NRING - 1)


def tokens(nc, g, dr):
    with ExitStack() as ctx:
        sb, ps, sem = scope(nc, ctx, "tok")
        k2 = sb("k2", [P, KD, NB, NS])
        v2 = sb("v2", [P, KD, NB, NS])
        qt = [sb(f"qt{a}", [P, KD, PB]) for a in range(2)]
        kx = sb("kx", [P, KD, 4, HC, NS])
        vx = sb("vx", [P, KD, 4, HC, NS])
        vo = sb("vo", [P, 4, KD, D])
        mx = sb("mx", [P, 2, KD, HC])
        df = sb("df", [P, 2, KD, HC, NS])
        ex = sb("ex", [P, 2, KD, HC, NS])
        sm = sb("sm", [P, 2, KD, HC])
        rc = sb("rc", [P, 2, KD, HC])
        pn = sb("pn", [P, 2, KD, HC, NS])
        pt = sb("pt", [P, 2, KD, P])
        xb = sb("xb", [P, 2, D])
        ot = [sb(f"ot{a}", [P, 2, D]) for a in range(2)]
        pVo = [ps(f"pVo{b}", [P, KD, D]) for b in range(4)]
        pS = ps("pS", [P, 2, KD, HC, NS])
        pT = ps("pT", [P, 2, KD, P])
        pO = [ps(f"pO{a}", [P, 2, D]) for a in range(2)]
        kv_ps, kv_sb, kx_ok, vx_ok, vo_ps, vo_sb = (sem(n) for n in ("kv_ps", "kv_sb", "kx_ok", "vx_ok", "vo_ps", "vo_sb"))
        s_ps, mx_ok, df_ok, ex_ok, sm_ok, rc_ok, pn_ok, pt_ps, pt_sb, o_ps, xb_ok, ot_ok = (
            sem(n) for n in ("s_ps", "mx_ok", "df_ok", "ex_ok", "sm_ok", "rc_ok", "pn_ok", "pt_ps", "pt_sb", "o_ps", "xb_ok", "ot_ok"))
        q_in = [sem(f"q_in{a}") for a in range(2)]
        o_out = [sem(f"o_out{a}") for a in range(2)]
        block = ctx.enter_context(nc.Block())

        def after(eng, semaphore, value):
            if not (isinstance(value, int) and value <= 0):
                eng.wait_ge(semaphore, value)

        def pairs(eng, body):
            body(0, 0)
            body(1, 1)
            with eng.Fori(1, NBODY // 2 - 1) as p:
                body(2 * p, 0)
                body(2 * p + 1, 1)
            body(NBODY - 2, 0)
            body(NBODY - 1, 1)

        def opening(i):
            return isinstance(i, int) and i == 0

        def closing(i):
            return isinstance(i, int) and i == NBODY - 1

        @block.sync
        def _(sp):
            def load(i, a):
                after(sp, s_ps, i - 1)
                sp.dma_start(qt[a][:, :, :], dr.q[bass.ds(i, 1)].rearrange("o p k n -> p (o k) n")).then_inc(q_in[a], 16)
            pairs(sp, load)
            for a in range(2):
                sp.wait_ge(q_in[a], 16 * NBODY // 2)

        @block.gpsimd
        def _(pool):
            def body(i, a):
                after(pool, ot_ok, i)
                nc.gpsimd.tensor_tensor(xb[:, :, :], g.x1[:, bass.ds(2 * i, 2), :], bc(g.rows[:, ROW_CBO, :], 1, 2), ALU.add).then_inc(xb_ok, 1)
            pairs(pool, body)
            for a in range(2):
                pool.wait_ge(o_out[a], 16 * NBODY // 2)

        @block.tensor
        def _(pe):
            for n, w in enumerate((W_CK, W_CV)):
                for m in range(KD):
                    for k in range(KD):
                        last = nc.tensor.matmul(pVo[2 * n + m][:, :, :].rearrange("p k n -> p (k n)"), g.w_small[:, w, k, m * P:(m + 1) * P],
                                                g.o2T[:, k, :, :].rearrange("p e b -> p (e b)"), start=k == 0, stop=k == KD - 1)
                    last.then_inc(kv_ps, 1)
            pe.wait_ge(kv_sb, 2 * KD)

            def scores(i, a):
                pe.wait_ge(q_in[a], 8 * (i - a) + 16)
                pe.wait_ge(kx_ok, KD * (i + 1))
                after(pe, df_ok, i)
                for s in range(2):
                    for c in range(KD):
                        for b in range(2):
                            last = nc.tensor.matmul(pS[b * S:(b + 1) * S, s, c, :, :].rearrange("p h s -> p (h s)"),
                                                    qt[a][:, c, s * P + b * S:s * P + (b + 1) * S],
                                                    kx[:, c, 2 * s + b, :, :].rearrange("p h s -> p (h s)"), start=True, stop=True)
                last.then_inc(s_ps, 1)

            def values(i):
                pe.wait_ge(vx_ok, KD * (i + 1))
                after(pe, vo_sb, 4 * i)
                for b in range(4):
                    for c in range(KD):
                        last = nc.tensor.matmul(pVo[b][:, c, :], vx[:, c, b, :, :].rearrange("p h s -> p (h s)"), g.w_small[:, W_CO, c, :], start=True, stop=True)
                    last.then_inc(vo_ps, 1)

            def end_turn(i):
                pe.wait_ge(pn_ok, i + 1)
                for s in range(2):
                    for c in range(KD):
                        last = nc.tensor.transpose(pT[:, s, c, :], pn[:, s, c, :, :].rearrange("p h s -> p (h s)"), g.ident[:, :])
                last.then_inc(pt_ps, 1)

            def end(i, a):
                pe.wait_ge(pt_sb, i + 1)
                pe.wait_ge(vo_sb, 4 * (i + 1))
                after(pe, ot_ok, i - 1)
                for s in range(2):
                    for b in range(2):
                        for c in range(KD):
                            last = nc.tensor.matmul(pO[a][b * S:(b + 1) * S, s, :], pt[:, s, c, b * S:(b + 1) * S], vo[:, 2 * s + b, c, :],
                                                    start=c == 0, stop=c == KD - 1)
                last.then_inc(o_ps, 1)

            def body(i, a):
                if not opening(i):
                    end_turn(i - 1)
                scores(i, a)
                if not opening(i):
                    end(i - 1, 1 - a)
                values(i)
            pairs(pe, body)
            end_turn(NBODY - 1)
            end(NBODY - 1, (NBODY - 1) % 2)

        @block.scalar
        def _(act):
            for n, (col, to) in enumerate(((COL_CBK, k2), (COL_CBV, v2))):
                for m in range(KD):
                    act.wait_ge(kv_ps, KD * n + m + 1)
                    nc.scalar.activation(to[:, m, :, :].rearrange("p b e -> p e b"), pVo[2 * n + m][:, :, :].rearrange("p k n -> p (k n)").rearrange("p (e b) -> p e b", e=NS),
                                         ACT.Identity, bias=g.cols[:, col, m:m + 1]).then_inc(kv_sb, 1)

            def weights(i):
                act.wait_ge(pt_ps, i + 1)
                after(act, o_ps, i)
                nc.scalar.activation(pt[:, :, :, :], pT[:, :, :, :], ACT.Copy).then_inc(pt_sb, 1)

            def values(i):
                for b in range(2):
                    act.wait_ge(vo_ps, 4 * i + b + 1)
                    after(act, o_ps, i)
                    nc.scalar.activation(vo[:, b, :, :], pVo[b][:, :, :], ACT.Copy).then_inc(vo_sb, 1)

            def store(i, a):
                act.wait_ge(ot_ok, i + 1)
                act.dma_start(dr.out[:, bass.ds(2 * i, 2), :], ot[a][:, :, :]).then_inc(o_out[a], 16)

            def body(i, a):
                if not opening(i):
                    weights(i - 1)
                act.wait_ge(df_ok, i + 1)
                after(act, pn_ok, i)
                nc.scalar.activation(ex[:, :, :, :, :], df[:, :, :, :, :], ACT.Exp, scale=SCALE).then_inc(ex_ok, 1)
                if not opening(i):
                    store(i - 1, 1 - a)
                values(i)
            pairs(act, body)
            weights(NBODY - 1)
            store(NBODY - 1, (NBODY - 1) % 2)

        @block.vector
        def _(dve):
            v = nc.vector
            mask = bc(bc(g.headmask[:, :], 1, 4), 3, NS)
            dve.wait_ge(kv_sb, 2 * KD)

            def masked(i, to, source, done, used, per_body):
                after(dve, used, per_body * i)
                for c in range(KD):
                    v.tensor_tensor(to[:, c, :, :, :], bc(source[:, c, bass.ds(4 * i, 4), :], 2, HC), mask, ALU.mult).then_inc(done, 1)

            def body(i, a):
                dve.wait_ge(s_ps, i + 1)
                after(dve, df_ok, i)
                v.tensor_reduce(mx[:, :, :, :], pS[:, :, :, :, :], AX_X, ALU.max).then_inc(mx_ok, 1)
                dve.wait_ge(mx_ok, i + 1)
                after(dve, ex_ok, i)
                v.tensor_tensor(df[:, :, :, :, :], pS[:, :, :, :, :], bc(mx[:, :, :, :], 4, NS), ALU.subtract).then_inc(df_ok, 1)
                if not closing(i):
                    masked(i + 1, kx, k2, kx_ok, s_ps, 1)
                dve.wait_ge(ex_ok, i + 1)
                after(dve, rc_ok, i)
                v.tensor_reduce(sm[:, :, :, :], ex[:, :, :, :, :], AX_X, ALU.add).then_inc(sm_ok, 1)
                dve.wait_ge(sm_ok, i + 1)
                after(dve, pn_ok, i)
                v.reciprocal(rc[:, :, :, :], sm[:, :, :, :]).then_inc(rc_ok, 1)
                dve.wait_ge(rc_ok, i + 1)
                after(dve, pt_ps, i)
                v.tensor_tensor(pn[:, :, :, :, :], ex[:, :, :, :, :], bc(rc[:, :, :, :], 4, NS), ALU.mult).then_inc(pn_ok, 1)
                if not opening(i):
                    result(i - 1, 1 - a)
                for b in range(2, 4):
                    dve.wait_ge(vo_ps, 4 * i + b + 1)
                    after(dve, o_ps, i)
                    v.tensor_copy(vo[:, b, :, :], pVo[b][:, :, :]).then_inc(vo_sb, 1)
                if not closing(i):
                    masked(i + 1, vx, v2, vx_ok, vo_ps, 4)

            def result(i, a):
                dve.wait_ge(o_ps, i + 1)
                dve.wait_ge(xb_ok, i + 1)
                if not (isinstance(i, int) and i < 2):
                    dve.wait_ge(o_out[a], 8 * (i - a))
                v.tensor_tensor(ot[a][:, :, :], pO[a][:, :, :], xb[:, :, :], ALU.add).then_inc(ot_ok, 1)
            masked(0, kx, k2, kx_ok, s_ps, 1)
            masked(0, vx, v2, vx_ok, vo_ps, 4)
            pairs(dve, body)
            result(NBODY - 1, (NBODY - 1) % 2)


def consts():
    p = np.arange(P)
    ident = np.eye(P, dtype=np.float32)
    tri = np.concatenate([(p[:, None] < p[None, :]), np.ones((P, P), bool)], axis=1).astype(np.float32)
    rev = np.zeros((P, P), np.float32)
    rev[:, 0:E1] = E1 - np.arange(E1)
    rev[:, 32:32 + E1] = SLOT * np.arange(E1)
    rev[:, 64:64 + NT] = np.arange(NT)
    headmask = (p[:, None] // DH == np.arange(HC)[None, :]).astype(np.float32)
    batchmask = (p[:, None] // 32 % 2 == np.arange(2)[None, :]).astype(np.float32)
    stack = (p[:, None] % 32 == np.arange(NB)[None, :]).astype(np.float32)
    return {"stack": stack, "batchmask": batchmask, "ident": ident, "tri": tri, "rev": rev, "headmask": headmask, "ones": np.ones((4, 512), np.float32)}


def layout(a):
    lay = consts()
    lay["x_tm"] = a["x"].reshape(TT, P, D).transpose(1, 0, 2)
    lay["condT"] = a["cond_256"].T
    lay["gg_W"] = a["L0_cond_gg_W"]
    lay["gg_b"] = a["L0_cond_gg_b"][None]
    lay["wg_b"] = a["L0_cond_wg_b"][None]
    lay["wg_W"] = a["L0_cond_wg_W"].reshape(KD, P, E1).transpose(1, 0, 2)
    lay["rms_w"] = a["L0_cond_rms_w"].reshape(KD, P).T
    for l, n in enumerate(("W1", "W2", "W3")):
        w = a["L0_cond_" + n]
        lay[f"w{l}"] = w.reshape(E1, w.shape[1] // P, P, w.shape[2]).transpose(0, 2, 1, 3).reshape(E1, P, -1)
    lay["b12"] = np.concatenate([a["L0_cond_b1"].reshape(E1, KM, P), a["L0_cond_b2"].reshape(E1, KM, P)], axis=1).transpose(0, 2, 1)
    lay["b3"] = a["L0_cond_b3"][:, None]
    c2, f = "L0_cond2_", "L0_ffn_"
    small = [a["L0_attn_Wv"].T, a["L0_attn_Wo"].T, a[c2 + "Wq"].T, a[c2 + "Wk"].T, a[c2 + "Wv"].T, a[f + "d_Wq"], a[f + "d_Wk"], a[f + "d_Wv"],
             a[f + "d_Wo"], a[f + "c_Wq"], a[f + "c_Wk"], a[f + "c_Wv"], a[f + "c_Wo"]]
    lay["w_small"] = np.stack([w.reshape(KD, P, D).transpose(1, 0, 2) for w in small], axis=1)
    p, j = np.arange(P)[:, None], np.arange(4)[None, :]
    feature = 32 * (2 * j + p // 64) + p % 32
    lay["wo4"] = a[c2 + "Wo"].T[feature]
    lay["adaw"] = np.stack([a[c2 + n].T for n in ("g1w", "b1w", "g2w", "b2w")], axis=1)
    lay["adab"] = np.stack([a[c2 + n].reshape(KD, P).T for n in ("g1b", "b1b", "g2b", "b2b")], axis=1)
    lay["w_ff"] = np.stack([a[c2 + "gate_w"].T.reshape(KD, P, FH).transpose(1, 0, 2).reshape(P, -1),
                            a[c2 + "hid_w"].T.reshape(KD, P, FH).transpose(1, 0, 2).reshape(P, -1),
                            a[c2 + "out_w"].T.reshape(FH // P, P, D).transpose(1, 0, 2).reshape(P, -1)], axis=1)
    lay["rows"] = np.stack([a["L0_attn_bv"], a["L0_attn_bo"], a[f + "d_bo"], a[f + "c_bo"]])[None]
    cols = [a["L0_attn_bv"], a[f + "d_bq"], a[f + "d_bk"], a[f + "d_bv"], a[f + "c_bq"], a[f + "c_bk"], a[f + "c_bv"]]
    lay["cols"] = np.stack([v.reshape(KD, P).T for v in cols], axis=1)
    lay["slotT"] = a[f + "slot_query"][0].T.reshape(KD, P, NS).transpose(1, 0, 2)
    lay["slot_tm"] = a[f + "slot_query"][0][p[:, 0] % NS]
    lay["ln"] = np.stack([a[f + "e_ln_g"][p[:, 0] % NS], a[f + "e_ln_b"][p[:, 0] % NS]], axis=1)
    eb = np.stack([a[f + "e_b1"], a[f + "e_bg"]], axis=1).reshape(NS, 4, 4, P)
    lay["eb"] = eb.transpose(3, 0, 2, 1).reshape(P, NS, 16)
    lay["b2"] = a[f + "e_b2"].reshape(NS, KD, P).transpose(2, 1, 0)
    lay["w_slot"] = np.concatenate([a[f + n].reshape(NS, -1, P, a[f + n].shape[2]).transpose(0, 2, 1, 3).reshape(NS, P, -1)
                                    for n in ("e_W1", "e_Wg", "e_W2")], axis=2)
    return lay


def program(nc, dr):
    with ExitStack() as ctx:
        sb, ps, sem = scope(nc, ctx, "k")
        g = Env()
        g.x = sb("x", [P, TT, D])
        g.x1 = sb("x1", [P, TT, D])
        g.ident = sb("ident", [P, P])
        g.tri = sb("tri", [P, 2 * P])
        g.rev = sb("rev", [P, P])
        g.headmask = sb("headmask", [P, HC])
        g.batchmask = sb("batchmask", [P, 2])
        g.slot = [sb(f"slot{c}", [P, TT], U32) for c in range(2)]
        g.weight = [sb(f"weight{c}", [P, TT]) for c in range(2)]
        g.tile_expert = sb("tile_expert", [P, NT], I32)
        g.w_small = sb("w_small", [P, 13, KD, D])
        g.w_o1 = g.w_small[:, W_O1]
        g.wo4 = sb("wo4", [P, 4, D])
        g.rows = sb("rows", [P, 4, D])
        g.cols = sb("cols", [P, 7, KD])
        g.ada = sb("ada", [P, 4, KD, NB])
        g.inv1 = sb("inv1", [P, TT])
        route(nc, g, dr)
        experts(nc, g, dr)
        g.w_ff = sb("w_ff", [P, 3, KD * FH])
        g.ss2 = sb("ss2", [P, TT])
        self_attention(nc, g, dr, True, [g.w_small[:, W_V1]], None, g.x, g.x1, None)
        project_first(nc, g, dr)
        self_attention(nc, g, dr, False, [g.w_small[:, W_Q2], g.w_small[:, W_K2], g.w_small[:, W_V2]], g.wo4[:, :, :], g.x1, g.x, g.ss2)
        swiglu(nc, g, dr)
        g.oT = g.wo4[:, :, :].rearrange("p j n -> p (j n)").rearrange("p (k a b s) -> p k a b s", k=KD, a=TT, b=2)
        g.resT, g.hT, g.baseT, g.o2T = (
            g.x[:, 4 * n:4 * n + 4, :].rearrange("p t n -> p (t n)").rearrange("p (k e b) -> p k e b", k=KD, e=NS) for n in range(4))
        g.slot_tm = sb("slot_tm", [P, D])
        g.ln = sb("ln", [P, 2, D])
        g.eb = sb("eb", [P, NS, 4 * 4])
        g.b2 = sb("b2", [P, KD, NS])
        g.stack = sb("stack", [P, NB])
        g.ffn_in = sem("ffn_in")
        g.extra_up, g.extra_down = sem("extra_up"), sem("extra_down")
        g.up_in = [sem(f"up_in{r}") for r in range(NRING)]
        g.down_in = [sem(f"down_in{r}") for r in range(NRING)]
        with ExitStack() as ring:
            g.ring = [g.w_ff[:, :, :].rearrange("p n m -> p (n m)")]
            for r in range(1, NRING):
                g.ring.append(ring.enter_context(nc.sbuf_tensor(f"ring{r}", [P, W_SLOT], F32)))
            slots(nc, g, dr)
            g.extra = ring.enter_context(nc.sbuf_tensor("ring_extra", [P, W_SLOT], F32))
            slot_norm(nc, g, dr)
            slot_experts(nc, g, dr)
        tokens(nc, g, dr)


def kernel(**inputs):
    import concourse.bacc as bacc
    from concourse.bass_utils import run_bass_kernel_spmd
    lay = layout({n: np.asarray(v) for n, v in inputs.items()})
    nc = bacc.Bacc("TRN2", target_bir_lowering=False, num_devices=1)
    arrays, dr = {}, Env()
    for n, v in lay.items():
        v = np.ascontiguousarray(v)
        arrays["in_" + n] = v
        dr.__dict__[n] = nc.dram_tensor("in_" + n, v.shape, mybir.dt.from_np(v.dtype), kind="ExternalInput").ap()
    dr.w = [dr.w0, dr.w1, dr.w2]
    dr.xs = nc.dram_tensor("rows_of_experts", (NT * SLOT, D), F32, kind="Internal").ap()
    dr.ys = nc.dram_tensor("results_of_experts", (NT * SLOT, D), F32, kind="Internal").ap()
    dr.heads = nc.dram_tensor("results_of_heads", (NB, NH, S, DH), F32, kind="Internal").ap()
    dr.q = nc.dram_tensor("queries_of_tokens", (NBODY, P, KD, PB), F32, kind="Internal").ap()
    dr.out = nc.dram_tensor("out", (P, TT, D), F32, kind="ExternalOutput").ap()
    program(nc, dr)
    r = run_bass_kernel_spmd(nc, [arrays], core_ids=[0])
    return r.results[0]["out"].transpose(1, 0, 2).reshape(NB, S, D)
```
